# Optimizing a Trainium2 kernel written in Bass

```python
import numpy as np
import jax
import jax.numpy as jnp

def _softmax(x, axis=-1):
    return jax.nn.softmax(x, axis=axis)

def _gelu(x):
    return jax.nn.gelu(x, approximate=True)

def _silu(x):
    return jax.nn.silu(x)

def _sigmoid(x):
    return jax.nn.sigmoid(x)

def _layernorm(x, axis=-1, eps=1e-05):
    m = jnp.mean(x, axis=axis, keepdims=True)
    v = jnp.var(x, axis=axis, keepdims=True)
    return (x - m) / jnp.sqrt(v + eps)

def _scatter_add(tgt, idx, src, axis=0):
    return tgt.at[idx].add(src)

def _segment_sum(src, seg, n):
    return jax.ops.segment_sum(src, seg, n)
kernel_name = 'mk_flamingo_gated_d1_seqx_r4_f12157'

def setup_inputs(seed: int=0):
    np.random.seed(seed)
    _w = jnp.asarray

    def _rec_inputs():
        import jax
        import jax.numpy as jnp
        _rk = jax.random.key(seed)
        x = -0.0003929 + 0.9999 * jax.random.normal(jax.random.fold_in(_rk, 1), (4, 512, 512), jnp.float32)
        _lenS = 512 - jax.random.randint(jax.random.fold_in(_rk, 7), (4,), 0, max(1, 512 // 4) + 1, jnp.int32)
        _lenS2 = 64 - jax.random.randint(jax.random.fold_in(_rk, 8), (4,), 0, max(1, 64 // 4) + 1, jnp.int32)
        _ctx_2048P = jax.random.normal(jax.random.fold_in(_rk, 11), (4, 16, 512), jnp.float32)
        _ctx_2048c = jax.random.dirichlet(jax.random.fold_in(_rk, 511), 0.3 * jnp.ones((16,), jnp.float32), (4, 64))
        _ctx_2048t = jnp.einsum('bsk,bkd->bsd', _ctx_2048c, _ctx_2048P)
        _ctx_2048t = _ctx_2048t * jax.lax.rsqrt(jnp.mean(jnp.square(_ctx_2048t)) + 1e-12) * 0.953939
        ctx_2048 = -0.000514642 + 1.00011 * (_ctx_2048t + 0.3 * jax.random.normal(jax.random.fold_in(_rk, 611), (4, 64, 512), jnp.float32))
        _validS = jnp.arange(512)[None, :] < _lenS[:, None]
        _validS2 = jnp.arange(64)[None, :] < _lenS2[:, None]
        _causal = jnp.tril(jnp.ones((512, 512), dtype=bool))
        mask_BxS2_ik0 = jnp.where(jnp.broadcast_to(_validS2[:, :], (4, 64)), 0, 1).astype(jnp.int32)
        _g = jax.random.normal(jax.random.fold_in(_rk, 9001), (2, 1), jnp.float32)
        _g = jnp.sign(_g) * jnp.maximum(jnp.abs(_g), 1.0) + (_g == 0) * 1.0
        g_xattn = _g[0]
        g_ffn = _g[1]
        return (x, ctx_2048, mask_BxS2_ik0, g_xattn, g_ffn)
    x, ctx_2048, mask_BxS2_ik0, g_xattn, g_ffn = _rec_inputs()

    def _L0_xattn_setup():
        import jax, jax.numpy as jnp
        import numpy as np
        import math
        H = 512
        NH = 16
        HD = H // NH
        EPS_LN = 1e-05
        RES_SCALE_MAX = 0.3

        def _nan_clean(x, lim=10000.0):
            return jnp.nan_to_num(x, nan=0.0, posinf=lim, neginf=-lim)
        key = jax.random.key(seed)
        ks = jax.random.split(key, 12)
        B, S, T = (4, 512, 64)
        std = 1.0 / math.sqrt(H)
        return {'hidden_states': jax.random.normal(ks[0], (B, S, H), jnp.float32), 'audio_tokens': jax.random.normal(ks[1], (B, T, H), jnp.float32), 'attention_mask': jax.random.randint(ks[2], (B, T), 0, 2, jnp.int32), 'Wq': jax.random.normal(ks[3], (H, H), jnp.float32) * std, 'bq': jnp.zeros((H,), jnp.float32), 'Wk': jax.random.normal(ks[4], (H, H), jnp.float32) * std, 'bk': jnp.zeros((H,), jnp.float32), 'Wv': jax.random.normal(ks[5], (H, H), jnp.float32) * std, 'bv': jnp.zeros((H,), jnp.float32), 'Wo': jax.random.normal(ks[6], (H, H), jnp.float32) * std, 'bo': jnp.zeros((H,), jnp.float32), 'ln_gamma': jnp.ones((H,), jnp.float32), 'ln_beta': jnp.zeros((H,), jnp.float32), 'residual_scale': jnp.float32(0.05)}
    _L0_xattn_all = _L0_xattn_setup()
    _L0_xattn_in = {k: v for k, v in _L0_xattn_all.items() if k in ('Wq', 'bq', 'Wk', 'bk', 'Wv', 'bv', 'Wo', 'bo', 'ln_gamma', 'ln_beta', 'residual_scale')}
    del _L0_xattn_all

    def _L0_ffn_setup():
        import jax, jax.numpy as jnp
        import numpy as np
        B, S, H, I, E, K = (4, 512, 512, 1024, 8, 2)
        key = jax.random.key(seed)
        k1, k2, k3, k4 = jax.random.split(key, 4)
        return {'hidden_states': jax.random.normal(k1, (B, S, H), dtype=jnp.float32), 'gate_weight': jax.random.normal(k2, (E, H), dtype=jnp.float32) * 0.02, 'gate_up_proj': jax.random.normal(k3, (E, 2 * I, H), dtype=jnp.float32) * 0.02, 'down_proj': jax.random.normal(k4, (E, H, I), dtype=jnp.float32) * 0.02}
    _L0_ffn_all = _L0_ffn_setup()
    _L0_ffn_in = {k: v for k, v in _L0_ffn_all.items() if k in ('gate_weight', 'gate_up_proj', 'down_proj')}
    del _L0_ffn_all
    return {'x': x, 'ctx_2048': ctx_2048, 'mask_BxS2_ik0': mask_BxS2_ik0, 'g_xattn': g_xattn, 'g_ffn': g_ffn, 'L0_xattn_Wq': _L0_xattn_in['Wq'], 'L0_xattn_bq': _L0_xattn_in['bq'], 'L0_xattn_Wk': _L0_xattn_in['Wk'], 'L0_xattn_bk': _L0_xattn_in['bk'], 'L0_xattn_Wv': _L0_xattn_in['Wv'], 'L0_xattn_bv': _L0_xattn_in['bv'], 'L0_xattn_Wo': _L0_xattn_in['Wo'], 'L0_xattn_bo': _L0_xattn_in['bo'], 'L0_xattn_ln_gamma': _L0_xattn_in['ln_gamma'], 'L0_xattn_ln_beta': _L0_xattn_in['ln_beta'], 'L0_xattn_residual_scale': _L0_xattn_in['residual_scale'], 'L0_ffn_gate_weight': _L0_ffn_in['gate_weight'], 'L0_ffn_gate_up_proj': _L0_ffn_in['gate_up_proj'], 'L0_ffn_down_proj': _L0_ffn_in['down_proj']}

def reference(x, ctx_2048, mask_BxS2_ik0, g_xattn, g_ffn, L0_xattn_Wq, L0_xattn_bq, L0_xattn_Wk, L0_xattn_bk, L0_xattn_Wv, L0_xattn_bv, L0_xattn_Wo, L0_xattn_bo, L0_xattn_ln_gamma, L0_xattn_ln_beta, L0_xattn_residual_scale, L0_ffn_gate_weight, L0_ffn_gate_up_proj, L0_ffn_down_proj):
    import jax
    import jax.numpy as jnp

    def _L0_xattn_ref(hidden_states, audio_tokens, attention_mask, Wq, bq, Wk, bk, Wv, bv, Wo, bo, ln_gamma, ln_beta, residual_scale):
        import jax, jax.numpy as jnp
        import numpy as np
        import math
        H = 512
        NH = 16
        HD = H // NH
        EPS_LN = 1e-05
        RES_SCALE_MAX = 0.3

        def _nan_clean(x, lim=10000.0):
            return jnp.nan_to_num(x, nan=0.0, posinf=lim, neginf=-lim)
        B, S, _ = hidden_states.shape
        T = audio_tokens.shape[1]
        hs = _nan_clean(hidden_states).astype(jnp.float32)
        at = _nan_clean(audio_tokens).astype(jnp.float32)

        def proj(x, W, b, L):
            y = x @ W.T + b
            return y.reshape(B, L, NH, HD).transpose(0, 2, 1, 3)
        q = _nan_clean(proj(hs, Wq, bq, S))
        k = _nan_clean(proj(at, Wk, bk, T))
        v = _nan_clean(proj(at, Wv, bv, T))
        scale = max(math.sqrt(HD), 1e-08)
        scores = jnp.einsum('bhsd,bhtd->bhst', q, k) / scale
        scores = jnp.clip(scores, -50.0, 50.0)
        scores = jnp.nan_to_num(scores, nan=0.0, posinf=50.0, neginf=-50.0)
        attend = (attention_mask.astype(jnp.float32) > 0.5)[:, None, None, :]
        scores = jnp.where(attend, scores, -10000.0)
        scores = jnp.clip(scores, -50.0, 50.0)
        probs = jax.nn.softmax(scores, axis=-1)
        probs = jnp.nan_to_num(probs, nan=0.0, posinf=1.0, neginf=0.0)
        probs = probs / (probs.sum(axis=-1, keepdims=True) + 1e-08)
        ctx = jnp.einsum('bhst,bhtd->bhsd', probs, v)
        ctx = ctx.transpose(0, 2, 1, 3).reshape(B, S, H)
        delta = _nan_clean(ctx @ Wo.T + bo)
        rs = jnp.clip(residual_scale, 0.0, RES_SCALE_MAX)
        delta = rs * delta
        mu = delta.mean(axis=-1, keepdims=True)
        var = jnp.mean((delta - mu) ** 2, axis=-1, keepdims=True)
        delta = (delta - mu) / jnp.sqrt(var + EPS_LN) * ln_gamma + ln_beta
        return delta

    def _L0_ffn_ref(hidden_states, gate_weight, gate_up_proj, down_proj):
        import jax, jax.numpy as jnp
        import numpy as np
        B, S, H, I, E, K = (4, 512, 512, 1024, 8, 2)
        b, s, h = hidden_states.shape
        num_experts, top_k = (gate_weight.shape[0], K)
        x = hidden_states.reshape(-1, h)
        router_logits = x @ gate_weight.T
        probs = jax.nn.softmax(router_logits.astype(jnp.float32), axis=-1)
        top_v, top_i = jax.lax.top_k(probs, top_k)
        top_v = top_v / top_v.sum(axis=-1, keepdims=True)
        combine_w = jnp.einsum('tke,tk->te', jax.nn.one_hot(top_i, num_experts, dtype=top_v.dtype), top_v).astype(x.dtype)

        def expert_step(acc, inp):
            gu, dp, w = inp
            gate, up = jnp.split(x @ gu.T, 2, axis=-1)
            hidden = jax.nn.silu(gate) * up
            y = hidden @ dp.T
            return (acc + w[:, None] * y, None)
        out, _ = jax.lax.scan(expert_step, jnp.zeros_like(x), (gate_up_proj, down_proj, combine_w.T))
        return out.reshape(b, s, h)
    x = x + jnp.tanh(g_xattn[0]) * _L0_xattn_ref(_layernorm(x, axis=-1), ctx_2048, mask_BxS2_ik0, L0_xattn_Wq, L0_xattn_bq, L0_xattn_Wk, L0_xattn_bk, L0_xattn_Wv, L0_xattn_bv, L0_xattn_Wo, L0_xattn_bo, L0_xattn_ln_gamma, L0_xattn_ln_beta, L0_xattn_residual_scale)
    x = x + jnp.tanh(g_ffn[0]) * _L0_ffn_ref(_layernorm(x, axis=-1), L0_ffn_gate_weight, L0_ffn_gate_up_proj, L0_ffn_down_proj)
    return x

_drawn_inputs = setup_inputs


def setup_inputs(seed=0):
    import zlib

    import numpy as np

    out = dict(_drawn_inputs(seed))
    spreads = {'L0_xattn_bq': (0.0, 0.272),
     'L0_xattn_bk': (0.0, 0.8),
     'L0_xattn_bv': (0.0, 0.1),
     'L0_xattn_bo': (0.0, 0.1),
     'L0_xattn_ln_gamma': (1.0, 0.2),
     'L0_xattn_ln_beta': (0.0, 0.1)}
    factors = {}
    for name, (base, spread) in spreads.items():
        noise = np.random.default_rng([zlib.crc32(name.encode()), seed]).standard_normal(out[name].shape)
        drawn = base * np.exp(spread * noise) if base else spread * noise
        out[name] = jnp.asarray(drawn.astype(out[name].dtype))
    for name, factor in factors.items():
        out[name] = (out[name] * factor).astype(out[name].dtype)
    return out
```

```python
import concourse.bass as bass
from concourse import mybir
from contextlib import ExitStack

ALU = mybir.AluOpType
ACT = mybir.ActivationFunctionType
AX = mybir.AxisListType
F32 = mybir.dt.float32
F32R = mybir.dt.float32r
I32 = mybir.dt.int32

P = 128
H = 512
KC = H // P
NB = 4
S = 512
TT = S // P
NT = NB * TT
TOK = NB * S
T = 64
NH, HD = 16, 32
PAIRS = NH // 2
E = 8
I = 1024
TOPK = 2
GU = 4
DH = 2
PW = 4 * 512
IC = I // P
MAXT = TOK * TOPK // P + E - 1
SLOTT = MAXT + 1
EPS = 1e-5
INV_SCALE = float(HD) ** -0.5
CLIP = 50.0 / INV_SCALE
NEG_BIG = -3.0e38


def flamingo_gated_block(nc, x, ctx_t, mask, w_attn, b_cols, b_rows, gates, gate_t, w_exp, out):
    st = ExitStack()
    with st:
        def sb(name, shape, dt=F32, scope=st):
            return scope.enter_context(nc.sbuf_tensor(name, shape, dt))

        def sem(name):
            return st.enter_context(nc.semaphore(name))

        bank = [st.enter_context(nc.psum_tensor(f"bank{i}", [P, 512], F32)) for i in range(8)]
        h_dram = nc.dram_tensor("h_rows", [TOK + P, H], F32).ap()
        h_rows = h_dram.rearrange("(n p) d -> n p d", p=P)
        out_rows = out.rearrange("(n p) d -> n p d", p=P)
        x_b = x.rearrange("(b t p) d -> b p t d", p=P, t=TT)

        ident = sb("ident", [P, P])
        raw = sb("raw", [P, GU + DH, PW])
        logits = sb("logits", [P, NT, E])
        gate_w = sb("gate_w", [P, KC, E])
        gsc = sb("gsc", [P, 3])
        tg = sb("tg", [P, 3])
        slot_idx = sb("slot_idx", [P, SLOTT], I32)
        slot_w = sb("slot_w", [P, SLOTT])
        tile_tab = sb("tile_tab", [P, SLOTT, 4], I32)
        n_tiles = sb("n_tiles", [P, 4], I32)

        pa = ExitStack()
        w_hi = sb("w_hi", [P, 4, KC, H], F32R, pa)
        w_lo = sb("w_lo", [P, 4, KC, H], F32R, pa)
        rows = sb("rows", [P, 4, H], F32, pa)
        bcol = sb("bcol", [P, 2, KC], F32, pa)
        lim = sb("lim", [P, NB], F32, pa)
        mask_sb = sb("mask_sb", [P, NB], I32, pa)
        c_raw = sb("c_raw", [P, KC, 2, T], F32, pa)
        c_hi = sb("c_hi", [P, KC, 2, T], F32R, pa)
        c_lo = sb("c_lo", [P, KC, 2, T], F32R, pa)
        k_sb = sb("k_sb", [P, KC, T], F32, pa)
        kbd_hi = sb("kbd_hi", [P, KC, 2, P], F32R, pa)
        kbd_lo = sb("kbd_lo", [P, KC, 2, P], F32R, pa)
        vbd_hi = sb("vbd_hi", [P, KC, 2, 4, HD], F32R, pa)
        vbd_lo = sb("vbd_lo", [P, KC, 2, 4, HD], F32R, pa)
        obd = sb("obd", [P, 2, 4, HD], F32R, pa)
        xs = sb("xs", [P, TT, H], F32, pa)
        hs = sb("hs", [P, TT, H], F32, pa)
        st6 = sb("st6", [P, TT, 6], F32, pa)
        mv = sb("mv", [P, TT, 2], F32, pa)
        ve = sb("ve", [P, TT], F32, pa)
        rstd = sb("rstd", [P, TT], F32, pa)
        mhalf = sb("mhalf", [P, TT], F32, pa)
        xt_hi = sb("xt_hi", [P, KC, S], F32R, pa)
        xt_lo = sb("xt_lo", [P, KC, S], F32R, pa)
        q_hi = sb("q_hi", [P, KC, S], F32R, pa)
        q_lo = sb("q_lo", [P, KC, S], F32R, pa)
        work = raw[:, GU:GU + DH, :].rearrange("p a (b n) -> p a b n", n=2 * S)
        sc, ex, rden, o_sb = (work[:, i // 2, i % 2, :].rearrange("p (j n) -> p j n", j=2) for i in range(4))
        ex_hi = sb("ex_hi", [P, 2, S], F32R, pa)
        ex_lo = sb("ex_lo", [P, 2, S], F32R, pa)
        o_hi, o_lo = xt_hi, xt_lo
        d_sb = hs
        ht = sb("ht", [P, 2, KC, P], F32, pa)
        v_sb = ht[:, 0, :, :].rearrange("p k n -> p (k n)")

        pa.close()
        pr = ExitStack()
        NE3 = [P, NT, E]
        iota_e = sb("iota_e", NE3, F32, pr)
        eq = sb("eq", NE3, F32, pr)
        oh1 = sb("oh1", NE3, F32, pr)
        oh2 = sb("oh2", NE3, F32, pr)
        sel = sb("sel", NE3, F32, pr)
        lg2 = sb("lg2", NE3, F32, pr)
        posn = sb("posn", NE3, F32, pr)
        tmp3 = sb("tmp3", NE3, F32, pr)
        m1 = sb("m1", [P, NT, 1], F32, pr)
        m2 = sb("m2", [P, NT, 1], F32, pr)
        i1 = sb("i1", [P, NT, 1], F32, pr)
        wk = sb("wk", [P, TOPK, NT], F32, pr)
        wden = sb("wden", [P, NT], F32, pr)
        slot = sb("slot", [P, TOPK, NT], F32, pr)
        slot_i = sb("slot_i", [P, TOPK, NT], I32, pr)
        sa_i = sb("sa_i", [P, TOPK, NT], I32, pr)
        sb_i = sb("sb_i", [P, TOPK, NT], I32, pr)
        sa = sb("sa", [P, TOPK, NT], F32, pr)
        sbp = sb("sbp", [P, TOPK, NT], F32, pr)
        tok1 = sb("tok1", [P, NT], F32, pr)
        iota40 = sb("iota40", [P, SLOTT], F32, pr)
        iota128 = sb("iota128", [P, P], F32, pr)
        pidx = sb("pidx", [P, 1], F32, pr)
        upper = sb("upper", [P, P], F32, pr)
        ones = sb("ones", [P, P], F32, pr)
        iota_n = sb("iota_n", [P, E, 16], F32, pr)
        cmp_n = sb("cmp_n", [P, E, 16], F32, pr)
        nexp = sb("nexp", [P, E], F32, pr)
        tl = sb("tl", [P, E, 1], F32, pr)
        tri = sb("tri", [P, E, E], F32, pr)
        trm = sb("trm", [P, E, E], F32, pr)
        tend = sb("tend", [P, E, 1], F32, pr)
        base = sb("base", [P, E], F32, pr)
        ind = sb("ind", [P, E, SLOTT], F32, pr)
        tabf = sb("tabf", [P, SLOTT, 4], F32, pr)
        ohb = sb("ohb", [P, NT, P], F32, pr)
        oha = sb("oha", [P, TOPK, NT, 2, SLOTT], F32, pr)
        ohe = sb("ohe", [P, NT, SLOTT], F32, pr)
        tv = sb("tv", [P, SLOTT], F32, pr)
        tz = sb("tz", [P, SLOTT], F32, pr)
        pr.close()

        pe_ = ExitStack()
        g_hi = sb("g_hi", [P, GU, KC, 512], F32R, pe_)
        g_lo = sb("g_lo", [P, GU, KC, 512], F32R, pe_)
        dn_hi = sb("dn_hi", [P, DH, 4, H], F32R, pe_)
        dn_lo = sb("dn_lo", [P, DH, 4, H], F32R, pe_)
        xg = sb("xg", [P, H], F32, pe_)
        gt_hi = sb("gt_hi", [P, KC, P], F32R, pe_)
        gt_lo = sb("gt_lo", [P, KC, P], F32R, pe_)
        silu = sb("silu", [P, GU, 256], F32, pe_)
        hid = sb("hid", [P, GU, 256], F32, pe_)
        hd_hi = sb("hd_hi", [P, IC, P], F32R, pe_)
        hd_lo = sb("hd_lo", [P, IC, P], F32R, pe_)
        y_sb = sb("y_sb", [P, H], F32, pe_)
        g_idx = sb("g_idx", [P, 1], I32, pe_)
        s_idx = sb("s_idx", [P, 1], I32, pe_)
        pe_.close()
        zrow = hs[:, 0, :]

        def f32(ap):
            return ap.bitcast(F32)

        wload = [sem(f"attn_weights{w}_loaded") for w in range(4)]
        cload, xload, rload, crload, setup = (sem(n) for n in
            ("constants_loaded", "x_loaded", "rows_loaded", "context_loaded", "pool_setup"))
        gates_ready, w_hi_done, w_lo_done = sem("gates_ready"), sem("attn_w_hi"), sem("attn_w_lo")
        dset = sem("vector_setup")
        ln_stats, ln_mean, ln_var, ln_rstd, hs_done = (sem(n) for n in ("ln_stats", "ln_mean", "ln_var", "ln_rstd", "hs_done"))
        xt_tr, xt_h, xt_l = sem("xt_transposed"), sem("xt_hi_done"), sem("xt_lo_done")
        c_h, c_l, kv_mm, kv_sb, bd_h, bd_l = (sem(n) for n in
            ("context_hi", "context_lo", "kv_product", "kv_biased", "kv_hi_placed", "kv_lo_placed"))
        q_mm, q_h, q_l = sem("q_product"), sem("q_hi_done"), sem("q_lo_done")
        s_mm, s_clip, s_exp, e_h, e_l = (sem(n) for n in
            ("scores_product", "scores_clipped", "exp_done", "exp_hi_done", "exp_lo_done"))
        pair_mm, den_r, o_n, o_h, o_l = (sem(n) for n in
            ("pv_product", "den_reciprocal", "context_normalised", "o_hi_done", "o_lo_done"))
        d_mm, d_ready, dmean, dstats, dvar, drstd, dnorm, dgam, x1_done = (sem(n) for n in
            ("delta_product", "delta_scaled", "delta_mean", "delta_stats", "delta_var", "delta_rstd", "delta_normed",
             "delta_gamma", "x1_done"))
        hmean, hstats, hvar, hrstd, h_done = (sem(n) for n in ("h_mean", "h_stats", "h_var", "h_rstd", "h_done"))
        h_tr, h_ev, lg_mm, lg_done = (sem(n) for n in ("h_transposed", "h_evacuated", "logits_product", "logits_done"))
        x1_store, h_store, pad_store = sem("x1_stored"), sem("h_stored"), sem("pad_rows_stored")
        zdone = sem("zero_rows_ready")
        rt, rt_pool, rt_act, rt_pe = (sem(n) for n in ("routing_vector", "routing_pool", "routing_act", "routing_product"))
        tables = sem("tables_ready")
        raw_in = [sem(f"raw_piece{p}_loaded") for p in range(GU + DH)]
        gu_hi, gu_split, dn_h, dn_split = (sem(n) for n in ("gu_hi_done", "gu_split_done", "down_hi_done", "down_split_done"))
        idx_0, idx_g, idx_s, gath, scat = (sem(n) for n in ("first_index", "gather_index", "scatter_index", "rows_gathered", "rows_scattered"))
        gt_tr, gt_h, gt_l = sem("slot_rows_transposed"), sem("slot_rows_hi"), sem("slot_rows_lo")
        gu_mm, silu_done, hid_done, hd_tr, hd_h, hd_l = (sem(n) for n in
            ("gate_up_product", "silu_done", "hidden_done", "hidden_transposed", "hidden_hi", "hidden_lo"))
        y_mm, y_ready, y_free = sem("down_product"), sem("y_ready"), sem("y_added")

        block = st.enter_context(nc.Block())

        def product3(eng, psum, a_hi, a_lo, b_hi, b_lo, n=KC, first=True, last=True):
            for k in range(n):
                for j, (a, b) in enumerate(((a_hi, b_hi), (a_hi, b_lo), (a_lo, b_hi))):
                    mm = eng.matmul(psum, a(k), b(k), start=(first and k == 0 and j == 0),
                                    stop=(last and k == n - 1 and j == 2))
            return mm

        def plain(eng):
            eng.wait_ge(wload[0], 16)

        @block.sync
        def _(sp):
            sp.sem_inc(x1_store, 16 * TT)
            sp.sem_inc(h_store, 16 * TT)
            for w in range(4):
                sp.dma_start(raw[:, w, :], w_attn[w]).then_inc(wload[w], 16)
            for p in range(GU):
                sp.wait_ge(w_lo_done, p + 1)
                sp.dma_start(raw[:, p, :], w_exp[0, p]).then_inc(raw_in[p], 16)
            with sp.Fori(0, NB) as b:
                sp.wait_ge(x1_store, (b + 1) * 16 * TT)
                sp.dma_start(xs[:, :, :], x_b[b]).then_inc(xload, 16)
                for t in range(TT):
                    sp.wait_ge(x1_done, b * TT + t + 1)
                    sp.dma_start(out_rows[b * TT + t], xs[:, t, :]).then_inc(x1_store, 16)
                    sp.wait_ge(h_done, b * TT + t + 1)
                    sp.dma_start(h_rows[b * TT + t], hs[:, t, :]).then_inc(h_store, 16)
            sp.wait_ge(h_store, 16 * (NT + TT))
            sp.wait_ge(pad_store, 32)
            for p in range(GU, GU + DH):
                sp.dma_start(raw[:, p, :], w_exp[0, p]).then_inc(raw_in[p], 16)
            with sp.Fori(1, E) as e:
                for p in range(GU):
                    sp.wait_ge(gu_split, (e - 1) * GU + p + 1)
                    sp.dma_start(raw[:, p, :], w_exp[e, p]).then_inc(raw_in[p], 16)
                for p in range(DH):
                    sp.wait_ge(dn_split, (e - 1) * DH + p + 1)
                    sp.dma_start(raw[:, GU + p, :], w_exp[e, GU + p]).then_inc(raw_in[GU + p], 16)

        @block.gpsimd
        def _(pool):
            pool.memset(ident[:, :], 0.0).then_inc(setup, 1)
            pool.wait_ge(setup, 1)
            pool.affine_select(out=ident[:, :], in_=ident[:, :], compare_op=ALU.not_equal, fill=1.0,
                               base=0, pattern=[[-1, P]], channel_multiplier=1).then_inc(setup, 1)
            pool.memset(mhalf[:, :], -0.5).then_inc(setup, 1)
            for tile in (kbd_hi, kbd_lo, vbd_hi, vbd_lo, obd):
                pool.memset(f32(tile[:]), 0.0).then_inc(setup, 1)
            pool.wait_ge(setup, 8)
            for q in range(2):
                for g in range(2):
                    pool.memset(f32(obd[g * 64:g * 64 + 64, q, 2 * q + g, :]), 1.0).then_inc(setup, 1)
            pool.dma_start(mask_sb[:, :], mask).then_inc(cload, 16)
            pool.dma_start(bcol[:, :, :], b_cols).then_inc(cload, 16)
            pool.dma_start(rows[:, :, :], b_rows.partition_broadcast(P)).then_inc(cload, 16)
            pool.dma_start(gsc[:, :], gates.partition_broadcast(P)).then_inc(cload, 16)
            pool.dma_start(gate_w[:, :, :], gate_t).then_inc(cload, 16)
            pool.wait_ge(setup, 12)
            pool.memset(zrow, 0.0).then_inc(zdone, 1)
            pool.wait_ge(zdone, 1)
            pool.dma_start(out_rows[NT], zrow).then_inc(pad_store, 16)
            pool.dma_start(h_rows[NT], zrow).then_inc(pad_store, 16)
            pool.wait_ge(pad_store, 32)
            pool.sem_inc(zdone, 1)
            with pool.Fori(0, NB) as b:
                pool.wait_ge(c_l, b + 1)
                for g in range(2):
                    pool.dma_start(c_raw[:, :, g, :], ctx_t[b]).then_inc(crload, 16)
                pool.wait_ge(ln_var, b + 1)
                pool.tensor_tensor(rstd[:, :], ve[:, :], mhalf[:, :], ALU.pow).then_inc(ln_rstd, 1)
                for pr_ in range(PAIRS):
                    j = pr_ % 2
                    pool.wait_ge(e_h, b * PAIRS + pr_ + 1)
                    pool.tensor_tensor(ex_lo[:, j, :], ex[:, j, :], f32(ex_hi[:, j, :]), ALU.subtract).then_inc(e_l, 1)
                for t in range(TT):
                    pool.wait_ge(dvar, b * TT + t + 1)
                    pool.tensor_tensor(rstd[:, t:t + 1], ve[:, t:t + 1], mhalf[:, 0:1], ALU.pow).then_inc(drstd, 1)
                    pool.wait_ge(dnorm, b * TT + t + 1)
                    pool.tensor_tensor(d_sb[:, t, :], d_sb[:, t, :], rows[:, 2, :], ALU.mult).then_inc(dgam, 1)
                    pool.wait_ge(dgam, b * TT * 2 + 2 * t + 1)
                    pool.tensor_tensor(d_sb[:, t, :], d_sb[:, t, :], rows[:, 3, :], ALU.add).then_inc(dgam, 1)
                    pool.wait_ge(dgam, b * TT * 2 + 2 * t + 2)
                    pool.tensor_tensor(xs[:, t, :], xs[:, t, :], d_sb[:, t, :], ALU.add).then_inc(x1_done, 1)
                    pool.wait_ge(hvar, b * TT + t + 1)
                    pool.tensor_tensor(rstd[:, t:t + 1], ve[:, t:t + 1], mhalf[:, 0:1], ALU.pow).then_inc(hrstd, 1)

            pool.wait_ge(lg_done, NB)
            pool.wait_ge(h_store, 16 * (NT + TT))

            def pattern(ap, pat, base_, cm):
                pool.iota(ap, pattern=pat, base=base_, channel_multiplier=cm,
                          allow_small_or_imprecise_dtypes=True).then_inc(rt_pool, 1)

            pattern(iota_e[:, :, :], [[0, NT], [1, E]], -E, 0)
            pool.memset(upper[:, :], 1.0).then_inc(rt_pool, 1)
            pool.memset(ones[:, :], 1.0).then_inc(rt_pool, 1)
            pool.memset(tri[:, :, :], 1.0).then_inc(rt_pool, 1)
            pool.wait_ge(rt_pool, 4)
            pool.affine_select(out=upper[:, :], in_=upper[:, :], compare_op=ALU.is_gt, fill=0.0,
                               base=0, pattern=[[1, P]], channel_multiplier=-1).then_inc(rt_pool, 1)
            pool.affine_select(out=tri[:, :, :], in_=tri[:, :, :], compare_op=ALU.is_ge, fill=0.0,
                               base=0, pattern=[[1, E], [-1, E]], channel_multiplier=0).then_inc(rt_pool, 1)
            pattern(iota_n[:, :, :], [[0, E], [P, 16]], 0, 0)
            pattern(iota40[:, :], [[1, SLOTT]], 0, 0)
            pattern(iota128[:, :], [[1, P]], 0, 0)
            pattern(tok1[:, :], [[P, NT]], 1, 1)
            pattern(pidx[:, :], [[0, 1]], TOK + 1, 1)

            pool.wait_ge(tables, 1)
            pool.wait_ge(h_store, 16 * (NT + TT))
            pool.wait_ge(pad_store, 32)
            used = pool.value_load(n_tiles[0:1, 0:1], min_val=1, max_val=MAXT)

            def gather():
                pool.indirect_dma_start(out=xg[:, :], out_offset=None, in_=h_dram[:, :],
                                        in_offset=bass.IndirectOffsetOnAxis(ap=g_idx[:, 0:1], axis=0)
                                        ).then_inc(gath, 16)

            pool.tensor_copy(g_idx[:, :], slot_idx[:, 0:1]).then_inc(idx_0, 1)
            pool.wait_ge(idx_0, 1)
            gather()
            with pool.Fori(0, used) as g:
                pool.wait_ge(gath, g * 16 + 16)
                plain(pool)
                pool.wait_ge(gt_tr, g + 1)
                pool.tensor_copy(g_idx[:, :], slot_idx[:, bass.ds(g + 1, 1)]).then_inc(idx_g, 1)
                plain(pool)
                pool.wait_ge(idx_g, g + 1)
                gather()
                plain(pool)
                pool.wait_ge(y_ready, g + 2)
                pool.tensor_copy(s_idx[:, :], slot_idx[:, bass.ds(g, 1)]).then_inc(idx_s, 1)
                plain(pool)
                pool.wait_ge(idx_s, g + 1)
                pool.indirect_dma_start(out=out[:, :],
                                        out_offset=bass.IndirectOffsetOnAxis(ap=s_idx[:, 0:1], axis=0),
                                        in_=y_sb[:, :], in_offset=None,
                                        compute_op=ALU.add).then_inc(scat, 16)
                pool.wait_ge(scat, g * 16 + 16)
                pool.sem_inc(y_free, 1)
            pool.wait_ge(gath, used * 16 + 16)
            pool.wait_ge(x1_store, 16 * (NT + TT))

        @block.vector
        def _(dve):
            dve.sem_inc(c_l, 1)
            dve.sem_inc(hd_l, 2)
            dve.wait_ge(cload, 80)
            dve.tensor_scalar(tg[:, 2:3], gsc[:, 2:3], 0.0, 0.3, ALU.max, ALU.min).then_inc(dset, 1)
            dve.tensor_scalar(lim[:, :], mask_sb[:, :], 0.5, 2.0 * CLIP, ALU.is_gt, ALU.mult).then_inc(dset, 1)
            dve.wait_ge(dset, 2)
            dve.wait_ge(gates_ready, 1)
            dve.tensor_scalar(lim[:, :], lim[:, :], -CLIP, None, ALU.add).then_inc(dset, 1)
            dve.tensor_scalar(rows[:, 1, :], rows[:, 1, :], tg[:, 2:3], None, ALU.mult).then_inc(dset, 1)
            dve.tensor_scalar(rows[:, 2:4, :], rows[:, 2:4, :], tg[:, 0:1], None, ALU.mult).then_inc(dset, 1)
            for w in range(4):
                dve.wait_ge(w_hi_done, w + 1)
                hi = w_hi[:, w, :, :].rearrange("p k n -> p (k n)")
                lo = w_lo[:, w, :, :].rearrange("p k n -> p (k n)")
                dve.tensor_tensor(lo, raw[:, w, :], f32(hi), ALU.subtract).then_inc(w_lo_done, 1)
            dve.wait_ge(setup, 12)
            dve.wait_ge(dset, 5)
            dve.wait_ge(zdone, 2)
            with dve.Fori(0, NB) as b:
                dve.wait_ge(c_h, b + 1)
                dve.tensor_tensor(c_lo[:, :, :, :], c_raw[:, :, :, :], f32(c_hi[:, :, :, :]),
                                  ALU.subtract).then_inc(c_l, 1)
                dve.wait_ge(xload, (b + 1) * 16)
                for t in range(TT):
                    bn = dve.bn_stats(st6[:, t, :], xs[:, t, :])
                bn.then_inc(ln_stats, 1)
                plain(dve)
                dve.wait_ge(ln_stats, b + 1)
                for t in range(TT):
                    bn = dve.bn_aggr(mv[:, t, :], st6[:, t, :])
                bn.then_inc(ln_mean, 1)
                dve.wait_ge(ln_mean, b + 1)
                dve.tensor_scalar(ve[:, :], mv[:, :, 1], EPS, None, ALU.add).then_inc(ln_var, 1)
                dve.wait_ge(ln_rstd, b + 1)
                dve.wait_ge(h_store, (b + 1) * (16 * TT))
                for t in range(TT):
                    dve.tensor_scalar(hs[:, t, :], xs[:, t, :], mv[:, t, 0:1], rstd[:, t:t + 1],
                                      ALU.subtract, ALU.mult).then_inc(hs_done, 1)
                for k in range(KC):
                    dve.wait_ge(xt_h, b * KC + k + 1)
                    dve.tensor_tensor(xt_lo[:, k, :], bank[k % 2][:, :], f32(xt_hi[:, k, :]),
                                      ALU.subtract).then_inc(xt_l, 1)
                dve.wait_ge(kv_mm, b * 2 + 1)
                dve.tensor_tensor(k_sb[:, :, :], bank[6][:, 0:KC * T].rearrange("p (k t) -> p k t", k=KC),
                                  bcol[:, 1, :].unsqueeze(2).to_broadcast([P, KC, T]), ALU.add).then_inc(kv_sb, 1)
                dve.wait_ge(kv_mm, b * 2 + 2)
                dve.tensor_tensor(v_sb[:, :], bank[7][:, :], rows[:, 0, :], ALU.add).then_inc(kv_sb, 1)
                dve.wait_ge(kv_sb, b * 2 + 2)
                dve.wait_ge(bd_h, b * 8 + 8)
                for g in range(4):
                    r = slice(g * HD, g * HD + HD)
                    c = slice((g % 2) * T, (g % 2) * T + T)
                    dve.tensor_tensor(kbd_lo[r, :, g // 2, c], k_sb[r, :, :], f32(kbd_hi[r, :, g // 2, c]),
                                      ALU.subtract).then_inc(bd_l, 1)
                for q in range(2):
                    for g in range(2):
                        r = slice(g * T, g * T + T)
                        dve.tensor_tensor(vbd_lo[r, :, q, 2 * q + g, :],
                                          v_sb[r, :].rearrange("p (m a d) -> p m a d", m=KC, a=4)[:, :, 2 * q + g, :],
                                          f32(vbd_hi[r, :, q, 2 * q + g, :]), ALU.subtract).then_inc(bd_l, 1)
                for m in range(KC):
                    dve.wait_ge(q_h, b * KC + m + 1)
                    dve.scalar_tensor_tensor(out=q_lo[:, m, :], in0=bank[2 + m % 2][:, :], scalar=bcol[:, 0, m:m + 1],
                                             in1=f32(q_hi[:, m, :]), op0=ALU.add, op1=ALU.subtract).then_inc(q_l, 1)

                def o_norm(m):
                    dve.wait_ge(pair_mm, b * PAIRS + 2 * m + 2)
                    dve.reciprocal(rden[:, m % 2, :], bank[7][:, :]).then_inc(den_r, 1)
                    dve.wait_ge(den_r, b * KC + m + 1)
                    dve.tensor_tensor(o_sb[:, m % 2, :], bank[6][:, :], rden[:, m % 2, :], ALU.mult).then_inc(o_n, 1)
                    dve.wait_ge(o_h, b * KC + m + 1)
                    dve.tensor_tensor(o_lo[:, m, :], o_sb[:, m % 2, :], f32(o_hi[:, m, :]), ALU.subtract).then_inc(o_l, 1)

                for pr_ in range(PAIRS):
                    dve.wait_ge(s_mm, b * PAIRS + pr_ + 1)
                    if pr_ >= 2:
                        dve.wait_ge(s_exp, b * PAIRS + pr_ - 1)
                    dve.tensor_scalar(sc[:, pr_ % 2, :], bank[4 + pr_ % 2][:, :], lim[:, bass.ds(b, 1)], -CLIP,
                                      ALU.min, ALU.max).then_inc(s_clip, 1)
                    if pr_ >= 3 and pr_ % 2 == 1:
                        o_norm(pr_ // 2 - 1)
                o_norm(KC - 1)
                for t in range(TT):
                    n = b * TT + t
                    dve.wait_ge(d_mm, n + 1)
                    dve.scalar_tensor_tensor(out=d_sb[:, t, :], in0=bank[2 + t % 2][:, :], scalar=tg[:, 2:3],
                                             in1=rows[:, 1, :], op0=ALU.mult, op1=ALU.add).then_inc(d_ready, 1)
                    dve.wait_ge(d_ready, n + 1)
                    dve.bn_stats(st6[:, t, :], d_sb[:, t, :]).then_inc(dstats, 1)
                    plain(dve)
                    dve.wait_ge(dstats, n + 1)
                    dve.bn_aggr(mv[:, t, :], st6[:, t, :]).then_inc(dmean, 1)
                    dve.wait_ge(dmean, n + 1)
                    dve.tensor_scalar(ve[:, t:t + 1], mv[:, t, 1:2], EPS, None, ALU.add).then_inc(dvar, 1)
                    dve.wait_ge(drstd, n + 1)
                    dve.tensor_scalar(d_sb[:, t, :], d_sb[:, t, :], mv[:, t, 0:1], rstd[:, t:t + 1],
                                      ALU.subtract, ALU.mult).then_inc(dnorm, 1)
                    dve.wait_ge(x1_done, n + 1)
                    dve.bn_stats(st6[:, t, :], xs[:, t, :]).then_inc(hstats, 1)
                    plain(dve)
                    dve.wait_ge(hstats, n + 1)
                    dve.bn_aggr(mv[:, t, :], st6[:, t, :]).then_inc(hmean, 1)
                    dve.wait_ge(hmean, n + 1)
                    dve.tensor_scalar(ve[:, t:t + 1], mv[:, t, 1:2], EPS, None, ALU.add).then_inc(hvar, 1)
                    dve.wait_ge(hrstd, n + 1)
                    dve.tensor_scalar(hs[:, t, :], xs[:, t, :], mv[:, t, 0:1], rstd[:, t:t + 1],
                                      ALU.subtract, ALU.mult).then_inc(h_done, 1)
                dve.wait_ge(lg_mm, b + 1)
                dve.tensor_copy(logits[:, bass.ds(b * TT, TT), :],
                                bank[4][:, 0:TT * E].rearrange("p (t e) -> p t e", e=E)).then_inc(lg_done, 1)

            step = [0]

            def link(ins):
                step[0] += 1
                ins.then_inc(rt, 1)
                dve.wait_ge(rt, step[0])

            def bc(ap):
                return ap.to_broadcast(NE3)

            dve.wait_ge(rt_pool, 11)
            dve.wait_ge(h_store, 16 * (NT + TT))
            dve.wait_ge(lg_done, NB)
            link(dve.tensor_reduce(m1[:, :, 0], logits[:, :, :], AX.X, ALU.max))

            def choose(oh, lg, m):
                link(dve.tensor_tensor(eq[:, :, :], lg, bc(m[:, :, :]), ALU.is_equal))
                link(dve.scalar_tensor_tensor(out=tmp3[:, :, :], in0=eq[:, :, :], scalar=-float(E),
                                              in1=iota_e[:, :, :], op0=ALU.mult, op1=ALU.add))
                link(dve.tensor_reduce(i1[:, :, 0], tmp3[:, :, :], AX.X, ALU.min))
                link(dve.tensor_scalar(tmp3[:, :, :], iota_e[:, :, :], -float(E), None, ALU.add))
                link(dve.tensor_tensor(oh, tmp3[:, :, :], bc(i1[:, :, :]), ALU.is_equal))

            choose(oh1[:, :, :], logits[:, :, :], m1)
            link(dve.scalar_tensor_tensor(out=lg2[:, :, :], in0=oh1[:, :, :], scalar=NEG_BIG,
                                          in1=logits[:, :, :], op0=ALU.mult, op1=ALU.add))
            link(dve.tensor_reduce(m2[:, :, 0], lg2[:, :, :], AX.X, ALU.max))
            choose(oh2[:, :, :], lg2[:, :, :], m2)
            link(dve.tensor_tensor(sel[:, :, :], oh1[:, :, :], oh2[:, :, :], ALU.add))
            sel_step[0] = step[0]
            link(dve.tensor_tensor(wk[:, 1, :], m2[:, :, 0], m1[:, :, 0], ALU.subtract))
            diff_step[0] = step[0]
            dve.wait_ge(rt_act, 1)
            link(dve.tensor_scalar(wden[:, :], wk[:, 1, :], 1.0, None, ALU.add))
            link(dve.reciprocal(wk[:, 0, :], wden[:, :]))
            link(dve.tensor_scalar(wk[:, 0, :], wk[:, 0, :], tg[:, 1:2], None, ALU.mult))
            link(dve.tensor_tensor(wk[:, 1, :], wk[:, 1, :], wk[:, 0, :], ALU.mult))
            dve.wait_ge(rt_pe, 1)
            link(dve.tensor_copy(nexp[:, :], bank[1][:, 0:E]))
            link(dve.tensor_tensor(cmp_n[:, :, :], nexp[:, :].unsqueeze(2).to_broadcast([P, E, 16]),
                                   iota_n[:, :, :], ALU.is_gt))
            link(dve.tensor_reduce(tl[:, :, 0], cmp_n[:, :, :], AX.X, ALU.add))
            link(dve.tensor_scalar(tl[:, :, 0], tl[:, :, 0], 1.0, None, ALU.max))
            link(dve.tensor_tensor(trm[:, :, :], tri[:, :, :],
                                   tl[:, :, 0].unsqueeze(1).to_broadcast([P, E, E]), ALU.mult))
            link(dve.tensor_reduce(tend[:, :, 0], trm[:, :, :], AX.X, ALU.add))
            link(dve.tensor_tensor(base[:, :], tend[:, :, 0], tl[:, :, 0], ALU.subtract))
            link(dve.tensor_scalar(base[:, :], base[:, :], float(P), None, ALU.mult))
            link(dve.tensor_tensor(posn[:, :, :], bank[0][:, 0:NT * E].rearrange("p (t e) -> p t e", e=E),
                                   base[:, :].unsqueeze(1).to_broadcast(NE3), ALU.add))
            for c, oh in enumerate((oh1, oh2)):
                link(dve.tensor_tensor(tmp3[:, :, :], posn[:, :, :], oh[:, :, :], ALU.mult))
                link(dve.tensor_reduce(slot[:, c, :], tmp3[:, :, :], AX.X, ALU.add))
            link(dve.tensor_copy(slot_i[:, :, :], slot[:, :, :]))
            link(dve.tensor_scalar(sa_i[:, :, :], slot_i[:, :, :], 7, None, ALU.logical_shift_right))
            link(dve.tensor_scalar(sb_i[:, :, :], slot_i[:, :, :], P - 1, None, ALU.bitwise_and))
            link(dve.tensor_copy(sa[:, :, :], sa_i[:, :, :]))
            link(dve.tensor_copy(sbp[:, :, :], sb_i[:, :, :]))
            for c in range(TOPK):
                link(dve.tensor_tensor(ohe[:, :, :], iota40[:, :].unsqueeze(1).to_broadcast([P, NT, SLOTT]),
                                       sa[:, c, :].unsqueeze(2).to_broadcast([P, NT, SLOTT]), ALU.is_equal))
                link(dve.tensor_tensor(oha[:, c, :, 0, :], ohe[:, :, :],
                                       tok1[:, :].unsqueeze(2).to_broadcast([P, NT, SLOTT]), ALU.mult))
                link(dve.tensor_tensor(oha[:, c, :, 1, :], ohe[:, :, :],
                                       wk[:, c, :].unsqueeze(2).to_broadcast([P, NT, SLOTT]), ALU.mult))
            for c in range(TOPK):
                if c:
                    dve.wait_ge(rt_pe, 1 + c)
                link(dve.tensor_tensor(ohb[:, :, :], iota128[:, :].unsqueeze(1).to_broadcast([P, NT, P]),
                                       sbp[:, c, :].unsqueeze(2).to_broadcast([P, NT, P]), ALU.is_equal))
                ohb_step[c] = step[0]
            link(dve.tensor_tensor(ind[:, :, :], iota40[:, :].unsqueeze(1).to_broadcast([P, E, SLOTT]),
                                   tend[:, :, :].to_broadcast([P, E, SLOTT]), ALU.is_ge))
            link(dve.tensor_reduce(tabf[:, :, 0], ind[:, 0:E - 1, :].rearrange("p e n -> p n e"), AX.X, ALU.add))
            link(dve.memset(tabf[:, :, 1:4], 0.0))
            link(dve.tensor_tensor(tabf[:, 0:SLOTT - 1, 1], tabf[:, 1:SLOTT, 0], tabf[:, 0:SLOTT - 1, 0], ALU.subtract))
            link(dve.tensor_copy(tabf[:, 1:SLOTT, 2], tabf[:, 0:SLOTT - 1, 1]))
            link(dve.memset(tabf[:, 0:1, 2:3], 1.0))
            link(dve.tensor_copy(tile_tab[:, :, :], tabf[:, :, :]))
            link(dve.tensor_copy(n_tiles[:, 0:1], tend[:, E - 1, :]))
            dve.wait_ge(rt_pe, 1 + TOPK)
            link(dve.tensor_copy(slot_w[:, :], bank[2][:, SLOTT:2 * SLOTT]))
            link(dve.tensor_copy(tv[:, :], bank[2][:, 0:SLOTT]))
            link(dve.tensor_scalar(tz[:, :], tv[:, :], 0.0, pidx[:, 0:1], ALU.is_equal, ALU.mult))
            link(dve.scalar_tensor_tensor(out=tz[:, :], in0=tv[:, :], scalar=-1.0, in1=tz[:, :],
                                          op0=ALU.add, op1=ALU.add))
            link(dve.tensor_copy(slot_idx[:, :], tz[:, :]))
            dve.sem_inc(tables, 1)

            def split_lo(dst, hi, p, done):
                dve.tensor_tensor(dst.rearrange("p k n -> p (k n)"), raw[:, p, :],
                                  f32(hi.rearrange("p k n -> p (k n)")), ALU.subtract).then_inc(done, 1)

            for p in range(GU):
                dve.wait_ge(gu_hi, p + 1)
                split_lo(g_lo[:, p, :, :], g_hi[:, p, :, :], p, gu_split)
            dve.wait_ge(gt_h, 1)
            dve.tensor_tensor(gt_lo[:, :, :].rearrange("p k n -> p (k n)"), bank[6][:, :],
                              f32(gt_hi[:, :, :].rearrange("p k n -> p (k n)")), ALU.subtract).then_inc(gt_l, 1)
            used = dve.value_load(n_tiles[0:1, 0:1], min_val=1, max_val=MAXT)
            with dve.Fori(0, used) as g:
                expert = dve.value_load(tile_tab[0:1, bass.ds(g, 1), 0:1].rearrange("p a b -> p (a b)"), min_val=0, max_val=E - 1)
                last = dve.value_load(tile_tab[0:1, bass.ds(g, 1), 1:2].rearrange("p a b -> p (a b)"), min_val=0, max_val=1)
                first = dve.value_load(tile_tab[0:1, bass.ds(g, 1), 2:3].rearrange("p a b -> p (a b)"), min_val=0, max_val=1)

                def hidden_lo(p):
                    dve.wait_ge(hd_h, g * GU + p + 1)
                    dve.tensor_tensor(hd_lo[:, 2 * p:2 * p + 2, :].rearrange("p k n -> p (k n)"),
                                      bank[4 + p % 2][:, 0:256],
                                      f32(hd_hi[:, 2 * p:2 * p + 2, :].rearrange("p k n -> p (k n)")),
                                      ALU.subtract).then_inc(hd_l, 1)

                for p in range(GU):
                    dve.wait_ge(silu_done, g * GU + p + 1)
                    dve.tensor_tensor(hid[:, p, :], silu[:, p, :], bank[p][:, 256:512], ALU.mult).then_inc(hid_done, 1)
                    if p >= 1:
                        hidden_lo(p - 1)
                    with dve.If(last):
                        dve.wait_ge(gu_hi, expert * GU + GU + p + 1)
                        split_lo(g_lo[:, p, :, :], g_hi[:, p, :, :], p, gu_split)
                    if p < DH:
                        with dve.If(first):
                            dve.wait_ge(dn_h, expert * DH + p + 1)
                            split_lo(dn_lo[:, p, :, :], dn_hi[:, p, :, :], GU + p, dn_split)
                hidden_lo(GU - 1)
                dve.wait_ge(gt_h, g + 2)
                dve.tensor_tensor(gt_lo[:, :, :].rearrange("p k n -> p (k n)"), bank[6][:, :],
                                  f32(gt_hi[:, :, :].rearrange("p k n -> p (k n)")), ALU.subtract).then_inc(gt_l, 1)

        @block.scalar
        def _(act):
            act.sem_inc(y_free, 1)
            act.wait_ge(cload, 80)
            act.activation(tg[:, 0:2], gsc[:, 0:2], ACT.Tanh).then_inc(gates_ready, 1)
            for w in range(4):
                act.wait_ge(wload[w], 16)
                act.activation(w_hi[:, w, :, :].rearrange("p k n -> p (k n)"), raw[:, w, :],
                               ACT.Copy).then_inc(w_hi_done, 1)
            act.wait_ge(zdone, 2)
            act.wait_ge(dset, 4)
            with act.Fori(0, NB) as b:
                act.wait_ge(crload, (b + 1) * 32)
                act.activation(c_hi[:, :, :, :], c_raw[:, :, :, :], ACT.Copy).then_inc(c_h, 1)
                for k in range(KC):
                    act.wait_ge(xt_tr, b * KC + k + 1)
                    act.activation(xt_hi[:, k, :], bank[k % 2][:, :], ACT.Copy).then_inc(xt_h, 1)
                act.wait_ge(kv_sb, b * 2 + 2)
                for g in range(4):
                    r = slice(g * HD, g * HD + HD)
                    act.activation(kbd_hi[r, :, g // 2, (g % 2) * T:(g % 2) * T + T], k_sb[r, :, :],
                                   ACT.Copy).then_inc(bd_h, 1)
                for q in range(2):
                    for g in range(2):
                        r = slice(g * T, g * T + T)
                        act.activation(vbd_hi[r, :, q, 2 * q + g, :],
                                       v_sb[r, :].rearrange("p (m a d) -> p m a d", m=KC, a=4)[:, :, 2 * q + g, :],
                                       ACT.Copy).then_inc(bd_h, 1)
                for m in range(KC):
                    act.wait_ge(q_mm, b * KC + m + 1)
                    act.activation(q_hi[:, m, :], bank[2 + m % 2][:, :], ACT.Identity,
                                   bias=bcol[:, 0, m:m + 1]).then_inc(q_h, 1)

                def o_high(m):
                    act.wait_ge(o_n, b * KC + m + 1)
                    act.activation(o_hi[:, m, :], o_sb[:, m % 2, :], ACT.Copy).then_inc(o_h, 1)

                for pr_ in range(PAIRS):
                    act.wait_ge(s_clip, b * PAIRS + pr_ + 1)
                    if pr_ >= 2:
                        act.wait_ge(e_l, b * PAIRS + pr_ - 1)
                    act.activation(ex[:, pr_ % 2, :], sc[:, pr_ % 2, :], ACT.Exp,
                                   scale=INV_SCALE).then_inc(s_exp, 1)
                    act.wait_ge(s_exp, b * PAIRS + pr_ + 1)
                    if pr_ >= 2:
                        act.wait_ge(pair_mm, b * PAIRS + pr_ - 1)
                    act.activation(ex_hi[:, pr_ % 2, :], ex[:, pr_ % 2, :], ACT.Copy).then_inc(e_h, 1)
                    if pr_ >= 3 and pr_ % 2 == 1:
                        o_high(pr_ // 2 - 1)
                o_high(KC - 1)
                for t in range(TT):
                    act.wait_ge(h_tr, b * TT + t + 1)
                    act.activation(ht[:, t % 2, :, :].rearrange("p k n -> p (k n)"), bank[t % 2][:, :],
                                   ACT.Copy).then_inc(h_ev, 1)
            act.wait_ge(rt, diff_step[0])
            act.activation(wk[:, 1, :], wk[:, 1, :], ACT.Exp).then_inc(rt_act, 1)

            act.wait_ge(tables, 1)

            def split_hi(dst, p, done):
                act.activation(dst.rearrange("p k n -> p (k n)"), raw[:, p, :], ACT.Copy).then_inc(done, 1)

            for p in range(GU):
                act.wait_ge(raw_in[p], 16)
                split_hi(g_hi[:, p, :, :], p, gu_hi)
            act.wait_ge(gt_tr, 1)
            act.activation(gt_hi[:, :, :].rearrange("p k n -> p (k n)"), bank[6][:, :], ACT.Copy).then_inc(gt_h, 1)
            used = act.value_load(n_tiles[0:1, 0:1], min_val=1, max_val=MAXT)
            with act.Fori(0, used) as g:
                expert = act.value_load(tile_tab[0:1, bass.ds(g, 1), 0:1].rearrange("p a b -> p (a b)"), min_val=0, max_val=E - 1)
                last = act.value_load(tile_tab[0:1, bass.ds(g, 1), 1:2].rearrange("p a b -> p (a b)"), min_val=0, max_val=1)
                first = act.value_load(tile_tab[0:1, bass.ds(g, 1), 2:3].rearrange("p a b -> p (a b)"), min_val=0, max_val=1)

                def hidden_hi(p):
                    act.wait_ge(hd_tr, g * GU + p + 1)
                    act.activation(hd_hi[:, 2 * p:2 * p + 2, :].rearrange("p k n -> p (k n)"),
                                   bank[4 + p % 2][:, 0:256], ACT.Copy).then_inc(hd_h, 1)

                for p in range(GU):
                    act.wait_ge(gu_mm, g * GU + p + 1)
                    act.activation(silu[:, p, :], bank[p][:, 0:256], ACT.Silu).then_inc(silu_done, 1)
                    if p >= 1:
                        hidden_hi(p - 1)
                    with act.If(last):
                        act.wait_ge(raw_in[p], expert * 16 + 32)
                        split_hi(g_hi[:, p, :, :], p, gu_hi)
                    if p < DH:
                        with act.If(first):
                            act.wait_ge(raw_in[GU + p], expert * 16 + 16)
                            split_hi(dn_hi[:, p, :, :], GU + p, dn_h)
                hidden_hi(GU - 1)
                act.wait_ge(gt_tr, g + 2)
                act.activation(gt_hi[:, :, :].rearrange("p k n -> p (k n)"), bank[6][:, :], ACT.Copy).then_inc(gt_h, 1)
                act.wait_ge(y_mm, g + 1)
                act.wait_ge(y_free, g + 1)
                act.activation(y_sb[:, :], bank[7][:, :], ACT.Copy, scale=slot_w[:, bass.ds(g, 1)]).then_inc(y_ready, 1)

        @block.tensor
        def _(pe):
            pe.sem_inc(y_ready, 1)
            pe.wait_ge(setup, 12)
            pe.wait_ge(w_lo_done, 4)
            pe.wait_ge(cload, 80)
            with pe.Fori(0, NB) as b:
                pe.wait_ge(hs_done, (b + 1) * TT)
                for k in range(KC):
                    if k >= 2:
                        pe.wait_ge(xt_l, b * KC + k - 1)
                    for t in range(TT):
                        tr = pe.transpose(bank[k % 2][:, t * P:(t + 1) * P], hs[:, t, k * P:(k + 1) * P], ident[:, :])
                    tr.then_inc(xt_tr, 1)
                pe.wait_ge(c_l, b + 2)
                for m in range(KC):
                    mm = product3(pe, bank[6][:, m * T:(m + 1) * T],
                                  lambda k: w_hi[:, 1, k, m * P:(m + 1) * P], lambda k: w_lo[:, 1, k, m * P:(m + 1) * P],
                                  lambda k: c_hi[:, k, 0, :], lambda k: c_lo[:, k, 0, :])
                mm.then_inc(kv_mm, 1)
                product3(pe, bank[7][:, :],
                         lambda k: c_hi[:, k, :, :].rearrange("p a t -> p (a t)"),
                         lambda k: c_lo[:, k, :, :].rearrange("p a t -> p (a t)"),
                         lambda k: w_hi[:, 2, k, :], lambda k: w_lo[:, 2, k, :]).then_inc(kv_mm, 1)
                pe.wait_ge(xt_l, b * KC + KC)
                for m in range(KC):
                    if m >= 2:
                        pe.wait_ge(q_l, b * KC + m - 1)
                    product3(pe, bank[2 + m % 2][:, :],
                             lambda k: w_hi[:, 0, k, m * P:(m + 1) * P], lambda k: w_lo[:, 0, k, m * P:(m + 1) * P],
                             lambda k: xt_hi[:, k, :], lambda k: xt_lo[:, k, :]).then_inc(q_mm, 1)
                pe.wait_ge(bd_l, b * 8 + 8)

                def scores(pr_):
                    m, j = pr_ // 2, pr_ % 2
                    pe.wait_ge(q_l, b * KC + m + 1)
                    if pr_ >= 2:
                        pe.wait_ge(s_clip, b * PAIRS + pr_ - 1)
                    product3(pe, bank[4 + j][:, :],
                             lambda k: kbd_hi[:, m, j, :], lambda k: kbd_lo[:, m, j, :],
                             lambda k: q_hi[:, m, :], lambda k: q_lo[:, m, :], n=1).then_inc(s_mm, 1)

                def pv(pr_):
                    m, j = pr_ // 2, pr_ % 2
                    pe.wait_ge(e_l, b * PAIRS + pr_ + 1)
                    if j == 0 and m >= 1:
                        pe.wait_ge(o_n, b * KC + m)
                    product3(pe, bank[6][:, :],
                             lambda k: vbd_hi[:, m, j, :, :].rearrange("p a d -> p (a d)"),
                             lambda k: vbd_lo[:, m, j, :, :].rearrange("p a d -> p (a d)"),
                             lambda k: ex_hi[:, j, :], lambda k: ex_lo[:, j, :], n=1, first=(j == 0), last=(j == 1))
                    for a, e_ in enumerate((ex_hi, ex_lo)):
                        mm = pe.matmul(bank[7][:, :], obd[:, j, :, :].rearrange("p a d -> p (a d)"), e_[:, j, :],
                                       start=(j == 0 and a == 0), stop=(j == 1 and a == 1))
                    mm.then_inc(pair_mm, 1)

                for pr_ in range(PAIRS + 1):
                    if pr_ < PAIRS:
                        scores(pr_)
                    if pr_ >= 1:
                        pv(pr_ - 1)
                pe.wait_ge(o_l, b * KC + KC)
                for t in range(TT):
                    if t >= 2:
                        pe.wait_ge(d_ready, b * TT + t - 1)
                    product3(pe, bank[2 + t % 2][:, :],
                             lambda k: o_hi[:, k, t * P:(t + 1) * P], lambda k: o_lo[:, k, t * P:(t + 1) * P],
                             lambda k: w_hi[:, 3, k, :], lambda k: w_lo[:, 3, k, :]).then_inc(d_mm, 1)
                for t in range(TT):
                    pe.wait_ge(h_done, b * TT + t + 1)
                    for k in range(KC):
                        tr = pe.transpose(bank[t % 2][:, k * P:(k + 1) * P], hs[:, t, k * P:(k + 1) * P], ident[:, :])
                    tr.then_inc(h_tr, 1)
                    pe.wait_ge(h_ev, b * TT + t + 1)
                    for k in range(KC):
                        mm = pe.matmul(bank[4][:, t * E:(t + 1) * E], ht[:, t % 2, k, :], gate_w[:, k, :],
                                       start=(k == 0), stop=(k == KC - 1))
                mm.then_inc(lg_mm, 1)

            pe.wait_ge(rt_pool, 11)
            pe.wait_ge(rt, sel_step[0])
            selv = sel[:, :, :].rearrange("p t e -> p (t e)")
            pe.matmul(bank[0][:, 0:NT * E], upper[:, :], selv, start=True, stop=False, skip_group_check=True)
            for s in range(1, NT):
                pe.matmul(bank[0][:, s * E:NT * E], ones[:, :], selv[:, 0:(NT - s) * E],
                          start=False, stop=(s == NT - 1), skip_group_check=True)
            for t in range(NT):
                mm = pe.matmul(bank[1][:, 0:E], ones[:, :], selv[:, t * E:(t + 1) * E], start=(t == 0), stop=(t == NT - 1))
            mm.then_inc(rt_pe, 1)
            for c in range(TOPK):
                pe.wait_ge(rt, ohb_step[c])
                for t in range(NT):
                    mm = pe.matmul(bank[2][:, 0:2 * SLOTT], ohb[:, t, :],
                                   oha[:, c, t, :, :].rearrange("p a n -> p (a n)"),
                                   start=(c == 0 and t == 0), stop=(c == TOPK - 1 and t == NT - 1))
                mm.then_inc(rt_pe, 1)

            pe.wait_ge(tables, 1)

            def slot_rows(n):
                pe.wait_ge(gath, n * 16 + 16)
                for k in range(KC):
                    tr = pe.transpose(bank[6][:, k * P:(k + 1) * P], xg[:, k * P:(k + 1) * P], ident[:, :])
                tr.then_inc(gt_tr, 1)

            slot_rows(0)
            used = pe.value_load(n_tiles[0:1, 0:1], min_val=1, max_val=MAXT)
            with pe.Fori(0, used) as g:
                expert = pe.value_load(tile_tab[0:1, bass.ds(g, 1), 0:1].rearrange("p a b -> p (a b)"), min_val=0, max_val=E - 1)

                def hidden_t(p):
                    pe.wait_ge(hid_done, g * GU + p + 1)
                    pe.wait_ge(hd_l, g * GU + p + 1)
                    for c in range(2):
                        tr = pe.transpose(bank[4 + p % 2][:, c * P:(c + 1) * P], hid[:, p, c * P:(c + 1) * P], ident[:, :])
                    tr.then_inc(hd_tr, 1)

                def down(c):
                    if c % 2 == 0:
                        pe.wait_ge(hd_l, g * GU + c // 2 + 3)
                    if c % 4 == 0:
                        pe.wait_ge(dn_split, expert * DH + c // 4 + 1)
                    if c == 0:
                        pe.wait_ge(y_ready, g + 1)
                    mm = product3(pe, bank[7][:, :], lambda k: hd_hi[:, c, :], lambda k: hd_lo[:, c, :],
                                  lambda k: dn_hi[:, c // 4, c % 4, :], lambda k: dn_lo[:, c // 4, c % 4, :],
                                  n=1, first=(c == 0), last=(c == IC - 1))
                    if c == IC - 1:
                        mm.then_inc(y_mm, 1)

                pe.wait_ge(gt_l, g + 1)
                for p in range(GU):
                    pe.wait_ge(gu_split, expert * GU + p + 1)
                    product3(pe, bank[p][:, :], lambda k: gt_hi[:, k, :], lambda k: gt_lo[:, k, :],
                             lambda k: g_hi[:, p, k, :], lambda k: g_lo[:, p, k, :]).then_inc(gu_mm, 1)
                    if p >= 1:
                        hidden_t(p - 1)
                down(0)
                down(1)
                hidden_t(GU - 1)
                down(2)
                down(3)
                slot_rows(g + 1)
                for c in range(4, IC):
                    down(c)


sel_step, diff_step, ohb_step = [0], [0], [0, 0]


def kernel(x, ctx_2048, mask_BxS2_ik0, g_xattn, g_ffn, L0_xattn_Wq, L0_xattn_bq, L0_xattn_Wk, L0_xattn_bk,
           L0_xattn_Wv, L0_xattn_bv, L0_xattn_Wo, L0_xattn_bo, L0_xattn_ln_gamma, L0_xattn_ln_beta,
           L0_xattn_residual_scale, L0_ffn_gate_weight, L0_ffn_gate_up_proj, L0_ffn_down_proj):
    import numpy as np
    import concourse.bacc as bacc
    from concourse.bass_utils import run_bass_kernel_spmd

    def c(a):
        return np.ascontiguousarray(np.asarray(a))

    def by_rows(w):
        return np.asarray(w).T.reshape(-1, P, w.shape[0]).transpose(1, 0, 2)

    mask = np.tile(np.asarray(mask_BxS2_ik0).T, (2, 1))
    ctx_t = np.asarray(ctx_2048).transpose(0, 2, 1).reshape(NB, KC, P, T).transpose(0, 2, 1, 3)
    w_attn = np.stack([by_rows(w).reshape(P, KC * H) for w in (L0_xattn_Wq, L0_xattn_Wk, L0_xattn_Wv, L0_xattn_Wo)])
    b_cols = np.stack([np.asarray(b).reshape(KC, P).T for b in (L0_xattn_bq, L0_xattn_bk)], axis=1)
    b_rows = np.stack([np.asarray(b) for b in (L0_xattn_bv, L0_xattn_bo, L0_xattn_ln_gamma, L0_xattn_ln_beta)])
    gates = np.concatenate([np.asarray(g).reshape(1) for g in (g_xattn, g_ffn, L0_xattn_residual_scale)])
    gate_t = by_rows(L0_ffn_gate_weight)
    gu = np.asarray(L0_ffn_gate_up_proj).reshape(E, 2, GU, 256, KC, P).transpose(0, 2, 5, 4, 1, 3)
    dn = np.asarray(L0_ffn_down_proj).reshape(E, H, DH, 4, P).transpose(0, 2, 4, 3, 1)
    w_exp = np.concatenate([gu.reshape(E, GU, P, PW), dn.reshape(E, DH, P, PW)], axis=1)

    ins = dict(x=np.asarray(x).reshape(TOK, H), ctx_t=ctx_t, mask=mask, w_attn=w_attn, b_cols=b_cols,
               b_rows=b_rows, gates=gates, gate_t=gate_t, w_exp=w_exp)
    nc = bacc.Bacc("TRN2", target_bir_lowering=False, num_devices=1)
    arrays, aps = {}, {}
    for name, a in ins.items():
        arrays[f"in_{name}"] = c(a)
        aps[name] = nc.dram_tensor(f"in_{name}", a.shape, mybir.dt.from_np(a.dtype), kind="ExternalInput").ap()
    out = nc.dram_tensor("out_rows", [TOK + P, H], F32, kind="ExternalOutput").ap()
    flamingo_gated_block(nc, out=out, **aps)
    r = run_bass_kernel_spmd(nc, [arrays], core_ids=[0])
    return r.results[0]["out_rows"][:TOK].reshape(NB, S, H)
```

```python
import concourse.bass as bass
from concourse import mybir
from contextlib import ExitStack

ALU = mybir.AluOpType
ACT = mybir.ActivationFunctionType
AX = mybir.AxisListType
F32 = mybir.dt.float32
F32R = mybir.dt.float32r
I32 = mybir.dt.int32

P = 128
H = 512
KC = H // P
NB = 4
S = 512
TT = S // P
NT = NB * TT
TOK = NB * S
T = 64
CT = (NB + 1) * T
NH, HD = 16, 32
PAIRS = NH // 2
E = 8
I = 1024
TOPK = 2
GU = 4
DH = 2
PW = 4 * 512
IC = I // P
MAXT = TOK * TOPK // P + E - 1
SLOTT = MAXT + 1
EPS = 1e-5
INV_SCALE = float(HD) ** -0.5
CLIP = 50.0 / INV_SCALE
NEG_BIG = -3.0e38


def flamingo_gated_block(nc, x, ctx_t, mask, w_attn, b_cols, b_rows, gates, gate_t, w_exp, out):
    st = ExitStack()
    with st:
        def sb(name, shape, dt=F32, scope=st):
            return scope.enter_context(nc.sbuf_tensor(name, shape, dt))

        def sem(name):
            return st.enter_context(nc.semaphore(name))

        bank = [st.enter_context(nc.psum_tensor(f"bank{i}", [P, 512], F32)) for i in range(8)]
        h_dram = nc.dram_tensor("h_rows", [TOK + P, H], F32).ap()
        h_rows = h_dram.rearrange("(n p) d -> n p d", p=P)
        out_rows = out.rearrange("(n p) d -> n p d", p=P)
        x_b = x.rearrange("(b t p) d -> b p t d", p=P, t=TT)

        ident = sb("ident", [P, P])
        logits = sb("logits", [P, NT, E])
        gate_w = sb("gate_w", [P, KC, E])
        gsc = sb("gsc", [P, 3])
        tg = sb("tg", [P, 3])
        slot_idx = sb("slot_idx", [P, SLOTT], I32)
        slot_w = sb("slot_w", [P, SLOTT])
        tile_tab = sb("tile_tab", [P, SLOTT, 4], I32)
        n_tiles = sb("n_tiles", [P, 4], I32)

        pa = ExitStack()
        o_hi = sb("o_hi", [P, KC, S], F32R, pa)
        o_lo = sb("o_lo", [P, KC, S], F32R, pa)
        dh = sb("dh", [P, TT, H], F32, pa)
        xr = sb("xr", [P, TT, H], F32, pa)
        o_un = sb("o_un", [P, KC, S], F32, pa)
        sc = sb("sc", [P, 2, S], F32, pa)
        ex = sb("ex", [P, 2, S], F32, pa)
        w_hi = sb("w_hi", [P, 2, KC, H], F32R, pa)
        w_lo = sb("w_lo", [P, 2, KC, H], F32R, pa)
        kvw = ExitStack()
        wkv_hi = sb("wkv_hi", [P, 2, KC, H], F32R, kvw)
        wkv_lo = sb("wkv_lo", [P, 2, KC, H], F32R, kvw)
        kvw.close()
        xt_hi = sb("xt_hi", [P, KC, S], F32R, pa)
        xt_lo = sb("xt_lo", [P, KC, S], F32R, pa)
        q_hi = sb("q_hi", [P, KC, S], F32R, pa)
        q_lo = sb("q_lo", [P, KC, S], F32R, pa)
        c_raw = sb("c_raw", [P, KC, CT], F32, pa)
        cts = ExitStack()
        c_hi = sb("c_hi", [P, KC, CT], F32R, cts)
        c_lo = sb("c_lo", [P, KC, CT], F32R, cts)
        cts.close()
        ex_hi = sb("ex_hi", [P, 2, S], F32R, pa)
        ex_lo = sb("ex_lo", [P, 2, S], F32R, pa)
        ht = sb("ht", [P, 2, KC, P], F32, pa)
        k_all = sb("k_all", [P, KC, NB * T], F32, pa)
        v_all = sb("v_all", [P, NB + 1, H], F32, pa)
        kbd_hi = sb("kbd_hi", [P, KC, P], F32R, pa)
        kbd_lo = sb("kbd_lo", [P, KC, P], F32R, pa)
        vbd_hi = sb("vbd_hi", [P, KC, 2, 4, HD], F32R, pa)
        vbd_lo = sb("vbd_lo", [P, KC, 2, 4, HD], F32R, pa)
        hsel = sb("hsel", [P, P + NH], F32R, pa)
        bsel = sb("bsel", [NH, KC, 4, HD], F32R, pa)
        den = sb("den", [NH, S], F32, pa)
        rden = sb("rden", [NH, S], F32, pa)
        r_hi = sb("r_hi", [NH, S], F32R, pa)
        r_lo = sb("r_lo", [NH, S], F32R, pa)
        xs = sb("xs", [P, TT, H], F32, pa)
        hs = sb("hs", [P, TT, H], F32, pa)
        rows = sb("rows", [P, 4, H], F32, pa)
        o_n = sb("o_n", [P, 2, S], F32, pa)
        bcol = sb("bcol", [P, 2, KC], F32, pa)
        lim = sb("lim", [P, NB], F32, pa)
        mask_sb = sb("mask_sb", [P, NB], I32, pa)
        st_a = sb("st_a", [P, TT, 6], F32, pa)
        mv_a = sb("mv_a", [P, TT, 2], F32, pa)
        ve_a = sb("ve_a", [P, TT], F32, pa)
        rs_a = sb("rs_a", [P, TT], F32, pa)
        mn_a = sb("mn_a", [P, TT], F32, pa)
        nm_a = sb("nm_a", [P, TT], F32, pa)
        st6 = sb("st6", [P, TT, 6], F32, pa)
        mv = sb("mv", [P, TT, 2], F32, pa)
        ve = sb("ve", [P, TT], F32, pa)
        rs = sb("rs", [P, TT], F32, pa)
        st6h = sb("st6h", [P, TT, 6], F32, pa)
        mvh = sb("mvh", [P, TT, 2], F32, pa)
        veh = sb("veh", [P, TT], F32, pa)
        rsh = sb("rsh", [P, TT], F32, pa)
        mhalf = sb("mhalf", [P, TT], F32, pa)
        pa.close()

        pe_ = ExitStack()
        raw = sb("raw", [P, GU + DH, PW], F32, pe_)
        g_hi = sb("g_hi", [P, GU, KC, 512], F32R, pe_)
        g_lo = sb("g_lo", [P, GU, KC, 512], F32R, pe_)
        dn_hi = sb("dn_hi", [P, DH, 4, H], F32R, pe_)
        dn_lo = sb("dn_lo", [P, DH, 4, H], F32R, pe_)
        xg = sb("xg", [P, H], F32, pe_)
        gt_hi = sb("gt_hi", [P, KC, P], F32R, pe_)
        gt_lo = sb("gt_lo", [P, KC, P], F32R, pe_)
        silu = sb("silu", [P, GU, 256], F32, pe_)
        hid = sb("hid", [P, GU, 256], F32, pe_)
        hd_hi = sb("hd_hi", [P, IC, P], F32R, pe_)
        hd_lo = sb("hd_lo", [P, IC, P], F32R, pe_)
        y_sb = sb("y_sb", [P, H], F32, pe_)
        g_idx = sb("g_idx", [P, 1], I32, pe_)
        s_idx = sb("s_idx", [P, 1], I32, pe_)

        pr = ExitStack()
        NE3 = [P, NT, E]
        iota_e = sb("iota_e", NE3, F32, pr)
        eq = sb("eq", NE3, F32, pr)
        oh1 = sb("oh1", NE3, F32, pr)
        oh2 = sb("oh2", NE3, F32, pr)
        sel = sb("sel", NE3, F32, pr)
        lg2 = sb("lg2", NE3, F32, pr)
        posn = sb("posn", NE3, F32, pr)
        tmp3 = sb("tmp3", NE3, F32, pr)
        m1 = sb("m1", [P, NT, 1], F32, pr)
        m2 = sb("m2", [P, NT, 1], F32, pr)
        i1 = sb("i1", [P, NT, 1], F32, pr)
        wk = sb("wk", [P, TOPK, NT], F32, pr)
        wden = sb("wden", [P, NT], F32, pr)
        slot = sb("slot", [P, TOPK, NT], F32, pr)
        slot_i = sb("slot_i", [P, TOPK, NT], I32, pr)
        sa_i = sb("sa_i", [P, TOPK, NT], I32, pr)
        sb_i = sb("sb_i", [P, TOPK, NT], I32, pr)
        sa = sb("sa", [P, TOPK, NT], F32, pr)
        sbp = sb("sbp", [P, TOPK, NT], F32, pr)
        tok1 = sb("tok1", [P, NT], F32, pr)
        iota40 = sb("iota40", [P, SLOTT], F32, pr)
        iota128 = sb("iota128", [P, P], F32, pr)
        pidx = sb("pidx", [P, 1], F32, pr)
        upper = sb("upper", [P, P], F32, pr)
        ones = sb("ones", [P, P], F32, pr)
        iota_n = sb("iota_n", [P, E, 16], F32, pr)
        cmp_n = sb("cmp_n", [P, E, 16], F32, pr)
        nexp = sb("nexp", [P, E], F32, pr)
        tl = sb("tl", [P, E, 1], F32, pr)
        tri = sb("tri", [P, E, E], F32, pr)
        trm = sb("trm", [P, E, E], F32, pr)
        tend = sb("tend", [P, E, 1], F32, pr)
        base = sb("base", [P, E], F32, pr)
        ind = sb("ind", [P, E, SLOTT], F32, pr)
        tabf = sb("tabf", [P, SLOTT, 4], F32, pr)
        ohb = sb("ohb", [P, NT, P], F32, pr)
        oha = sb("oha", [P, TOPK, NT, 2, SLOTT], F32, pr)
        ohe = sb("ohe", [P, NT, SLOTT], F32, pr)
        tv = sb("tv", [P, SLOTT], F32, pr)
        tz = sb("tz", [P, SLOTT], F32, pr)
        pr.close()
        pe_.close()

        def f32(ap):
            return ap.bitcast(F32)

        wload = [sem(f"attn_weights{w}_loaded") for w in range(4)]
        cload, xload, rload, crload, setup = (sem(n) for n in
            ("constants_loaded", "x_loaded", "residual_loaded", "context_loaded", "pool_setup"))
        gates_ready, w_hi_done, w_lo_done = sem("gates_ready"), sem("attn_w_hi"), sem("attn_w_lo")
        dset = sem("vector_setup")
        ln_bias, ln_stats, ln_mean, ln_var, ln_rstd, hs_done = (sem(n) for n in
            ("ln_bias", "ln_stats", "ln_mean", "ln_var", "ln_rstd", "hs_done"))
        xt_tr, xt_h, xt_l = sem("xt_transposed"), sem("xt_hi_done"), sem("xt_lo_done")
        c_h, c_l, kv_mm, kv_sb, k_h, k_l, v_h, v_l = (sem(n) for n in
            ("context_hi", "context_lo", "kv_product", "kv_biased", "k_hi_placed", "k_lo_placed",
             "v_hi_placed", "v_lo_placed"))
        q_mm, q_h, q_l = sem("q_product"), sem("q_hi_done"), sem("q_lo_done")
        s_mm, s_clip, s_exp, e_h, e_l = (sem(n) for n in
            ("scores_product", "scores_clipped", "exp_done", "exp_hi_done", "exp_lo_done"))
        pair_mm, o_ev, den_c, den_r, r_h, r_l, r_mm, o_nd, o_h, o_l = (sem(n) for n in
            ("pair_product", "context_copied", "sums_copied", "sums_inverted", "inverse_hi", "inverse_lo",
             "inverse_spread", "context_normalised", "o_hi_done", "o_lo_done"))
        d_mm, d_ready, dstats, dmean, dvar, drstd, dgam, xb_done, x1_done = (sem(n) for n in
            ("delta_product", "delta_scaled", "delta_stats", "delta_mean", "delta_var", "delta_rstd",
             "delta_gamma", "x_with_beta", "x1_done"))
        hstats, hmean, hvar, hrstd, h_done = (sem(n) for n in ("h_stats", "h_mean", "h_var", "h_rstd", "h_done"))
        h_tr, h_ev, lg_mm, lg_done = (sem(n) for n in ("h_transposed", "h_evacuated", "logits_product", "logits_done"))
        x1_store, h_store, pad_store = sem("x1_stored"), sem("h_stored"), sem("pad_rows_stored")
        rt, rt_pool, rt_act, rt_pe = (sem(n) for n in ("routing_vector", "routing_pool", "routing_act", "routing_product"))
        tables = sem("tables_ready")
        raw_in = [sem(f"raw_piece{p}_loaded") for p in range(GU + DH)]
        gu_hi, gu_split, dn_h, dn_split = (sem(n) for n in ("gu_hi_done", "gu_split_done", "down_hi_done", "down_split_done"))
        idx_0, idx_g, idx_s, gath, scat = (sem(n) for n in ("first_index", "gather_index", "scatter_index", "rows_gathered", "rows_scattered"))
        gt_tr, gt_h, gt_l = sem("slot_rows_transposed"), sem("slot_rows_hi"), sem("slot_rows_lo")
        gu_mm, silu_done, hid_done, hd_tr, hd_h, hd_l = (sem(n) for n in
            ("gate_up_product", "silu_done", "hidden_done", "hidden_transposed", "hidden_hi", "hidden_lo"))
        y_mm, y_ready, y_free = sem("down_product"), sem("y_ready"), sem("y_added")

        block = st.enter_context(nc.Block())

        def product3(eng, psum, a_hi, a_lo, b_hi, b_lo, n=KC, first=True, last=True):
            for k in range(n):
                for j, (a, b) in enumerate(((a_hi, b_hi), (a_hi, b_lo), (a_lo, b_hi))):
                    mm = eng.matmul(psum, a(k), b(k), start=(first and k == 0 and j == 0),
                                    stop=(last and k == n - 1 and j == 2))
            return mm

        def v_heads(n, q, g):
            v = v_all[g * T:g * T + T, bass.ds(n + 1 - g, 1), :].rearrange("p o (m a d) -> p (o m) a d", m=KC, a=4)
            return v[:, :, 2 * q + g, :]

        def plain(eng):
            eng.wait_ge(wload[0], 16)

        @block.sync
        def _(sp):
            sp.sem_inc(x1_store, 16 * TT)
            sp.sem_inc(h_store, 16 * TT)
            sp.dma_start(c_raw[:, :, :], ctx_t).then_inc(crload, 16)
            for w in range(2):
                sp.dma_start(raw[:, w, :], w_attn[w]).then_inc(wload[w], 16)
            sp.dma_start(xs[:, :, :], x_b[0]).then_inc(xload, 16)
            for w in range(2, 4):
                sp.dma_start(raw[:, w, :], w_attn[w]).then_inc(wload[w], 16)
            sp.wait_ge(w_lo_done, 4)

            def stores(n):
                for t in range(TT):
                    sp.wait_ge(x1_done, n * TT + t + 1)
                    sp.dma_start(out_rows[n * TT + t], xr[:, t, :]).then_inc(x1_store, 16)
                    sp.wait_ge(h_done, n * TT + t + 1)
                    sp.dma_start(h_rows[n * TT + t], dh[:, t, :]).then_inc(h_store, 16)

            def batch(b, back, front):
                if front:
                    sp.wait_ge(hs_done, b * TT + TT)
                    sp.dma_start(xs[:, :, :], x_b[b + 1]).then_inc(xload, 16)
                if back:
                    stores(b - 1)
                sp.wait_ge(x1_store, (b + 1) * 16 * TT)
                sp.dma_start(xr[:, :, :], x_b[b]).then_inc(rload, 16)

            batch(0, False, True)
            with sp.Fori(1, NB - 1) as b:
                batch(b, True, True)
            batch(NB - 1, True, False)
            stores(NB - 1)
            sp.wait_ge(x1_store, 16 * (NT + TT))
            sp.wait_ge(h_store, 16 * (NT + TT))
            sp.wait_ge(lg_done, TT + NT)
            for p in range(GU + DH):
                sp.dma_start(raw[:, p, :], w_exp[0, p]).then_inc(raw_in[p], 16)
            with sp.Fori(1, E) as e:
                for p in range(GU):
                    sp.wait_ge(gu_split, (e - 1) * GU + p + 1)
                    sp.dma_start(raw[:, p, :], w_exp[e, p]).then_inc(raw_in[p], 16)
                for p in range(DH):
                    sp.wait_ge(dn_split, (e - 1) * DH + p + 1)
                    sp.dma_start(raw[:, GU + p, :], w_exp[e, GU + p]).then_inc(raw_in[GU + p], 16)

        @block.gpsimd
        def _(pool):
            pool.memset(ident[:, :], 0.0).then_inc(setup, 1)
            pool.wait_ge(setup, 1)
            pool.affine_select(out=ident[:, :], in_=ident[:, :], compare_op=ALU.not_equal, fill=1.0,
                               base=0, pattern=[[-1, P]], channel_multiplier=1).then_inc(setup, 1)
            pool.memset(mhalf[:, :], -0.5).then_inc(setup, 1)
            for tile in (kbd_hi, kbd_lo, vbd_hi, vbd_lo, hsel):
                pool.memset(f32(tile[:]), 0.0).then_inc(setup, 1)
            pool.memset(rden[:, :], 1.0).then_inc(setup, 1)
            pool.wait_ge(setup, 9)
            for g in range(2):
                pool.memset(f32(hsel[g * T:g * T + T, NH - 2 + g:NH - 1 + g]), 1.0).then_inc(setup, 1)
            pool.affine_select(out=bsel[:, :, :, :], in_=rden[:, :].rearrange("p (m a d) -> p m a d", m=KC, a=4),
                               compare_op=ALU.is_equal,
                               fill=0.0, base=0, pattern=[[-4, KC], [-1, 4], [0, HD]],
                               channel_multiplier=1).then_inc(setup, 1)
            pool.dma_start(out_rows[NT], f32(kbd_hi[:, :, :]).rearrange("p k n -> p (k n)")).then_inc(pad_store, 16)
            pool.dma_start(h_rows[NT], f32(kbd_hi[:, :, :]).rearrange("p k n -> p (k n)")).then_inc(pad_store, 16)

            def ln_inverse(n):
                pool.wait_ge(ln_var, n + 1)
                pool.tensor_tensor(rs_a[:, :], ve_a[:, :], mhalf[:, :], ALU.pow).then_inc(ln_rstd, 1)
                pool.wait_ge(ln_rstd, n + 1)
                pool.tensor_tensor(nm_a[:, :], mn_a[:, :], rs_a[:, :], ALU.mult).then_inc(ln_bias, 1)

            def o_low(n, m):
                pool.wait_ge(o_h, n * KC + m + 1)
                pool.tensor_tensor(o_lo[:, m, :], o_n[:, m % 2, :], f32(o_hi[:, m, :]), ALU.subtract).then_inc(o_l, 1)

            def add_beta(n, t):
                pool.wait_ge(rload, (n + 1) * 16)
                pool.tensor_tensor(xr[:, t, :], xr[:, t, :], rows[:, 3, :], ALU.add).then_inc(xb_done, 1)

            def inverse_delta(n, t):
                pool.wait_ge(dvar, n * TT + t + 1)
                pool.tensor_tensor(rs[:, t:t + 1], ve[:, t:t + 1], mhalf[:, 0:1], ALU.pow).then_inc(drstd, 1)

            def inverse_h(n, t):
                pool.wait_ge(hvar, n * TT + t + 1)
                pool.tensor_tensor(rsh[:, t:t + 1], veh[:, t:t + 1], mhalf[:, 0:1], ALU.pow).then_inc(hrstd, 1)

            def batch(b, back, front):
                for s in range(PAIRS + 1):
                    if s < PAIRS:
                        pool.wait_ge(e_h, b * PAIRS + s + 1)
                        pool.tensor_tensor(ex_lo[:, s % 2, :], ex[:, s % 2, :], f32(ex_hi[:, s % 2, :]),
                                           ALU.subtract).then_inc(e_l, 1)
                    if s == 0 and back:
                        for m in range(KC):
                            o_low(b - 1, m)
                    if 2 <= s < 6 and back:
                        inverse_delta(b - 1, s - 2)
                    if 3 <= s < 7 and back:
                        inverse_h(b - 1, s - 3)
                    if s == 2 and front:
                        ln_inverse(b + 1)
                    if s in (1, 2) and back:
                        add_beta(b - 1, 2 * s - 2)
                        add_beta(b - 1, 2 * s - 1)

            pool.wait_ge(setup, 12)
            ln_inverse(0)
            pool.wait_ge(dset, 5)
            batch(0, False, True)
            with pool.Fori(1, NB - 1) as b:
                batch(b, True, True)
            batch(NB - 1, True, False)
            for m in range(KC):
                o_low(NB - 1, m)
            for t in range(TT):
                add_beta(NB - 1, t)
            for t in range(TT + 1):
                if t < TT:
                    inverse_delta(NB - 1, t)
                if t >= 1:
                    inverse_h(NB - 1, t - 1)

            pool.wait_ge(lg_done, TT + NT)
            pool.wait_ge(h_store, 16 * (NT + TT))

            def pattern(ap, pat, base_, cm):
                pool.iota(ap, pattern=pat, base=base_, channel_multiplier=cm,
                          allow_small_or_imprecise_dtypes=True).then_inc(rt_pool, 1)

            pattern(iota_e[:, :, :], [[0, NT], [1, E]], -E, 0)
            pool.memset(upper[:, :], 1.0).then_inc(rt_pool, 1)
            pool.memset(ones[:, :], 1.0).then_inc(rt_pool, 1)
            pool.memset(tri[:, :, :], 1.0).then_inc(rt_pool, 1)
            pool.wait_ge(rt_pool, 4)
            pool.affine_select(out=upper[:, :], in_=upper[:, :], compare_op=ALU.is_gt, fill=0.0,
                               base=0, pattern=[[1, P]], channel_multiplier=-1).then_inc(rt_pool, 1)
            pool.affine_select(out=tri[:, :, :], in_=tri[:, :, :], compare_op=ALU.is_ge, fill=0.0,
                               base=0, pattern=[[1, E], [-1, E]], channel_multiplier=0).then_inc(rt_pool, 1)
            pattern(iota_n[:, :, :], [[0, E], [P, 16]], 0, 0)
            pattern(iota40[:, :], [[1, SLOTT]], 0, 0)
            pattern(iota128[:, :], [[1, P]], 0, 0)
            pattern(tok1[:, :], [[P, NT]], 1, 1)
            pattern(pidx[:, :], [[0, 1]], TOK + 1, 1)

            pool.wait_ge(tables, 1)
            pool.wait_ge(h_store, 16 * (NT + TT))
            pool.wait_ge(pad_store, 32)
            used = pool.value_load(n_tiles[0:1, 0:1], min_val=1, max_val=MAXT)

            def gather():
                pool.indirect_dma_start(out=xg[:, :], out_offset=None, in_=h_dram[:, :],
                                        in_offset=bass.IndirectOffsetOnAxis(ap=g_idx[:, 0:1], axis=0)
                                        ).then_inc(gath, 16)

            pool.tensor_copy(g_idx[:, :], slot_idx[:, 0:1]).then_inc(idx_0, 1)
            pool.wait_ge(idx_0, 1)
            gather()
            with pool.Fori(0, used) as g:
                pool.wait_ge(gath, g * 16 + 16)
                plain(pool)
                pool.wait_ge(gt_tr, g + 1)
                pool.tensor_copy(g_idx[:, :], slot_idx[:, bass.ds(g + 1, 1)]).then_inc(idx_g, 1)
                plain(pool)
                pool.wait_ge(idx_g, g + 1)
                gather()
                plain(pool)
                pool.wait_ge(y_ready, g + 2)
                pool.tensor_copy(s_idx[:, :], slot_idx[:, bass.ds(g, 1)]).then_inc(idx_s, 1)
                plain(pool)
                pool.wait_ge(idx_s, g + 1)
                pool.indirect_dma_start(out=out[:, :],
                                        out_offset=bass.IndirectOffsetOnAxis(ap=s_idx[:, 0:1], axis=0),
                                        in_=y_sb[:, :], in_offset=None,
                                        compute_op=ALU.add).then_inc(scat, 16)
                pool.wait_ge(scat, g * 16 + 16)
                pool.sem_inc(y_free, 1)
            pool.wait_ge(gath, used * 16 + 16)
            pool.wait_ge(x1_store, 16 * (NT + TT))

        @block.vector
        def _(dve):
            dve.sem_inc(hd_l, 2)
            dve.sem_inc(lg_done, TT)
            dve.wait_ge(crload, 16)
            dve.wait_ge(c_h, 1)
            dve.tensor_tensor(c_lo[:, :, :], c_raw[:, :, :], f32(c_hi[:, :, :]), ALU.subtract).then_inc(c_l, 1)

            def split_weight(w):
                hi, lo = (a[:, w % 2, :, :].rearrange("p k n -> p (k n)")
                          for a in ((wkv_hi, wkv_lo) if w < 2 else (w_hi, w_lo)))
                dve.wait_ge(w_hi_done, w + 1)
                dve.tensor_tensor(lo, raw[:, w, :], f32(hi), ALU.subtract).then_inc(w_lo_done, 1)

            def ln_statistics(n, tiles=range(TT)):
                for t in tiles:
                    if t == 0:
                        dve.wait_ge(xload, (n + 1) * 16)
                    bn = dve.bn_stats(st_a[:, t, :], xs[:, t, :])
                if TT - 1 not in tiles:
                    return
                bn.then_inc(ln_stats, 1)
                plain(dve)
                dve.wait_ge(ln_stats, n + 1)
                for t in range(TT):
                    bn = dve.bn_aggr(mv_a[:, t, :], st_a[:, t, :])
                bn.then_inc(ln_mean, 1)
                dve.wait_ge(ln_mean, n + 1)
                dve.tensor_scalar(mn_a[:, :], mv_a[:, :, 0], -1.0, None, ALU.mult)
                dve.tensor_scalar(ve_a[:, :], mv_a[:, :, 1], EPS, None, ALU.add).then_inc(ln_var, 1)

            def x_low(n):
                for k in range(KC):
                    dve.wait_ge(xt_h, n * KC + k + 1)
                    dve.tensor_tensor(xt_lo[:, k, :], bank[k % 2][:, :], f32(xt_hi[:, k, :]),
                                      ALU.subtract).then_inc(xt_l, 1)

            def q_low(n, m):
                dve.wait_ge(q_h, n * KC + m + 1)
                dve.scalar_tensor_tensor(out=q_lo[:, m, :], in0=bank[2 + m % 2][:, :], scalar=bcol[:, 0, m:m + 1],
                                         in1=f32(q_hi[:, m, :]), op0=ALU.add, op1=ALU.subtract).then_inc(q_l, 1)

            def k_low(n):
                for g in range(4):
                    r = slice(g * HD, g * HD + HD)
                    c = slice((g % 2) * T, (g % 2) * T + T)
                    dve.wait_ge(k_h, n * 4 + g + 1)
                    dve.tensor_tensor(kbd_lo[r, :, c], k_all[r, :, bass.ds(n * T, T)], f32(kbd_hi[r, :, c]),
                                      ALU.subtract).then_inc(k_l, 1)

            def v_low(n):
                for i in range(4):
                    q, g = i // 2, i % 2
                    r = slice(g * T, g * T + T)
                    dve.wait_ge(v_h, n * 4 + i + 1)
                    dve.tensor_tensor(vbd_lo[r, :, q, 2 * q + g, :], v_heads(n, q, g),
                                      f32(vbd_hi[r, :, q, 2 * q + g, :]), ALU.subtract).then_inc(v_l, 1)

            def invert_sums(n):
                dve.wait_ge(den_c, n + 1)
                dve.reciprocal(rden[:, :], den[:, :]).then_inc(den_r, 1)
                dve.wait_ge(den_r, n + 1)
                dve.tensor_scalar(r_hi[:, :], rden[:, :], 1.0, None, ALU.mult).then_inc(r_h, 1)
                dve.wait_ge(r_h, n + 1)
                dve.tensor_tensor(r_lo[:, :], rden[:, :], f32(r_hi[:, :]), ALU.subtract).then_inc(r_l, 1)

            def normalise(n, m):
                dve.wait_ge(r_mm, n * KC + m + 1)
                dve.wait_ge(o_ev, n * KC + m + 1)
                if m >= 2:
                    dve.wait_ge(o_l, n * KC + m - 1)
                dve.tensor_tensor(o_n[:, m % 2, :], bank[3 - m % 2][:, :], o_un[:, m, :], ALU.mult).then_inc(o_nd, 1)

            def update(n, t):
                dve.wait_ge(h_store, (n + 1) * 16 * TT)
                dve.wait_ge(d_mm, n * TT + t + 1)
                dve.scalar_tensor_tensor(out=dh[:, t, :], in0=bank[2 + t % 2][:, :], scalar=tg[:, 2:3],
                                         in1=rows[:, 1, :], op0=ALU.mult, op1=ALU.add).then_inc(d_ready, 1)
                dve.wait_ge(d_ready, n * TT + t + 1)
                dve.bn_stats(st6[:, t, :], dh[:, t, :]).then_inc(dstats, 1)
                plain(dve)
                dve.wait_ge(dstats, n * TT + t + 1)
                dve.bn_aggr(mv[:, t, :], st6[:, t, :]).then_inc(dmean, 1)
                dve.wait_ge(dmean, n * TT + t + 1)
                dve.tensor_scalar(ve[:, t:t + 1], mv[:, t, 1:2], EPS, None, ALU.add).then_inc(dvar, 1)
                dve.scalar_tensor_tensor(out=dh[:, t, :], in0=dh[:, t, :], scalar=mv[:, t, 0:1],
                                         in1=rows[:, 2, :], op0=ALU.subtract, op1=ALU.mult).then_inc(dgam, 1)

            def residual(n, t):
                dve.wait_ge(dgam, n * TT + t + 1)
                dve.wait_ge(drstd, n * TT + t + 1)
                dve.wait_ge(xb_done, n * TT + t + 1)
                dve.scalar_tensor_tensor(out=xr[:, t, :], in0=dh[:, t, :], scalar=rs[:, t:t + 1],
                                         in1=xr[:, t, :], op0=ALU.mult, op1=ALU.add).then_inc(x1_done, 1)
                dve.wait_ge(x1_done, n * TT + t + 1)
                dve.bn_stats(st6h[:, t, :], xr[:, t, :]).then_inc(hstats, 1)
                plain(dve)
                dve.wait_ge(hstats, n * TT + t + 1)
                dve.bn_aggr(mvh[:, t, :], st6h[:, t, :]).then_inc(hmean, 1)
                dve.wait_ge(hmean, n * TT + t + 1)
                dve.tensor_scalar(veh[:, t:t + 1], mvh[:, t, 1:2], EPS, None, ALU.add).then_inc(hvar, 1)

            def normalised(n, t):
                dve.wait_ge(hrstd, n * TT + t + 1)
                dve.tensor_scalar(dh[:, t, :], xr[:, t, :], mvh[:, t, 0:1], rsh[:, t:t + 1],
                                  ALU.subtract, ALU.mult).then_inc(h_done, 1)

            def keep_logits(n, t):
                dve.wait_ge(lg_mm, n * TT + t + 1)
                dve.tensor_copy(logits[:, bass.ds(n * TT + t, 1), :],
                                bank[t % 2][:, 0:E].unsqueeze(1)).then_inc(lg_done, 1)

            def batch(b, back, front):
                for s in range(PAIRS + 1):
                    if s < PAIRS:
                        dve.wait_ge(s_mm, b * PAIRS + s + 1)
                        if s >= 2 or back:
                            dve.wait_ge(s_exp, b * PAIRS + s - 1)
                        dve.tensor_scalar(sc[:, s % 2, :], bank[4 + s % 2][:, :], lim[:, bass.ds(b, 1)], -CLIP,
                                          ALU.min, ALU.max).then_inc(s_clip, 1)
                    if s == 0:
                        q_low(b, 2)
                        if back:
                            for m in range(KC):
                                normalise(b - 1, m)
                    if s == 1:
                        q_low(b, 3)
                    if s in (1, 2) and front:
                        ln_statistics(b + 1, range(2 * s - 2, 2 * s))
                    if 4 <= s < 8 and back:
                        normalised(b - 1, s - 4)
                    if 3 <= s < 7 and back:
                        residual(b - 1, s - 3)
                    if 2 <= s < 6 and back:
                        update(b - 1, s - 2)
                    if s == 4 and front:
                        x_low(b + 1)
                    if s in (6, 7) and front:
                        q_low(b + 1, s - 6)
                    if s >= 6 and back:
                        keep_logits(b - 1, s - 6)
                if front:
                    k_low(b + 1)
                    v_low(b + 1)
                invert_sums(b)
                if back:
                    keep_logits(b - 1, 3)

            split_weight(0)
            split_weight(1)
            ln_statistics(0)
            dve.wait_ge(cload, 80)
            dve.tensor_scalar(tg[:, 2:3], gsc[:, 2:3], 0.0, 0.3, ALU.max, ALU.min).then_inc(dset, 1)
            dve.tensor_scalar(lim[:, :], mask_sb[:, :], 0.5, 2.0 * CLIP, ALU.is_gt, ALU.mult).then_inc(dset, 1)
            dve.wait_ge(dset, 2)
            dve.wait_ge(gates_ready, 1)
            dve.tensor_scalar(lim[:, :], lim[:, :], -CLIP, None, ALU.add).then_inc(dset, 1)
            dve.tensor_scalar(rows[:, 1, :], rows[:, 1, :], tg[:, 2:3], None, ALU.mult).then_inc(dset, 1)
            dve.tensor_scalar(rows[:, 2:4, :], rows[:, 2:4, :], tg[:, 0:1], None, ALU.mult).then_inc(dset, 1)
            dve.wait_ge(dset, 5)
            dve.wait_ge(kv_mm, 1)
            for h in range(2):
                dve.tensor_tensor(k_all[:, 2 * h:2 * h + 2, :], bank[6 + h][:, :].rearrange("p (k t) -> p k t", k=2),
                                  bcol[:, 1, 2 * h:2 * h + 2].unsqueeze(2).to_broadcast([P, 2, NB * T]),
                                  ALU.add).then_inc(kv_sb, 1)
            split_weight(2)
            dve.wait_ge(kv_mm, 2)
            for place in range(NB + 1):
                dve.tensor_tensor(v_all[:, place, :], bank[2 + (place - 1) % NB][:, :], rows[:, 0, :],
                                  ALU.add).then_inc(kv_sb, 1)
            x_low(0)
            dve.wait_ge(kv_sb, 3 + NB)
            k_low(0)
            v_low(0)
            q_low(0, 0)
            q_low(0, 1)
            split_weight(3)
            batch(0, False, True)
            with dve.Fori(1, NB - 1) as b:
                batch(b, True, True)
            batch(NB - 1, True, False)
            for m in range(KC):
                normalise(NB - 1, m)
            for t in range(TT + 2):
                if t < TT:
                    update(NB - 1, t)
                if 1 <= t <= TT:
                    residual(NB - 1, t - 1)
                if t >= 2:
                    normalised(NB - 1, t - 2)
            for t in range(TT):
                keep_logits(NB - 1, t)

            step = [0]

            def link(ins):
                step[0] += 1
                ins.then_inc(rt, 1)
                dve.wait_ge(rt, step[0])

            def bc(ap):
                return ap.to_broadcast(NE3)

            dve.wait_ge(rt_pool, 11)
            dve.wait_ge(h_store, 16 * (NT + TT))
            dve.wait_ge(lg_done, TT + NT)
            link(dve.tensor_reduce(m1[:, :, 0], logits[:, :, :], AX.X, ALU.max))

            def choose(oh, lg, m):
                link(dve.tensor_tensor(eq[:, :, :], lg, bc(m[:, :, :]), ALU.is_equal))
                link(dve.scalar_tensor_tensor(out=tmp3[:, :, :], in0=eq[:, :, :], scalar=-float(E),
                                              in1=iota_e[:, :, :], op0=ALU.mult, op1=ALU.add))
                link(dve.tensor_reduce(i1[:, :, 0], tmp3[:, :, :], AX.X, ALU.min))
                link(dve.tensor_scalar(tmp3[:, :, :], iota_e[:, :, :], -float(E), None, ALU.add))
                link(dve.tensor_tensor(oh, tmp3[:, :, :], bc(i1[:, :, :]), ALU.is_equal))

            choose(oh1[:, :, :], logits[:, :, :], m1)
            link(dve.scalar_tensor_tensor(out=lg2[:, :, :], in0=oh1[:, :, :], scalar=NEG_BIG,
                                          in1=logits[:, :, :], op0=ALU.mult, op1=ALU.add))
            link(dve.tensor_reduce(m2[:, :, 0], lg2[:, :, :], AX.X, ALU.max))
            choose(oh2[:, :, :], lg2[:, :, :], m2)
            link(dve.tensor_tensor(sel[:, :, :], oh1[:, :, :], oh2[:, :, :], ALU.add))
            sel_step[0] = step[0]
            link(dve.tensor_tensor(wk[:, 1, :], m2[:, :, 0], m1[:, :, 0], ALU.subtract))
            diff_step[0] = step[0]
            dve.wait_ge(rt_act, 1)
            link(dve.tensor_scalar(wden[:, :], wk[:, 1, :], 1.0, None, ALU.add))
            link(dve.reciprocal(wk[:, 0, :], wden[:, :]))
            link(dve.tensor_scalar(wk[:, 0, :], wk[:, 0, :], tg[:, 1:2], None, ALU.mult))
            link(dve.tensor_tensor(wk[:, 1, :], wk[:, 1, :], wk[:, 0, :], ALU.mult))
            dve.wait_ge(rt_pe, 1)
            link(dve.tensor_copy(nexp[:, :], bank[1][:, 0:E]))
            link(dve.tensor_tensor(cmp_n[:, :, :], nexp[:, :].unsqueeze(2).to_broadcast([P, E, 16]),
                                   iota_n[:, :, :], ALU.is_gt))
            link(dve.tensor_reduce(tl[:, :, 0], cmp_n[:, :, :], AX.X, ALU.add))
            link(dve.tensor_scalar(tl[:, :, 0], tl[:, :, 0], 1.0, None, ALU.max))
            link(dve.tensor_tensor(trm[:, :, :], tri[:, :, :],
                                   tl[:, :, 0].unsqueeze(1).to_broadcast([P, E, E]), ALU.mult))
            link(dve.tensor_reduce(tend[:, :, 0], trm[:, :, :], AX.X, ALU.add))
            link(dve.tensor_tensor(base[:, :], tend[:, :, 0], tl[:, :, 0], ALU.subtract))
            link(dve.tensor_scalar(base[:, :], base[:, :], float(P), None, ALU.mult))
            link(dve.tensor_tensor(posn[:, :, :], bank[0][:, 0:NT * E].rearrange("p (t e) -> p t e", e=E),
                                   base[:, :].unsqueeze(1).to_broadcast(NE3), ALU.add))
            for c, oh in enumerate((oh1, oh2)):
                link(dve.tensor_tensor(tmp3[:, :, :], posn[:, :, :], oh[:, :, :], ALU.mult))
                link(dve.tensor_reduce(slot[:, c, :], tmp3[:, :, :], AX.X, ALU.add))
            link(dve.tensor_copy(slot_i[:, :, :], slot[:, :, :]))
            link(dve.tensor_scalar(sa_i[:, :, :], slot_i[:, :, :], 7, None, ALU.logical_shift_right))
            link(dve.tensor_scalar(sb_i[:, :, :], slot_i[:, :, :], P - 1, None, ALU.bitwise_and))
            link(dve.tensor_copy(sa[:, :, :], sa_i[:, :, :]))
            link(dve.tensor_copy(sbp[:, :, :], sb_i[:, :, :]))
            for c in range(TOPK):
                link(dve.tensor_tensor(ohe[:, :, :], iota40[:, :].unsqueeze(1).to_broadcast([P, NT, SLOTT]),
                                       sa[:, c, :].unsqueeze(2).to_broadcast([P, NT, SLOTT]), ALU.is_equal))
                link(dve.tensor_tensor(oha[:, c, :, 0, :], ohe[:, :, :],
                                       tok1[:, :].unsqueeze(2).to_broadcast([P, NT, SLOTT]), ALU.mult))
                link(dve.tensor_tensor(oha[:, c, :, 1, :], ohe[:, :, :],
                                       wk[:, c, :].unsqueeze(2).to_broadcast([P, NT, SLOTT]), ALU.mult))
            for c in range(TOPK):
                if c:
                    dve.wait_ge(rt_pe, 1 + c)
                link(dve.tensor_tensor(ohb[:, :, :], iota128[:, :].unsqueeze(1).to_broadcast([P, NT, P]),
                                       sbp[:, c, :].unsqueeze(2).to_broadcast([P, NT, P]), ALU.is_equal))
                ohb_step[c] = step[0]
            link(dve.tensor_tensor(ind[:, :, :], iota40[:, :].unsqueeze(1).to_broadcast([P, E, SLOTT]),
                                   tend[:, :, :].to_broadcast([P, E, SLOTT]), ALU.is_ge))
            link(dve.tensor_reduce(tabf[:, :, 0], ind[:, 0:E - 1, :].rearrange("p e n -> p n e"), AX.X, ALU.add))
            link(dve.memset(tabf[:, :, 1:4], 0.0))
            link(dve.tensor_tensor(tabf[:, 0:SLOTT - 1, 1], tabf[:, 1:SLOTT, 0], tabf[:, 0:SLOTT - 1, 0], ALU.subtract))
            link(dve.tensor_copy(tabf[:, 1:SLOTT, 2], tabf[:, 0:SLOTT - 1, 1]))
            link(dve.memset(tabf[:, 0:1, 2:3], 1.0))
            link(dve.tensor_copy(tile_tab[:, :, :], tabf[:, :, :]))
            link(dve.tensor_copy(n_tiles[:, 0:1], tend[:, E - 1, :]))
            dve.wait_ge(rt_pe, 1 + TOPK)
            link(dve.tensor_copy(slot_w[:, :], bank[2][:, SLOTT:2 * SLOTT]))
            link(dve.tensor_copy(tv[:, :], bank[2][:, 0:SLOTT]))
            link(dve.tensor_scalar(tz[:, :], tv[:, :], 0.0, pidx[:, 0:1], ALU.is_equal, ALU.mult))
            link(dve.scalar_tensor_tensor(out=tz[:, :], in0=tv[:, :], scalar=-1.0, in1=tz[:, :],
                                          op0=ALU.add, op1=ALU.add))
            link(dve.tensor_copy(slot_idx[:, :], tz[:, :]))
            dve.sem_inc(tables, 1)

            def split_lo(dst, hi, p, done):
                dve.tensor_tensor(dst.rearrange("p k n -> p (k n)"), raw[:, p, :],
                                  f32(hi.rearrange("p k n -> p (k n)")), ALU.subtract).then_inc(done, 1)

            for p in range(GU):
                dve.wait_ge(gu_hi, p + 1)
                split_lo(g_lo[:, p, :, :], g_hi[:, p, :, :], p, gu_split)
            dve.wait_ge(gt_h, 1)
            dve.tensor_tensor(gt_lo[:, :, :].rearrange("p k n -> p (k n)"), bank[6][:, :],
                              f32(gt_hi[:, :, :].rearrange("p k n -> p (k n)")), ALU.subtract).then_inc(gt_l, 1)
            used = dve.value_load(n_tiles[0:1, 0:1], min_val=1, max_val=MAXT)
            with dve.Fori(0, used) as g:
                expert = dve.value_load(tile_tab[0:1, bass.ds(g, 1), 0:1].rearrange("p a b -> p (a b)"), min_val=0, max_val=E - 1)
                last = dve.value_load(tile_tab[0:1, bass.ds(g, 1), 1:2].rearrange("p a b -> p (a b)"), min_val=0, max_val=1)
                first = dve.value_load(tile_tab[0:1, bass.ds(g, 1), 2:3].rearrange("p a b -> p (a b)"), min_val=0, max_val=1)

                def hidden_lo(p):
                    dve.wait_ge(hd_h, g * GU + p + 1)
                    dve.tensor_tensor(hd_lo[:, 2 * p:2 * p + 2, :].rearrange("p k n -> p (k n)"),
                                      bank[4 + p % 2][:, 0:256],
                                      f32(hd_hi[:, 2 * p:2 * p + 2, :].rearrange("p k n -> p (k n)")),
                                      ALU.subtract).then_inc(hd_l, 1)

                for p in range(GU):
                    dve.wait_ge(silu_done, g * GU + p + 1)
                    dve.tensor_tensor(hid[:, p, :], silu[:, p, :], bank[p][:, 256:512], ALU.mult).then_inc(hid_done, 1)
                    if p >= 1:
                        hidden_lo(p - 1)
                    with dve.If(last):
                        dve.wait_ge(gu_hi, expert * GU + GU + p + 1)
                        split_lo(g_lo[:, p, :, :], g_hi[:, p, :, :], p, gu_split)
                    if p < DH:
                        with dve.If(first):
                            dve.wait_ge(dn_h, expert * DH + p + 1)
                            split_lo(dn_lo[:, p, :, :], dn_hi[:, p, :, :], GU + p, dn_split)
                hidden_lo(GU - 1)
                dve.wait_ge(gt_h, g + 2)
                dve.tensor_tensor(gt_lo[:, :, :].rearrange("p k n -> p (k n)"), bank[6][:, :],
                                  f32(gt_hi[:, :, :].rearrange("p k n -> p (k n)")), ALU.subtract).then_inc(gt_l, 1)

        @block.scalar
        def _(act):
            act.sem_inc(y_free, 1)
            act.dma_start(mask_sb[:, :], mask).then_inc(cload, 16)
            act.dma_start(bcol[:, :, :], b_cols).then_inc(cload, 16)
            act.dma_start(gsc[:, :], gates.partition_broadcast(P)).then_inc(cload, 16)
            act.dma_start(gate_w[:, :, :], gate_t).then_inc(cload, 16)
            act.dma_start(rows[:, :, :], b_rows.partition_broadcast(P)).then_inc(cload, 16)
            act.wait_ge(crload, 16)
            act.activation(c_hi[:, :, :], c_raw[:, :, :], ACT.Copy).then_inc(c_h, 1)

            def split_weight(w):
                act.wait_ge(wload[w], 16)
                hi = (wkv_hi if w < 2 else w_hi)[:, w % 2, :, :].rearrange("p k n -> p (k n)")
                act.activation(hi, raw[:, w, :], ACT.Copy).then_inc(w_hi_done, 1)

            def normalise_x(n):
                act.wait_ge(ln_bias, n + 1)
                for t in range(TT):
                    act.activation(hs[:, t, :], xs[:, t, :], ACT.Identity, scale=rs_a[:, t:t + 1],
                                   bias=nm_a[:, t:t + 1]).then_inc(hs_done, 1)

            def x_high(n):
                for k in range(KC):
                    act.wait_ge(xt_tr, n * KC + k + 1)
                    act.activation(xt_hi[:, k, :], bank[k % 2][:, :], ACT.Copy).then_inc(xt_h, 1)

            def q_high(n, m):
                act.wait_ge(q_mm, n * KC + m + 1)
                act.activation(q_hi[:, m, :], bank[2 + m % 2][:, :], ACT.Identity,
                               bias=bcol[:, 0, m:m + 1]).then_inc(q_h, 1)

            def k_high(n):
                for g in range(4):
                    r = slice(g * HD, g * HD + HD)
                    act.activation(kbd_hi[r, :, (g % 2) * T:(g % 2) * T + T], k_all[r, :, bass.ds(n * T, T)],
                                   ACT.Copy).then_inc(k_h, 1)

            def v_high(n):
                for i in range(4):
                    q, g = i // 2, i % 2
                    act.activation(vbd_hi[g * T:g * T + T, :, q, 2 * q + g, :], v_heads(n, q, g),
                                   ACT.Copy).then_inc(v_h, 1)

            def o_high(n, m):
                act.wait_ge(o_nd, n * KC + m + 1)
                act.activation(o_hi[:, m, :], o_n[:, m % 2, :], ACT.Copy).then_inc(o_h, 1)

            def h_copy(n, t):
                act.wait_ge(h_tr, n * TT + t + 1)
                act.activation(ht[:, t % 2, :, :].rearrange("p k n -> p (k n)"), bank[t % 2][:, :],
                               ACT.Copy).then_inc(h_ev, 1)

            def batch(b, back, front):
                for s in range(PAIRS + 1):
                    if s < PAIRS:
                        act.wait_ge(s_clip, b * PAIRS + s + 1)
                        if s >= 2 or back:
                            act.wait_ge(e_l, b * PAIRS + s - 1)
                        act.activation(ex[:, s % 2, :], sc[:, s % 2, :], ACT.Exp, scale=INV_SCALE).then_inc(s_exp, 1)
                        act.wait_ge(s_exp, b * PAIRS + s + 1)
                        if s >= 2 or back:
                            act.wait_ge(pair_mm, b * PAIRS + s - 1)
                        act.activation(ex_hi[:, s % 2, :], ex[:, s % 2, :], ACT.Copy).then_inc(e_h, 1)
                    if s == 0:
                        q_high(b, 2)
                        if back:
                            for m in range(KC):
                                o_high(b - 1, m)
                    if s == 1:
                        q_high(b, 3)
                    if s == 3 and front:
                        normalise_x(b + 1)
                    if s == 4 and front:
                        x_high(b + 1)
                    if s in (6, 7) and front:
                        q_high(b + 1, s - 6)
                    if s == PAIRS and front:
                        act.wait_ge(s_mm, b * PAIRS + PAIRS)
                        k_high(b + 1)
                    if s >= 5 and back:
                        h_copy(b - 1, s - 5)
                    if s >= 2 and s % 2 == 0:
                        act.wait_ge(pair_mm, b * PAIRS + s)
                        if s == PAIRS:
                            act.activation(den[:, :], bank[7][0:NH, :], ACT.Copy, scale=1.0 + 1e-8).then_inc(den_c, 1)
                        act.activation(o_un[:, s // 2 - 1, :], bank[6][:, :], ACT.Copy).then_inc(o_ev, 1)
                    if s == PAIRS and front:
                        v_high(b + 1)

            split_weight(0)
            split_weight(1)
            act.wait_ge(cload, 80)
            act.activation(tg[:, 0:2], gsc[:, 0:2], ACT.Tanh).then_inc(gates_ready, 1)
            normalise_x(0)
            split_weight(2)
            x_high(0)
            act.wait_ge(setup, 12)
            act.wait_ge(pad_store, 32)
            act.wait_ge(kv_sb, 3 + NB)
            k_high(0)
            v_high(0)
            q_high(0, 0)
            q_high(0, 1)
            split_weight(3)
            batch(0, False, True)
            with act.Fori(1, NB - 1) as b:
                batch(b, True, True)
            batch(NB - 1, True, False)
            for m in range(KC):
                o_high(NB - 1, m)
            for t in range(TT):
                h_copy(NB - 1, t)
            act.wait_ge(rt, diff_step[0])
            act.activation(wk[:, 1, :], wk[:, 1, :], ACT.Exp).then_inc(rt_act, 1)

            act.wait_ge(tables, 1)

            def split_hi(dst, p, done):
                act.activation(dst.rearrange("p k n -> p (k n)"), raw[:, p, :], ACT.Copy).then_inc(done, 1)

            for p in range(GU):
                act.wait_ge(raw_in[p], 16)
                split_hi(g_hi[:, p, :, :], p, gu_hi)
            act.wait_ge(gt_tr, 1)
            act.activation(gt_hi[:, :, :].rearrange("p k n -> p (k n)"), bank[6][:, :], ACT.Copy).then_inc(gt_h, 1)
            used = act.value_load(n_tiles[0:1, 0:1], min_val=1, max_val=MAXT)
            with act.Fori(0, used) as g:
                expert = act.value_load(tile_tab[0:1, bass.ds(g, 1), 0:1].rearrange("p a b -> p (a b)"), min_val=0, max_val=E - 1)
                last = act.value_load(tile_tab[0:1, bass.ds(g, 1), 1:2].rearrange("p a b -> p (a b)"), min_val=0, max_val=1)
                first = act.value_load(tile_tab[0:1, bass.ds(g, 1), 2:3].rearrange("p a b -> p (a b)"), min_val=0, max_val=1)

                def hidden_hi(p):
                    act.wait_ge(hd_tr, g * GU + p + 1)
                    act.activation(hd_hi[:, 2 * p:2 * p + 2, :].rearrange("p k n -> p (k n)"),
                                   bank[4 + p % 2][:, 0:256], ACT.Copy).then_inc(hd_h, 1)

                for p in range(GU):
                    act.wait_ge(gu_mm, g * GU + p + 1)
                    act.activation(silu[:, p, :], bank[p][:, 0:256], ACT.Silu).then_inc(silu_done, 1)
                    if p >= 1:
                        hidden_hi(p - 1)
                    with act.If(last):
                        act.wait_ge(raw_in[p], expert * 16 + 32)
                        split_hi(g_hi[:, p, :, :], p, gu_hi)
                    if p < DH:
                        with act.If(first):
                            act.wait_ge(raw_in[GU + p], expert * 16 + 16)
                            split_hi(dn_hi[:, p, :, :], GU + p, dn_h)
                hidden_hi(GU - 1)
                act.wait_ge(gt_tr, g + 2)
                act.activation(gt_hi[:, :, :].rearrange("p k n -> p (k n)"), bank[6][:, :], ACT.Copy).then_inc(gt_h, 1)
                act.wait_ge(y_mm, g + 1)
                act.wait_ge(y_free, g + 1)
                act.activation(y_sb[:, :], bank[7][:, :], ACT.Copy, scale=slot_w[:, bass.ds(g, 1)]).then_inc(y_ready, 1)

        @block.tensor
        def _(pe):
            pe.sem_inc(y_ready, 1)
            pe.wait_ge(setup, 12)

            def x_transposes(n, b):
                pe.wait_ge(hs_done, n * TT + TT)
                if b is not None:
                    pe.wait_ge(lg_done, b * TT)
                for k in range(KC):
                    if k >= 2:
                        pe.wait_ge(xt_l, n * KC + k - 1)
                    for t in range(TT):
                        tr = pe.transpose(bank[k % 2][:, t * P:(t + 1) * P], hs[:, t, k * P:(k + 1) * P], ident[:, :])
                    tr.then_inc(xt_tr, 1)

            def q_product(n, m):
                if m == 0:
                    pe.wait_ge(xt_l, n * KC + KC)
                product3(pe, bank[2 + m % 2][:, :],
                         lambda k: w_hi[:, 0, k, m * P:(m + 1) * P], lambda k: w_lo[:, 0, k, m * P:(m + 1) * P],
                         lambda k: xt_hi[:, k, :], lambda k: xt_lo[:, k, :]).then_inc(q_mm, 1)

            def scores(b, s):
                m, r = s // 2, slice((s % 2) * 64, (s % 2) * 64 + 64)
                pe.wait_ge(q_l, b * KC + m + 1)
                if s == 0:
                    pe.wait_ge(k_l, b * 4 + 4)
                if s >= 2:
                    pe.wait_ge(s_clip, b * PAIRS + s - 1)
                product3(pe, bank[4 + s % 2][:, :], lambda k: kbd_hi[r, m, :], lambda k: kbd_lo[r, m, :],
                         lambda k: q_hi[r, m, :], lambda k: q_lo[r, m, :], n=1).then_inc(s_mm, 1)

            def pv(b, s, back):
                m, j = s // 2, s % 2
                pe.wait_ge(e_l, b * PAIRS + s + 1)
                if s == 0:
                    pe.wait_ge(v_l, b * 4 + 4)
                if j == 0 and (m >= 1 or back):
                    pe.wait_ge(o_ev, b * KC + m)
                if s == 0 and back:
                    pe.wait_ge(den_c, b)
                product3(pe, bank[6][:, :],
                         lambda k: vbd_hi[:, m, j, :, :].rearrange("p a d -> p (a d)"),
                         lambda k: vbd_lo[:, m, j, :, :].rearrange("p a d -> p (a d)"),
                         lambda k: ex_hi[:, j, :], lambda k: ex_lo[:, j, :], n=1, first=(j == 0), last=(j == 1))
                at = NH - 2 - 2 * s
                for a, e_ in enumerate((ex_hi, ex_lo)):
                    mm = pe.matmul(bank[7][:, :], hsel[:, at:at + P], e_[:, j, :],
                                   start=(s == 0 and a == 0), stop=(s == PAIRS - 1 and a == 1))
                mm.then_inc(pair_mm, 1)

            def spread(n, m):
                if m == 0:
                    pe.wait_ge(r_l, n + 1)
                if m >= 2:
                    pe.wait_ge(o_nd, n * KC + m - 1)
                for a, r_ in enumerate((r_hi, r_lo)):
                    mm = pe.matmul(bank[3 - m % 2][:, :], bsel[:, m, :, :].rearrange("p a d -> p (a d)"), r_[:, :],
                                   start=(a == 0), stop=(a == 1))
                mm.then_inc(r_mm, 1)

            def o_product(n, t):
                if t == 0:
                    pe.wait_ge(o_l, n * KC + KC)
                if t >= 2:
                    pe.wait_ge(d_ready, n * TT + t - 1)
                product3(pe, bank[2 + t % 2][:, :],
                         lambda k: o_hi[:, k, t * P:(t + 1) * P], lambda k: o_lo[:, k, t * P:(t + 1) * P],
                         lambda k: w_hi[:, 1, k, :], lambda k: w_lo[:, 1, k, :]).then_inc(d_mm, 1)

            def h_transposes(n, t):
                pe.wait_ge(h_done, n * TT + t + 1)
                if t >= 2:
                    pe.wait_ge(lg_done, n * TT + TT + t - 1)
                for k in range(KC):
                    tr = pe.transpose(bank[t % 2][:, k * P:(k + 1) * P], dh[:, t, k * P:(k + 1) * P], ident[:, :])
                tr.then_inc(h_tr, 1)

            def router(n, t):
                pe.wait_ge(h_ev, n * TT + t + 1)
                for k in range(KC):
                    mm = pe.matmul(bank[t % 2][:, 0:E], ht[:, t % 2, k, :], gate_w[:, k, :],
                                   start=(k == 0), stop=(k == KC - 1))
                mm.then_inc(lg_mm, 1)

            def batch(b, back, front):
                for s in range(PAIRS + 1):
                    if s < PAIRS:
                        scores(b, s)
                    if s == 0:
                        q_product(b, 2)
                        if back:
                            pe.wait_ge(q_l, b * KC + 2)
                            spread(b - 1, 0)
                            pe.wait_ge(q_l, b * KC + 3)
                            for m in range(1, KC):
                                spread(b - 1, m)
                    if s == 1:
                        if back:
                            pe.wait_ge(o_nd, b * KC - 1)
                        else:
                            pe.wait_ge(q_l, b * KC + 2)
                        q_product(b, 3)
                    if 2 <= s < 6 and back:
                        if s == 3:
                            pe.wait_ge(q_l, b * KC + 4)
                        o_product(b - 1, s - 2)
                    if s == 4 and front:
                        x_transposes(b + 1, b if back else None)
                    if s in (6, 7) and front:
                        if back:
                            pe.wait_ge(d_ready, b * TT + s - 7)
                        q_product(b + 1, s - 6)
                    if s >= 6 and back:
                        router(b - 1, s - 6)
                    if s in (5, 6) and back:
                        if front:
                            pe.wait_ge(xt_l, b * KC + KC + s - 2)
                        else:
                            pe.wait_ge(lg_done, b * TT)
                    if s >= 5 and back:
                        h_transposes(b - 1, s - 5)
                    if s >= 1:
                        pv(b, s - 1, back)
                if back:
                    router(b - 1, 3)

            pe.wait_ge(c_l, 1)
            pe.wait_ge(w_lo_done, 1)
            for m in range(KC):
                mm = product3(pe, bank[6 + m // 2][:, (m % 2) * NB * T:(m % 2 + 1) * NB * T],
                              lambda k: wkv_hi[:, 0, k, m * P:(m + 1) * P], lambda k: wkv_lo[:, 0, k, m * P:(m + 1) * P],
                              lambda k: c_hi[:, k, 0:NB * T], lambda k: c_lo[:, k, 0:NB * T])
            mm.then_inc(kv_mm, 1)
            pe.wait_ge(w_lo_done, 2)
            for n in range(NB):
                two = slice(n * T, n * T + 2 * T)
                mm = product3(pe, bank[2 + n][:, :], lambda k: c_hi[:, k, two], lambda k: c_lo[:, k, two],
                              lambda k: wkv_hi[:, 1, k, :], lambda k: wkv_lo[:, 1, k, :])
            mm.then_inc(kv_mm, 1)
            x_transposes(0, None)
            pe.wait_ge(w_lo_done, 3)
            pe.wait_ge(kv_sb, 3 + NB)
            q_product(0, 0)
            q_product(0, 1)
            batch(0, False, True)
            with pe.Fori(1, NB - 1) as b:
                batch(b, True, True)
            batch(NB - 1, True, False)
            for m in range(KC):
                spread(NB - 1, m)
            for t in range(TT):
                o_product(NB - 1, t)
            for t in range(TT):
                h_transposes(NB - 1, t)
                router(NB - 1, t)

            pe.wait_ge(rt_pool, 11)
            pe.wait_ge(rt, sel_step[0])
            selv = sel[:, :, :].rearrange("p t e -> p (t e)")
            pe.matmul(bank[0][:, 0:NT * E], upper[:, :], selv, start=True, stop=False, skip_group_check=True)
            for s in range(1, NT):
                pe.matmul(bank[0][:, s * E:NT * E], ones[:, :], selv[:, 0:(NT - s) * E],
                          start=False, stop=(s == NT - 1), skip_group_check=True)
            for t in range(NT):
                mm = pe.matmul(bank[1][:, 0:E], ones[:, :], selv[:, t * E:(t + 1) * E], start=(t == 0), stop=(t == NT - 1))
            mm.then_inc(rt_pe, 1)
            for c in range(TOPK):
                pe.wait_ge(rt, ohb_step[c])
                for t in range(NT):
                    mm = pe.matmul(bank[2][:, 0:2 * SLOTT], ohb[:, t, :],
                                   oha[:, c, t, :, :].rearrange("p a n -> p (a n)"),
                                   start=(c == 0 and t == 0), stop=(c == TOPK - 1 and t == NT - 1))
                mm.then_inc(rt_pe, 1)

            pe.wait_ge(tables, 1)

            def slot_rows(n):
                pe.wait_ge(gath, n * 16 + 16)
                for k in range(KC):
                    tr = pe.transpose(bank[6][:, k * P:(k + 1) * P], xg[:, k * P:(k + 1) * P], ident[:, :])
                tr.then_inc(gt_tr, 1)

            slot_rows(0)
            used = pe.value_load(n_tiles[0:1, 0:1], min_val=1, max_val=MAXT)
            with pe.Fori(0, used) as g:
                expert = pe.value_load(tile_tab[0:1, bass.ds(g, 1), 0:1].rearrange("p a b -> p (a b)"), min_val=0, max_val=E - 1)

                def hidden_t(p):
                    pe.wait_ge(hid_done, g * GU + p + 1)
                    pe.wait_ge(hd_l, g * GU + p + 1)
                    for c in range(2):
                        tr = pe.transpose(bank[4 + p % 2][:, c * P:(c + 1) * P], hid[:, p, c * P:(c + 1) * P], ident[:, :])
                    tr.then_inc(hd_tr, 1)

                def down(c):
                    if c % 2 == 0:
                        pe.wait_ge(hd_l, g * GU + c // 2 + 3)
                    if c % 4 == 0:
                        pe.wait_ge(dn_split, expert * DH + c // 4 + 1)
                    if c == 0:
                        pe.wait_ge(y_ready, g + 1)
                    mm = product3(pe, bank[7][:, :], lambda k: hd_hi[:, c, :], lambda k: hd_lo[:, c, :],
                                  lambda k: dn_hi[:, c // 4, c % 4, :], lambda k: dn_lo[:, c // 4, c % 4, :],
                                  n=1, first=(c == 0), last=(c == IC - 1))
                    if c == IC - 1:
                        mm.then_inc(y_mm, 1)

                pe.wait_ge(gt_l, g + 1)
                for p in range(GU):
                    pe.wait_ge(gu_split, expert * GU + p + 1)
                    product3(pe, bank[p][:, :], lambda k: gt_hi[:, k, :], lambda k: gt_lo[:, k, :],
                             lambda k: g_hi[:, p, k, :], lambda k: g_lo[:, p, k, :]).then_inc(gu_mm, 1)
                    if p >= 1:
                        hidden_t(p - 1)
                down(0)
                down(1)
                hidden_t(GU - 1)
                down(2)
                down(3)
                slot_rows(g + 1)
                for c in range(4, IC):
                    down(c)


sel_step, diff_step, ohb_step = [0], [0], [0, 0]


def kernel(x, ctx_2048, mask_BxS2_ik0, g_xattn, g_ffn, L0_xattn_Wq, L0_xattn_bq, L0_xattn_Wk, L0_xattn_bk,
           L0_xattn_Wv, L0_xattn_bv, L0_xattn_Wo, L0_xattn_bo, L0_xattn_ln_gamma, L0_xattn_ln_beta,
           L0_xattn_residual_scale, L0_ffn_gate_weight, L0_ffn_gate_up_proj, L0_ffn_down_proj):
    import numpy as np
    import concourse.bacc as bacc
    from concourse.bass_utils import run_bass_kernel_spmd

    def c(a):
        return np.ascontiguousarray(np.asarray(a))

    def by_rows(w):
        return np.asarray(w).T.reshape(-1, P, w.shape[0]).transpose(1, 0, 2)

    mask = np.tile(np.asarray(mask_BxS2_ik0).T, (2, 1))
    ctx_t = np.asarray(ctx_2048)[[0, 1, 2, 3, 0]].transpose(2, 0, 1).reshape(KC, P, CT).transpose(1, 0, 2)
    w_attn = np.stack([by_rows(w).reshape(P, KC * H) for w in (L0_xattn_Wk, L0_xattn_Wv, L0_xattn_Wq, L0_xattn_Wo)])
    b_cols = np.stack([np.asarray(b).reshape(KC, P).T for b in (L0_xattn_bq, L0_xattn_bk)], axis=1)
    b_rows = np.stack([np.asarray(b) for b in (L0_xattn_bv, L0_xattn_bo, L0_xattn_ln_gamma, L0_xattn_ln_beta)])
    gates = np.concatenate([np.asarray(g).reshape(1) for g in (g_xattn, g_ffn, L0_xattn_residual_scale)])
    gate_t = by_rows(L0_ffn_gate_weight)
    gu = np.asarray(L0_ffn_gate_up_proj).reshape(E, 2, GU, 256, KC, P).transpose(0, 2, 5, 4, 1, 3)
    dn = np.asarray(L0_ffn_down_proj).reshape(E, H, DH, 4, P).transpose(0, 2, 4, 3, 1)
    w_exp = np.concatenate([gu.reshape(E, GU, P, PW), dn.reshape(E, DH, P, PW)], axis=1)

    ins = dict(x=np.asarray(x).reshape(TOK, H), ctx_t=ctx_t, mask=mask, w_attn=w_attn, b_cols=b_cols,
               b_rows=b_rows, gates=gates, gate_t=gate_t, w_exp=w_exp)
    nc = bacc.Bacc("TRN2", target_bir_lowering=False, num_devices=1)
    arrays, aps = {}, {}
    for name, a in ins.items():
        arrays[f"in_{name}"] = c(a)
        aps[name] = nc.dram_tensor(f"in_{name}", a.shape, mybir.dt.from_np(a.dtype), kind="ExternalInput").ap()
    out = nc.dram_tensor("out_rows", [TOK + P, H], F32, kind="ExternalOutput").ap()
    flamingo_gated_block(nc, out=out, **aps)
    r = run_bass_kernel_spmd(nc, [arrays], core_ids=[0])
    return r.results[0]["out_rows"][:TOK].reshape(NB, S, H)
```

```python
import concourse.bass as bass
from concourse import mybir
from contextlib import ExitStack

ALU = mybir.AluOpType
ACT = mybir.ActivationFunctionType
AX = mybir.AxisListType
F32 = mybir.dt.float32
F32R = mybir.dt.float32r
I32 = mybir.dt.int32
F16 = mybir.dt.float16

P = 128
H = 512
KC = H // P
NB = 4
S = 512
TT = S // P
NT = NB * TT
TOK = NB * S
T = 64
CT = (NB + 1) * T
NH, HD = 16, 32
PAIRS = NH // 2
E = 8
I = 1024
TOPK = 2
GU = 4
DH = 2
PW = 4 * 512
IC = I // P
MAXT = TOK * TOPK // P + E - 1
V_ORDER = (3, 0, 1, 2)
SLOTT = MAXT + 1
EPS = 1e-5
INV_SCALE = float(HD) ** -0.5
CLIP = 50.0 / INV_SCALE
NEG_BIG = -3.0e38
HW = H + E


def flamingo_gated_block(nc, x, ctx_t, mask, w_attn, b_cols, b_rows, gates, gate_t, w_exp, out):
    st = ExitStack()
    with st:
        def sb(name, shape, dt=F32, scope=st):
            return scope.enter_context(nc.sbuf_tensor(name, shape, dt))

        def sem(name):
            return st.enter_context(nc.semaphore(name))

        bank = [st.enter_context(nc.psum_tensor(f"bank{i}", [P, 512], F32)) for i in range(8)]
        h_dram = nc.dram_tensor("h_rows", [TOK + P, HW], F32).ap()
        h_rows = h_dram.rearrange("(n p) d -> n p d", p=P)[:, :, 0:H]
        h_cw = h_dram.rearrange("(n p) d -> p n d", p=P)[:, 0:NT, H:HW]
        pad_cw = h_dram.rearrange("(n p) d -> n p d", p=P)[NT][:, H:HW]
        out_rows = out.rearrange("(n p) d -> n p d", p=P)
        x_b = x.rearrange("(b t p) d -> b p t d", p=P, t=TT)

        ident = sb("ident", [P, P])
        logits_t = sb("logits_t", [E, TOK])
        gate_w = sb("gate_w", [P, KC, E])
        gsc = sb("gsc", [P, 3])
        tg = sb("tg", [P, 3])
        slot_idx = sb("slot_idx", [P, SLOTT], I32)
        w_cur = sb("w_cur", [P, 1])
        tile_tab = sb("tile_tab", [P, SLOTT, 4], I32)
        n_tiles = sb("n_tiles", [P, 4], I32)
        iota_e = sb("iota_e", [P, NT, E])
        iota_e2 = sb("iota_e2", [P, NT, E])
        iota_n = sb("iota_n", [P, E, 16])
        iota_tile = sb("iota_tile", [P, SLOTT], F16)
        iota_p = sb("iota_p", [P, P], F16)
        tok1 = sb("tok1", [P, NT], F16)
        pidx = sb("pidx", [P, 1])
        tri = sb("tri", [P, E, E])
        upper = sb("upper", [P, P], F16)
        ones = sb("ones", [P, P], F16)

        pa = ExitStack()
        o_un = sb("o_un", [P, KC, S], F32, pa)
        sc = sb("sc", [P, 2, S], F32, pa)
        ex = sb("ex", [P, 2, S], F32, pa)
        o_hi = sb("o_hi", [P, KC, S], F32R, pa)
        o_lo = sb("o_lo", [P, KC, S], F32R, pa)
        dh = sb("dh", [P, TT, H], F32, pa)
        xr = sb("xr", [P, TT, H], F32, pa)
        w_hi = sb("w_hi", [P, 2, KC, H], F32R, pa)
        w_lo = sb("w_lo", [P, 2, KC, H], F32R, pa)
        kvw = ExitStack()
        wk_hi, wk_lo, wv_hi, wv_lo = (sb(n, [P, KC, H], F32R, kvw) for n in ("wk_hi", "wk_lo", "wv_hi", "wv_lo"))
        kvw.close()
        xt_hi = sb("xt_hi", [P, KC, S], F32R, pa)
        xt_lo = sb("xt_lo", [P, KC, S], F32R, pa)
        q_hi = sb("q_hi", [P, KC, S], F32R, pa)
        q_lo = sb("q_lo", [P, KC, S], F32R, pa)
        c_raw = sb("c_raw", [P, KC, CT], F32, pa)
        cts = ExitStack()
        c_hi = sb("c_hi", [P, KC, CT], F32R, cts)
        c_lo = sb("c_lo", [P, KC, CT], F32R, cts)
        cts.close()
        ex_hi = sb("ex_hi", [P, 2, S], F32R, pa)
        ex_lo = sb("ex_lo", [P, 2, S], F32R, pa)
        ht = sb("ht", [P, 2, KC, P], F32, pa)
        k_all = sb("k_all", [P, KC, NB * T], F32, pa)
        v_all = sb("v_all", [P, NB + 1, H], F32, pa)
        kbd_hi = sb("kbd_hi", [P, KC, P], F32R, pa)
        kbd_lo = sb("kbd_lo", [P, KC, P], F32R, pa)
        vbd_hi = sb("vbd_hi", [P, KC, 2, 4, HD], F32R, pa)
        vbd_lo = sb("vbd_lo", [P, KC, 2, 4, HD], F32R, pa)
        hsel = sb("hsel", [P, P + NH], F32R, pa)
        bsel = sb("bsel", [NH, KC, 4, HD], F32R, pa)
        den = sb("den", [NH, S], F32, pa)
        rden = sb("rden", [NH, S], F32, pa)
        r_hi = sb("r_hi", [NH, S], F32R, pa)
        r_lo = sb("r_lo", [NH, S], F32R, pa)
        xs = sb("xs", [P, TT, H], F32, pa)
        hs = sb("hs", [P, TT, H], F32, pa)
        rows = sb("rows", [P, 4, H], F32, pa)
        o_n = sb("o_n", [P, 2, S], F32, pa)
        bcol = sb("bcol", [P, 2, KC], F32, pa)
        lim = sb("lim", [P, NB], F32, pa)
        mask_sb = sb("mask_sb", [P, NB], I32, pa)
        st_a = sb("st_a", [P, TT, 6], F32, pa)
        mv_a = sb("mv_a", [P, TT, 2], F32, pa)
        ve_a = sb("ve_a", [P, TT], F32, pa)
        rs_a = sb("rs_a", [P, TT], F32, pa)
        mn_a = sb("mn_a", [P, TT], F32, pa)
        nm_a = sb("nm_a", [P, TT], F32, pa)
        st6 = sb("st6", [P, TT, 6], F32, pa)
        mv = sb("mv", [P, TT, 2], F32, pa)
        ve = sb("ve", [P, TT], F32, pa)
        rs = sb("rs", [P, TT], F32, pa)
        st6h = sb("st6h", [P, TT, 6], F32, pa)
        mvh = sb("mvh", [P, TT, 2], F32, pa)
        veh = sb("veh", [P, TT], F32, pa)
        rsh = sb("rsh", [P, TT], F32, pa)
        mhalf = sb("mhalf", [P, TT], F32, pa)
        pa.close()

        pe_ = ExitStack()
        raw = sb("raw", [P, GU + DH, PW], F32, pe_)
        g_hi = sb("g_hi", [P, GU, KC, 512], F32R, pe_)
        g_lo = sb("g_lo", [P, GU, KC, 512], F32R, pe_)
        dn_hi = sb("dn_hi", [P, DH, 4, H], F32R, pe_)
        dn_lo = sb("dn_lo", [P, DH, 4, H], F32R, pe_)
        xg = sb("xg", [P, HW + 1], F32, pe_)
        gt_hi = sb("gt_hi", [P, KC, P], F32R, pe_)
        gt_lo = sb("gt_lo", [P, KC, P], F32R, pe_)
        silu = sb("silu", [P, GU, 256], F32, pe_)
        hid = sb("hid", [P, GU, 256], F32, pe_)
        hd_hi = sb("hd_hi", [P, IC, P], F32R, pe_)
        hd_lo = sb("hd_lo", [P, IC, P], F32R, pe_)
        y_sb = sb("y_sb", [P, H], F32, pe_)
        g_idx = sb("g_idx", [P, 1], I32, pe_)
        s_idx = sb("s_idx", [P, 1], I32, pe_)

        pr = ExitStack()
        NE3, NE4, OH4 = [P, NT, E], [P, TOPK, NT, E], [P, TOPK, NT, SLOTT]
        logits = sb("logits", NE3, F32, pr)
        eq = sb("eq", NE3, F32, pr)
        tmp3 = sb("tmp3", NE3, F32, pr)
        lg2 = sb("lg2", NE3, F32, pr)
        oh = sb("oh", NE4, F32, pr)
        sel = sb("sel", [P, NT + 1, E], F16, pr)
        cw = sb("cw", NE3, F32, pr)
        m1 = sb("m1", [P, NT, 1], F32, pr)
        m2 = sb("m2", [P, NT, 1], F32, pr)
        i1 = sb("i1", [P, NT, 1], F32, pr)
        wk = sb("wk", [P, TOPK, NT], F32, pr)
        wden = sb("wden", [P, NT], F32, pr)
        prod = sb("prod", NE4, F32, pr)
        rank = sb("rank", [P, TOPK, NT], F32, pr)
        rank_i = sb("rank_i", [P, TOPK, NT], I32, pr)
        tile_i = sb("tile_i", [P, TOPK, NT], I32, pr)
        place_i = sb("place_i", [P, TOPK, NT], I32, pr)
        tile_f = sb("tile_f", [P, TOPK, NT], F16, pr)
        place_f = sb("place_f", [P, TOPK, NT], F16, pr)
        base_f = sb("base_f", [P, TOPK, NT], F32, pr)
        cmp_n = sb("cmp_n", [P, E, 16], F32, pr)
        tl = sb("tl", [P, E, 1], F32, pr)
        trm = sb("trm", [P, E, E], F32, pr)
        tend = sb("tend", [P, E, 1], F32, pr)
        base = sb("base", [P, E], F32, pr)
        ind = sb("ind", [P, E, SLOTT], F32, pr)
        tabf = sb("tabf", [P, SLOTT, 4], F32, pr)
        oh_place = sb("oh_place", [P, TOPK, NT, P], F16, pr)
        oh_tile = sb("oh_tile", OH4, F16, pr)
        tok_tile = sb("tok_tile", OH4, F16, pr)
        tv = sb("tv", [P, SLOTT], F32, pr)
        tz = sb("tz", [P, SLOTT], F32, pr)
        pr.close()
        pe_.close()

        def f32(ap):
            return ap.bitcast(F32)

        wload = [sem(f"attn_weights{w}_loaded") for w in range(4)]
        cload, xload, rload, crload, setup = (sem(n) for n in
            ("constants_loaded", "x_loaded", "residual_loaded", "context_loaded", "pool_setup"))
        gates_ready, w_hi_done, w_lo_done = sem("gates_ready"), sem("attn_w_hi"), sem("attn_w_lo")
        dset = sem("vector_setup")
        ln_bias, ln_stats, ln_mean, ln_var, ln_rstd, hs_done = (sem(n) for n in
            ("ln_bias", "ln_stats", "ln_mean", "ln_var", "ln_rstd", "hs_done"))
        xt_tr, xt_h, xt_l = sem("xt_transposed"), sem("xt_hi_done"), sem("xt_lo_done")
        c_h, c_l, kv_mm, kv_sb, k_h, k_l, v_h, v_l = (sem(n) for n in
            ("context_hi", "context_lo", "kv_product", "kv_biased", "k_hi_placed", "k_lo_placed",
             "v_hi_placed", "v_lo_placed"))
        q_mm, q_h, q_l = sem("q_product"), sem("q_hi_done"), sem("q_lo_done")
        s_mm, s_clip, s_exp, e_h, e_l = (sem(n) for n in
            ("scores_product", "scores_clipped", "exp_done", "exp_hi_done", "exp_lo_done"))
        pair_mm, o_ev, den_c, den_r, r_h, r_l, r_mm, o_nd, o_h, o_l = (sem(n) for n in
            ("pair_product", "context_copied", "sums_copied", "sums_inverted", "inverse_hi", "inverse_lo",
             "inverse_spread", "context_normalised", "o_hi_done", "o_lo_done"))
        d_mm, d_ready, dstats, dmean, dvar, drstd, dgam, xb_done, x1_done = (sem(n) for n in
            ("delta_product", "delta_scaled", "delta_stats", "delta_mean", "delta_var", "delta_rstd",
             "delta_gamma", "x_with_beta", "x1_done"))
        hstats, hmean, hvar, hrstd, h_done = (sem(n) for n in
            ("h_stats", "h_mean", "h_var", "h_rstd", "h_done"))
        h_tr, h_ev, lg_mm, lg_done = (sem(n) for n in
            ("h_transposed", "h_evacuated", "logits_product", "logits_done"))
        x1_store, h_store, pad_store = sem("x1_stored"), sem("h_stored"), sem("pad_rows_stored")
        rt, rt_pool, rt_act, rt_pe = (sem(n) for n in
            ("routing_vector", "routing_pool", "routing_act", "routing_product"))
        slots, cw_ready, cw_store, w_next = (sem(n) for n in
            ("slots_ready", "combine_weights_ready", "combine_weights_stored", "slot_weights_copied"))
        tables = sem("tables_ready")
        raw_in = [sem(f"raw_piece{p}_loaded") for p in range(GU + DH)]
        gu_hi, gu_split, dn_h, dn_split = (sem(n) for n in
            ("gu_hi_done", "gu_split_done", "down_hi_done", "down_split_done"))
        idx_0, idx_g, idx_s, gath, scat = (sem(n) for n in
            ("first_index", "gather_index", "scatter_index", "rows_gathered", "rows_scattered"))
        gt_tr, gt_h, gt_l = sem("slot_rows_transposed"), sem("slot_rows_hi"), sem("slot_rows_lo")
        gu_mm, silu_done, hid_done, hd_tr, hd_h, hd_l = (sem(n) for n in
            ("gate_up_product", "silu_done", "hidden_done", "hidden_transposed", "hidden_hi", "hidden_lo"))
        y_mm, y_ready, y_free = sem("down_product"), sem("y_ready"), sem("y_added")

        block = st.enter_context(nc.Block())

        def product3(eng, psum, a_hi, a_lo, b_hi, b_lo, n=KC, first=True, last=True):
            for k in range(n):
                for j, (a, b) in enumerate(((a_hi, b_hi), (a_hi, b_lo), (a_lo, b_hi))):
                    mm = eng.matmul(psum, a(k), b(k), start=(first and k == 0 and j == 0),
                                    stop=(last and k == n - 1 and j == 2))
            return mm

        weight_halves = ((wk_hi[:, :, :], wk_lo[:, :, :]), (wv_hi[:, :, :], wv_lo[:, :, :]),
                         (w_hi[:, 0, :, :], w_lo[:, 0, :, :]), (w_hi[:, 1, :, :], w_lo[:, 1, :, :]))

        def h_bank(t, tail):
            return bank[t % 2 + (4 if tail and t >= 2 else 0)]

        def v_heads(n, q, g):
            v = v_all[g * T:g * T + T, bass.ds(n + 1 - g, 1), :].rearrange("p o (m a d) -> p (o m) a d", m=KC, a=4)
            return v[:, :, 2 * q + g, :]

        def tile_entry(eng, tile, column, most):
            return eng.value_load(tile_tab[0:1, bass.ds(tile, 1), column:column + 1].rearrange("p a b -> p (a b)"),
                                  min_val=0, max_val=most)

        def plain(eng):
            eng.wait_ge(wload[0], 16)

        @block.sync
        def _(sp):
            sp.sem_inc(x1_store, 16 * TT)
            sp.sem_inc(h_store, 16 * TT)
            sp.dma_start(c_raw[:, :, :], ctx_t).then_inc(crload, 16)
            for w in range(2):
                sp.dma_start(raw[:, w, :], w_attn[w]).then_inc(wload[w], 16)
            sp.dma_start(xs[:, :, :], x_b[0]).then_inc(xload, 16)
            for w in range(2, 4):
                sp.dma_start(raw[:, w, :], w_attn[w]).then_inc(wload[w], 16)
            sp.wait_ge(w_lo_done, 4)

            def stores(n):
                for t in range(TT):
                    sp.wait_ge(x1_done, n * TT + t + 1)
                    sp.dma_start(out_rows[n * TT + t], xr[:, t, :]).then_inc(x1_store, 16)
                    sp.wait_ge(h_done, n * TT + t + 1)
                    sp.dma_start(h_rows[n * TT + t], dh[:, t, :]).then_inc(h_store, 16)

            def batch(b, back, front):
                if front:
                    sp.wait_ge(hs_done, b * TT + TT)
                    sp.dma_start(xs[:, :, :], x_b[b + 1]).then_inc(xload, 16)
                if back:
                    stores(b - 1)
                sp.wait_ge(x1_store, (b + 1) * 16 * TT)
                sp.dma_start(xr[:, :, :], x_b[b]).then_inc(rload, 16)

            batch(0, False, True)
            with sp.Fori(1, NB - 1) as b:
                batch(b, True, True)
            batch(NB - 1, True, False)
            sp.wait_ge(o_nd, NT)
            sp.wait_ge(e_l, NB * PAIRS)
            for p in range(2):
                sp.dma_start(raw[:, p, :], w_exp[0, p]).then_inc(raw_in[p], 16)
            sp.wait_ge(d_mm, NT)
            for p in range(2, GU):
                sp.dma_start(raw[:, p, :], w_exp[0, p]).then_inc(raw_in[p], 16)
            stores(NB - 1)
            sp.wait_ge(x1_store, 16 * (NT + TT))
            sp.wait_ge(h_store, 16 * (NT + TT))
            sp.wait_ge(lg_done, TT + NT)
            for p in range(GU, GU + DH):
                sp.dma_start(raw[:, p, :], w_exp[0, p]).then_inc(raw_in[p], 16)
            sp.wait_ge(cw_ready, 1)
            sp.dma_start(h_cw, cw[:, :, :]).then_inc(cw_store, 16)
            sp.wait_ge(gath, 16)
            with sp.Fori(1, E) as e:
                for p in range(GU):
                    sp.wait_ge(gu_split, (e - 1) * GU + p + 1)
                    sp.dma_start(raw[:, p, :], w_exp[e, p]).then_inc(raw_in[p], 16)
                for p in range(DH):
                    sp.wait_ge(dn_split, (e - 1) * DH + p + 1)
                    sp.dma_start(raw[:, GU + p, :], w_exp[e, GU + p]).then_inc(raw_in[GU + p], 16)

        @block.vector
        def _(dve):
            dve.sem_inc(hd_l, 2)
            dve.sem_inc(lg_done, TT)
            dve.wait_ge(crload, 16)
            dve.wait_ge(c_h, 1)
            dve.tensor_tensor(c_lo[:, :, :], c_raw[:, :, :], f32(c_hi[:, :, :]), ALU.subtract).then_inc(c_l, 1)

            def split_weight(w):
                hi, lo = (a.rearrange("p k n -> p (k n)") for a in weight_halves[w])
                dve.wait_ge(w_hi_done, w + 1)
                dve.tensor_tensor(lo, raw[:, w, :], f32(hi), ALU.subtract).then_inc(w_lo_done, 1)

            def ln_statistics(n, tiles=range(TT)):
                for t in tiles:
                    if t == 0:
                        dve.wait_ge(xload, (n + 1) * 16)
                    bn = dve.bn_stats(st_a[:, t, :], xs[:, t, :])
                if TT - 1 not in tiles:
                    return
                bn.then_inc(ln_stats, 1)
                plain(dve)
                dve.wait_ge(ln_stats, n + 1)
                for t in range(TT):
                    bn = dve.bn_aggr(mv_a[:, t, :], st_a[:, t, :])
                bn.then_inc(ln_mean, 1)
                dve.wait_ge(ln_mean, n + 1)
                dve.tensor_scalar(mn_a[:, :], mv_a[:, :, 0], -1.0, None, ALU.mult)
                dve.tensor_scalar(ve_a[:, :], mv_a[:, :, 1], EPS, None, ALU.add).then_inc(ln_var, 1)

            def x_low(n, k):
                dve.wait_ge(xt_h, n * KC + k + 1)
                dve.tensor_tensor(xt_lo[:, k, :], bank[k % 2][:, :], f32(xt_hi[:, k, :]),
                                  ALU.subtract).then_inc(xt_l, 1)

            def q_low(n, m):
                dve.wait_ge(q_h, n * KC + m + 1)
                dve.scalar_tensor_tensor(out=q_lo[:, m, :], in0=bank[2 + m % 2][:, :], scalar=bcol[:, 0, m:m + 1],
                                         in1=f32(q_hi[:, m, :]), op0=ALU.add, op1=ALU.subtract).then_inc(q_l, 1)

            def k_low(n):
                for g in range(4):
                    r = slice(g * HD, g * HD + HD)
                    c = slice((g % 2) * T, (g % 2) * T + T)
                    dve.wait_ge(k_h, n * 4 + g + 1)
                    dve.tensor_tensor(kbd_lo[r, :, c], k_all[r, :, bass.ds(n * T, T)], f32(kbd_hi[r, :, c]),
                                      ALU.subtract).then_inc(k_l, 1)

            def v_low(n):
                for i in range(4):
                    q, g = i // 2, i % 2
                    r = slice(g * T, g * T + T)
                    dve.wait_ge(v_h, n * 4 + i + 1)
                    dve.tensor_tensor(vbd_lo[r, :, q, 2 * q + g, :], v_heads(n, q, g),
                                      f32(vbd_hi[r, :, q, 2 * q + g, :]), ALU.subtract).then_inc(v_l, 1)

            def invert_sums(n):
                dve.wait_ge(den_c, n + 1)
                dve.reciprocal(rden[:, :], den[:, :]).then_inc(den_r, 1)
                dve.wait_ge(den_r, n + 1)
                dve.tensor_scalar(r_hi[:, :], rden[:, :], 1.0, None, ALU.mult).then_inc(r_h, 1)
                dve.wait_ge(r_h, n + 1)
                dve.tensor_tensor(r_lo[:, :], rden[:, :], f32(r_hi[:, :]), ALU.subtract).then_inc(r_l, 1)

            def normalise(n, m):
                dve.wait_ge(r_mm, n * KC + m + 1)
                dve.wait_ge(o_ev, n * KC + m + 1)
                if m >= 2:
                    dve.wait_ge(o_l, n * KC + m - 1)
                dve.tensor_tensor(o_n[:, m % 2, :], bank[m % 2][:, :], o_un[:, m, :], ALU.mult).then_inc(o_nd, 1)

            def update_and_residual(n, u, r):
                if r is not None:
                    dve.wait_ge(dgam, n * TT + r + 1)
                    dve.wait_ge(drstd, n * TT + r + 1)
                    dve.wait_ge(xb_done, n * TT + r + 1)
                    dve.scalar_tensor_tensor(out=xr[:, r, :], in0=dh[:, r, :], scalar=rs[:, r:r + 1],
                                             in1=xr[:, r, :], op0=ALU.mult, op1=ALU.add).then_inc(x1_done, 1)
                    dve.wait_ge(x1_done, n * TT + r + 1)
                    dve.bn_stats(st6h[:, r, :], xr[:, r, :]).then_inc(hstats, 1)
                if u is not None:
                    dve.wait_ge(h_store, (n + 1) * 16 * TT)
                    dve.wait_ge(d_mm, n * TT + u + 1)
                    dve.scalar_tensor_tensor(out=dh[:, u, :], in0=bank[2 + u % 2][:, :], scalar=tg[:, 2:3],
                                             in1=rows[:, 1, :], op0=ALU.mult, op1=ALU.add).then_inc(d_ready, 1)
                if r is not None:
                    plain(dve)
                    dve.wait_ge(hstats, n * TT + r + 1)
                    dve.bn_aggr(mvh[:, r, :], st6h[:, r, :]).then_inc(hmean, 1)
                if u is not None:
                    dve.wait_ge(d_ready, n * TT + u + 1)
                    dve.bn_stats(st6[:, u, :], dh[:, u, :]).then_inc(dstats, 1)
                if r is not None:
                    dve.wait_ge(hmean, n * TT + r + 1)
                    dve.tensor_scalar(veh[:, r:r + 1], mvh[:, r, 1:2], EPS, None, ALU.add).then_inc(hvar, 1)
                if u is not None:
                    plain(dve)
                    dve.wait_ge(dstats, n * TT + u + 1)
                    dve.bn_aggr(mv[:, u, :], st6[:, u, :]).then_inc(dmean, 1)
                    dve.wait_ge(dmean, n * TT + u + 1)
                    dve.tensor_scalar(ve[:, u:u + 1], mv[:, u, 1:2], EPS, None, ALU.add).then_inc(dvar, 1)
                    dve.scalar_tensor_tensor(out=dh[:, u, :], in0=dh[:, u, :], scalar=mv[:, u, 0:1],
                                             in1=rows[:, 2, :], op0=ALU.subtract, op1=ALU.mult).then_inc(dgam, 1)

            def normalised(n, t):
                dve.wait_ge(hrstd, n * TT + t + 1)
                dve.tensor_scalar(dh[:, t, :], xr[:, t, :], mvh[:, t, 0:1], rsh[:, t:t + 1],
                                  ALU.subtract, ALU.mult).then_inc(h_done, 1)

            def keep_logits(n, t, tail=False):
                dve.wait_ge(lg_mm, n * TT + t + 1)
                dve.tensor_copy(logits_t[:, bass.ds((n * TT + t) * P, P)],
                                h_bank(t, tail)[0:E, 0:P]).then_inc(lg_done, 1)

            def batch(b, back, front):
                for s in range(PAIRS + 1):
                    if s < PAIRS:
                        dve.wait_ge(s_mm, b * PAIRS + s + 1)
                        if s >= 2 or back:
                            dve.wait_ge(s_exp, b * PAIRS + s - 1)
                        dve.tensor_scalar(sc[:, s % 2, :], bank[4 + s % 2][:, :], lim[:, bass.ds(b, 1)], -CLIP,
                                          ALU.min, ALU.max).then_inc(s_clip, 1)
                    if s == 0:
                        if back:
                            normalise(b - 1, 0)
                            normalise(b - 1, 1)
                        q_low(b, 2)
                        if back:
                            v_low(b)
                            normalise(b - 1, 2)
                            normalise(b - 1, 3)
                        q_low(b, 3)
                    if s in (1, 2) and front:
                        ln_statistics(b + 1, range(2 * s - 2, 2 * s))
                    if 4 <= s < 8 and back:
                        normalised(b - 1, s - 4)
                    if s == 4 and front:
                        x_low(b + 1, 0)
                        x_low(b + 1, 1)
                    if 2 <= s < 7 and back:
                        update_and_residual(b - 1, s - 2 if s < 6 else None, s - 3 if s > 2 else None)
                    if s == 4 and front:
                        x_low(b + 1, 2)
                        x_low(b + 1, 3)
                    if s in (6, 7) and front:
                        q_low(b + 1, s - 6)
                    if s >= 6 and back:
                        keep_logits(b - 1, s - 6)
                if front:
                    k_low(b + 1)
                if back:
                    keep_logits(b - 1, 3)
                invert_sums(b)

            split_weight(0)
            split_weight(1)
            ln_statistics(0)
            dve.wait_ge(cload, 80)
            dve.tensor_scalar(tg[:, 2:3], gsc[:, 2:3], 0.0, 0.3, ALU.max, ALU.min).then_inc(dset, 1)
            dve.tensor_scalar(lim[:, :], mask_sb[:, :], 0.5, 2.0 * CLIP, ALU.is_gt, ALU.mult).then_inc(dset, 1)
            dve.wait_ge(dset, 2)
            dve.wait_ge(gates_ready, 1)
            dve.tensor_scalar(lim[:, :], lim[:, :], -CLIP, None, ALU.add).then_inc(dset, 1)
            dve.tensor_scalar(rows[:, 1, :], rows[:, 1, :], tg[:, 2:3], None, ALU.mult).then_inc(dset, 1)
            dve.tensor_scalar(rows[:, 2:4, :], rows[:, 2:4, :], tg[:, 0:1], None, ALU.mult).then_inc(dset, 1)
            dve.wait_ge(dset, 5)
            dve.wait_ge(kv_mm, 1)
            for h in range(2):
                dve.tensor_tensor(k_all[:, 2 * h:2 * h + 2, :], bank[6 + h][:, :].rearrange("p (k t) -> p k t", k=2),
                                  bcol[:, 1, 2 * h:2 * h + 2].unsqueeze(2).to_broadcast([P, 2, NB * T]),
                                  ALU.add).then_inc(kv_sb, 1)

            def v_bias(i, places):
                dve.wait_ge(kv_mm, i + 2)
                for place in places:
                    dve.tensor_tensor(v_all[:, place, :], bank[2 + (place - 1) % NB][:, :], rows[:, 0, :],
                                      ALU.add).then_inc(kv_sb, 1)

            v_bias(0, (NB, 0))
            x_low(0, 0)
            x_low(0, 1)
            split_weight(2)
            v_bias(1, (1,))
            x_low(0, 2)
            x_low(0, 3)
            v_bias(2, (2,))
            k_low(0)
            v_low(0)
            v_bias(3, (3,))
            q_low(0, 0)
            q_low(0, 1)
            split_weight(3)
            batch(0, False, True)
            with dve.Fori(1, NB - 1) as b:
                batch(b, True, True)
            batch(NB - 1, True, False)
            normalise(NB - 1, 0)
            for m in range(KC):
                if m < KC - 1:
                    normalise(NB - 1, m + 1)
                dve.wait_ge(o_h, (NB - 1) * KC + m + 1)
                dve.tensor_tensor(o_lo[:, m, :], o_n[:, m % 2, :], f32(o_hi[:, m, :]), ALU.subtract).then_inc(o_l, 1)
            for t in range(TT + 2):
                if t <= TT:
                    update_and_residual(NB - 1, t if t < TT else None, t - 1 if t > 0 else None)
                if t >= 2:
                    normalised(NB - 1, t - 2)
            for t in range(TT):
                keep_logits(NB - 1, t, tail=True)

            def split_lo(dst, hi, p, done):
                dve.tensor_tensor(dst.rearrange("p k n -> p (k n)"), raw[:, p, :],
                                  f32(hi.rearrange("p k n -> p (k n)")), ALU.subtract).then_inc(done, 1)

            def first_gu(p):
                dve.wait_ge(gu_hi, p + 1)
                split_lo(g_lo[:, p, :, :], g_hi[:, p, :, :], p, gu_split)

            step = [0]

            def link(ins):
                step[0] += 1
                ins.then_inc(rt, 1)
                dve.wait_ge(rt, step[0])

            def bc(ap):
                return ap.to_broadcast(NE3)

            dve.wait_ge(rt_pool, 12)
            dve.wait_ge(rt_pe, 1)
            link(dve.tensor_copy(logits[:, :, :], bank[3][:, 0:NT * E].rearrange("p (t e) -> p t e", e=E)))

            def choose(c, lg, m):
                link(dve.tensor_reduce(m[:, :, 0], lg, AX.X, ALU.max))
                link(dve.tensor_tensor(eq[:, :, :], lg, bc(m[:, :, :]), ALU.is_equal))
                link(dve.scalar_tensor_tensor(out=tmp3[:, :, :], in0=eq[:, :, :], scalar=-float(E),
                                              in1=iota_e[:, :, :], op0=ALU.mult, op1=ALU.add))
                link(dve.tensor_reduce(i1[:, :, 0], tmp3[:, :, :], AX.X, ALU.min))
                link(dve.tensor_tensor(oh[:, c, :, :], iota_e2[:, :, :], bc(i1[:, :, :]), ALU.is_equal))

            choose(0, logits[:, :, :], m1)
            link(dve.scalar_tensor_tensor(out=lg2[:, :, :], in0=oh[:, 0, :, :], scalar=NEG_BIG,
                                          in1=logits[:, :, :], op0=ALU.mult, op1=ALU.add))
            choose(1, lg2[:, :, :], m2)
            link(dve.tensor_tensor(wk[:, 1, :], m2[:, :, 0], m1[:, :, 0], ALU.subtract))
            diff_step[0] = step[0]
            dve.memset(sel[:, NT, :], 0.0)
            link(dve.tensor_tensor(sel[:, 0:NT, :], oh[:, 0, :, :], oh[:, 1, :, :], ALU.add))
            sel_step[0] = step[0]
            dve.wait_ge(rt_act, 1)
            link(dve.tensor_scalar(wden[:, :], wk[:, 1, :], 1.0, None, ALU.add))
            link(dve.reciprocal(wk[:, 0, :], wden[:, :]))
            link(dve.tensor_scalar(wk[:, 0, :], wk[:, 0, :], tg[:, 1:2], None, ALU.mult))
            link(dve.tensor_tensor(wk[:, 1, :], wk[:, 1, :], wk[:, 0, :], ALU.mult))
            link(dve.tensor_tensor(prod[:, :, :, :], oh[:, :, :, :],
                                   wk[:, :, :].unsqueeze(3).to_broadcast(NE4), ALU.mult))
            link(dve.tensor_tensor(cw[:, :, :], prod[:, 0, :, :], prod[:, 1, :, :], ALU.add))
            dve.sem_inc(cw_ready, 1)
            dve.wait_ge(rt_pe, 2)
            link(dve.tensor_tensor(prod[:, :, :, :], oh[:, :, :, :],
                                   bank[0][:, 0:NT * E].rearrange("p (t e) -> p t e", e=E).unsqueeze(1).to_broadcast(NE4),
                                   ALU.mult))
            link(dve.tensor_reduce(rank[:, :, :], prod[:, :, :, :], AX.X, ALU.add))
            link(dve.tensor_copy(rank_i[:, :, :], rank[:, :, :]))
            link(dve.tensor_scalar(place_i[:, :, :], rank_i[:, :, :], P - 1, None, ALU.bitwise_and))
            link(dve.tensor_copy(place_f[:, :, :], place_i[:, :, :]))
            link(dve.tensor_tensor(cmp_n[:, :, :], bank[0][:, NT * E:(NT + 1) * E].unsqueeze(2).to_broadcast([P, E, 16]),
                                   iota_n[:, :, :], ALU.is_gt))
            link(dve.tensor_reduce(tl[:, :, 0], cmp_n[:, :, :], AX.X, ALU.add))
            link(dve.tensor_scalar(tl[:, :, 0], tl[:, :, 0], 1.0, None, ALU.max))
            link(dve.tensor_tensor(trm[:, :, :], tri[:, :, :],
                                   tl[:, :, 0].unsqueeze(1).to_broadcast([P, E, E]), ALU.mult))
            link(dve.tensor_reduce(tend[:, :, 0], trm[:, :, :], AX.X, ALU.add))
            link(dve.tensor_tensor(base[:, :], tend[:, :, 0], tl[:, :, 0], ALU.subtract))
            link(dve.tensor_tensor(prod[:, :, :, :], oh[:, :, :, :],
                                   base[:, :].unsqueeze(1).unsqueeze(1).to_broadcast(NE4), ALU.mult))
            link(dve.tensor_reduce(base_f[:, :, :], prod[:, :, :, :], AX.X, ALU.add))
            link(dve.tensor_scalar(tile_i[:, :, :], rank_i[:, :, :], 7, None, ALU.logical_shift_right))
            link(dve.tensor_copy(tile_f[:, :, :], tile_i[:, :, :]))
            link(dve.tensor_tensor(tile_f[:, :, :], tile_f[:, :, :], base_f[:, :, :], ALU.add))
            link(dve.tensor_tensor(oh_tile[:, :, :, :], iota_tile[:, :].unsqueeze(1).unsqueeze(1).to_broadcast(OH4),
                                   tile_f[:, :, :].unsqueeze(3).to_broadcast(OH4), ALU.is_equal))
            tile_step[0] = step[0]
            for c in range(TOPK):
                link(dve.tensor_tensor(oh_place[:, c, :, :], iota_p[:, :].unsqueeze(1).to_broadcast([P, NT, P]),
                                       place_f[:, c, :].unsqueeze(2).to_broadcast([P, NT, P]), ALU.is_equal))
                place_step[c] = step[0]
            dve.wait_ge(rt_pe, 3)
            link(dve.tensor_copy(tv[:, :], bank[2][:, 0:SLOTT]))
            link(dve.tensor_scalar(tz[:, :], tv[:, :], 0.0, pidx[:, 0:1], ALU.is_equal, ALU.mult))
            link(dve.scalar_tensor_tensor(out=tz[:, :], in0=tv[:, :], scalar=-1.0, in1=tz[:, :],
                                          op0=ALU.add, op1=ALU.add))
            link(dve.tensor_copy(slot_idx[:, :], tz[:, :]))
            dve.sem_inc(slots, 1)
            link(dve.tensor_tensor(ind[:, :, :], iota_tile[:, :].unsqueeze(1).to_broadcast([P, E, SLOTT]),
                                   tend[:, :, :].to_broadcast([P, E, SLOTT]), ALU.is_ge))
            link(dve.tensor_reduce(tabf[:, :, 0], ind[:, 0:E - 1, :].rearrange("p e n -> p n e"), AX.X, ALU.add))
            link(dve.memset(tabf[:, :, 1:4], 0.0))
            link(dve.tensor_tensor(tabf[:, 0:SLOTT - 1, 1], tabf[:, 1:SLOTT, 0], tabf[:, 0:SLOTT - 1, 0], ALU.subtract))
            link(dve.tensor_copy(tabf[:, 1:SLOTT, 2], tabf[:, 0:SLOTT - 1, 1]))
            link(dve.memset(tabf[:, 0:1, 2:3], 1.0))
            link(dve.tensor_copy(tile_tab[:, :, :], tabf[:, :, :]))
            link(dve.tensor_copy(n_tiles[:, 0:1], tend[:, E - 1, :]))
            dve.sem_inc(tables, 1)

            first_gu(0)
            dve.wait_ge(gt_h, 1)
            dve.tensor_tensor(gt_lo[:, :, :].rearrange("p k n -> p (k n)"), bank[6][:, :],
                              f32(gt_hi[:, :, :].rearrange("p k n -> p (k n)")), ALU.subtract).then_inc(gt_l, 1)
            first_gu(1)
            first_gu(2)
            first_gu(3)
            used = dve.value_load(n_tiles[0:1, 0:1], min_val=1, max_val=MAXT)
            with dve.Fori(0, used) as g:
                expert = tile_entry(dve, g, 0, E - 1)
                last = tile_entry(dve, g, 1, 1)
                first = tile_entry(dve, g, 2, 1)

                def hidden_lo(p):
                    dve.wait_ge(hd_h, g * GU + p + 1)
                    dve.tensor_tensor(hd_lo[:, 2 * p:2 * p + 2, :].rearrange("p k n -> p (k n)"),
                                      bank[4 + p % 2][:, 0:256],
                                      f32(hd_hi[:, 2 * p:2 * p + 2, :].rearrange("p k n -> p (k n)")),
                                      ALU.subtract).then_inc(hd_l, 1)

                def next_lo(p):
                    dve.wait_ge(gu_hi, expert * GU + GU + p + 1)
                    split_lo(g_lo[:, p, :, :], g_hi[:, p, :, :], p, gu_split)

                def down_lo(p):
                    dve.wait_ge(dn_h, expert * DH + p + 1)
                    split_lo(dn_lo[:, p, :, :], dn_hi[:, p, :, :], GU + p, dn_split)

                with dve.If(first):
                    down_lo(0)
                for p in range(GU):
                    dve.wait_ge(silu_done, g * GU + p + 1)
                    dve.tensor_tensor(hid[:, p, :], silu[:, p, :], bank[p][:, 256:512], ALU.mult).then_inc(hid_done, 1)
                    if p >= 2:
                        hidden_lo(p - 2)
                    if p < 2:
                        with dve.If(last):
                            next_lo(p)
                    if p == 1:
                        with dve.If(first):
                            down_lo(1)
                hidden_lo(GU - 2)
                hidden_lo(GU - 1)
                dve.wait_ge(gt_h, g + 2)
                dve.tensor_tensor(gt_lo[:, :, :].rearrange("p k n -> p (k n)"), bank[6][:, :],
                                  f32(gt_hi[:, :, :].rearrange("p k n -> p (k n)")), ALU.subtract).then_inc(gt_l, 1)
                with dve.If(last):
                    next_lo(2)
                    next_lo(3)

        @block.gpsimd
        def _(pool):
            pool.memset(ident[:, :], 0.0).then_inc(setup, 1)
            pool.wait_ge(setup, 1)
            pool.affine_select(out=ident[:, :], in_=ident[:, :], compare_op=ALU.not_equal, fill=1.0,
                               base=0, pattern=[[-1, P]], channel_multiplier=1).then_inc(setup, 1)
            pool.memset(mhalf[:, :], -0.5).then_inc(setup, 1)
            for tile in (kbd_hi, kbd_lo, vbd_hi, vbd_lo, hsel):
                pool.memset(f32(tile[:]), 0.0).then_inc(setup, 1)
            pool.memset(rden[:, :], 1.0).then_inc(setup, 1)
            pool.wait_ge(setup, 9)
            for g in range(2):
                pool.memset(f32(hsel[g * T:g * T + T, NH - 2 + g:NH - 1 + g]), 1.0).then_inc(setup, 1)
            pool.affine_select(out=bsel[:, :, :, :], in_=rden[:, :].rearrange("p (m a d) -> p m a d", m=KC, a=4),
                               compare_op=ALU.is_equal,
                               fill=0.0, base=0, pattern=[[-4, KC], [-1, 4], [0, HD]],
                               channel_multiplier=1).then_inc(setup, 1)
            pool.dma_start(out_rows[NT], f32(kbd_hi[:, :, :]).rearrange("p k n -> p (k n)")).then_inc(pad_store, 16)
            pool.dma_start(h_rows[NT], f32(kbd_hi[:, :, :]).rearrange("p k n -> p (k n)")).then_inc(pad_store, 16)
            pool.dma_start(pad_cw, f32(kbd_hi[:, 0, 0:E])).then_inc(pad_store, 16)

            def ln_inverse(n):
                pool.wait_ge(ln_var, n + 1)
                pool.tensor_tensor(rs_a[:, :], ve_a[:, :], mhalf[:, :], ALU.pow).then_inc(ln_rstd, 1)
                pool.wait_ge(ln_rstd, n + 1)
                pool.tensor_tensor(nm_a[:, :], mn_a[:, :], rs_a[:, :], ALU.mult).then_inc(ln_bias, 1)

            def o_low(n, m):
                pool.wait_ge(o_h, n * KC + m + 1)
                pool.tensor_tensor(o_lo[:, m, :], o_n[:, m % 2, :], f32(o_hi[:, m, :]), ALU.subtract).then_inc(o_l, 1)

            def add_beta(n, t):
                pool.wait_ge(rload, (n + 1) * 16)
                pool.tensor_tensor(xr[:, t, :], xr[:, t, :], rows[:, 3, :], ALU.add).then_inc(xb_done, 1)

            def inverse_delta(n, t):
                pool.wait_ge(dvar, n * TT + t + 1)
                pool.tensor_tensor(rs[:, t:t + 1], ve[:, t:t + 1], mhalf[:, 0:1], ALU.pow).then_inc(drstd, 1)

            def inverse_h(n, t):
                pool.wait_ge(hvar, n * TT + t + 1)
                pool.tensor_tensor(rsh[:, t:t + 1], veh[:, t:t + 1], mhalf[:, 0:1], ALU.pow).then_inc(hrstd, 1)

            def batch(b, back, front):
                for s in range(PAIRS + 1):
                    if s < PAIRS:
                        pool.wait_ge(e_h, b * PAIRS + s + 1)
                        pool.tensor_tensor(ex_lo[:, s % 2, :], ex[:, s % 2, :], f32(ex_hi[:, s % 2, :]),
                                           ALU.subtract).then_inc(e_l, 1)
                    if s == 0 and back:
                        for m in range(KC):
                            o_low(b - 1, m)
                    if s == 2 and front:
                        ln_inverse(b + 1)
                    if 2 <= s < 6 and back:
                        inverse_delta(b - 1, s - 2)
                    if 3 <= s < 7 and back:
                        inverse_h(b - 1, s - 3)
                    if 1 <= s < 5 and back:
                        add_beta(b - 1, s - 1)

            pool.wait_ge(setup, 12)
            ln_inverse(0)

            def pattern(ap, pat, base_, cm):
                pool.iota(ap, pattern=pat, base=base_, channel_multiplier=cm,
                          allow_small_or_imprecise_dtypes=True).then_inc(rt_pool, 1)

            pattern(iota_e[:, :, :], [[0, NT], [1, E]], -E, 0)
            pattern(iota_e2[:, :, :], [[0, NT], [1, E]], -2 * E, 0)
            pattern(iota_n[:, :, :], [[0, E], [P, 16]], 0, 0)
            pattern(iota_tile[:, :], [[1, SLOTT]], 0, 0)
            pattern(iota_p[:, :], [[1, P]], 0, 0)
            pattern(tok1[:, :], [[P, NT]], 1, 1)
            pattern(pidx[:, :], [[0, 1]], TOK + 1, 1)
            pool.memset(upper[:, :], 1.0).then_inc(rt_pool, 1)
            pool.memset(ones[:, :], 1.0).then_inc(rt_pool, 1)
            pool.memset(tri[:, :, :], 1.0).then_inc(rt_pool, 1)
            pool.wait_ge(rt_pool, 10)
            pool.affine_select(out=upper[:, :], in_=upper[:, :], compare_op=ALU.is_gt, fill=0.0,
                               base=0, pattern=[[1, P]], channel_multiplier=-1).then_inc(rt_pool, 1)
            pool.affine_select(out=tri[:, :, :], in_=tri[:, :, :], compare_op=ALU.is_ge, fill=0.0,
                               base=0, pattern=[[1, E], [-1, E]], channel_multiplier=0).then_inc(rt_pool, 1)
            pool.wait_ge(dset, 5)
            batch(0, False, True)
            with pool.Fori(1, NB - 1) as b:
                batch(b, True, True)
            batch(NB - 1, True, False)
            for t in range(TT):
                add_beta(NB - 1, t)
            for t in range(TT + 1):
                if t < TT:
                    inverse_delta(NB - 1, t)
                if t >= 1:
                    inverse_h(NB - 1, t - 1)

            pool.wait_ge(rt, tile_step[0])
            for c in range(TOPK):
                pool.tensor_tensor(tok_tile[:, c, :, :], oh_tile[:, c, :, :],
                                   tok1[:, :].unsqueeze(2).to_broadcast([P, NT, SLOTT]), ALU.mult).then_inc(rt_pool, 1)

            pool.wait_ge(slots, 1)
            pool.wait_ge(h_store, 16 * (NT + TT))
            pool.wait_ge(cw_store, 16)
            pool.wait_ge(pad_store, 48)

            def gather():
                pool.indirect_dma_start(out=xg[:, 0:HW], out_offset=None, in_=h_dram[:, :],
                                        in_offset=bass.IndirectOffsetOnAxis(ap=g_idx[:, 0:1], axis=0)
                                        ).then_inc(gath, 16)

            pool.tensor_copy(g_idx[:, :], slot_idx[:, 0:1]).then_inc(idx_0, 1)
            pool.wait_ge(idx_0, 1)
            gather()
            pool.wait_ge(tables, 1)
            used = pool.value_load(n_tiles[0:1, 0:1], min_val=1, max_val=MAXT)
            with pool.Fori(0, used) as g:
                pool.wait_ge(gath, g * 16 + 16)
                plain(pool)
                pool.wait_ge(gt_tr, g + 1)
                pool.wait_ge(w_next, g + 1)
                pool.tensor_copy(g_idx[:, :], slot_idx[:, bass.ds(g + 1, 1)]).then_inc(idx_g, 1)
                plain(pool)
                pool.wait_ge(idx_g, g + 1)
                gather()
                plain(pool)
                pool.wait_ge(y_ready, g + 2)
                pool.tensor_copy(s_idx[:, :], slot_idx[:, bass.ds(g, 1)]).then_inc(idx_s, 1)
                plain(pool)
                pool.wait_ge(idx_s, g + 1)
                pool.indirect_dma_start(out=out[:, :],
                                        out_offset=bass.IndirectOffsetOnAxis(ap=s_idx[:, 0:1], axis=0),
                                        in_=y_sb[:, :], in_offset=None,
                                        compute_op=ALU.add).then_inc(scat, 16)
                pool.wait_ge(scat, g * 16 + 16)
                pool.sem_inc(y_free, 1)
            pool.wait_ge(gath, used * 16 + 16)
            pool.wait_ge(x1_store, 16 * (NT + TT))

        @block.scalar
        def _(act):
            act.sem_inc(y_free, 1)
            act.dma_start(mask_sb[:, :], mask).then_inc(cload, 16)
            act.dma_start(bcol[:, :, :], b_cols).then_inc(cload, 16)
            act.dma_start(gsc[:, :], gates.partition_broadcast(P)).then_inc(cload, 16)
            act.dma_start(gate_w[:, :, :], gate_t).then_inc(cload, 16)
            act.dma_start(rows[:, :, :], b_rows.partition_broadcast(P)).then_inc(cload, 16)
            act.wait_ge(crload, 16)
            act.activation(c_hi[:, :, :], c_raw[:, :, :], ACT.Copy).then_inc(c_h, 1)

            def split_weight(w):
                act.wait_ge(wload[w], 16)
                hi = weight_halves[w][0].rearrange("p k n -> p (k n)")
                act.activation(hi, raw[:, w, :], ACT.Copy).then_inc(w_hi_done, 1)

            def normalise_x(n, tiles=range(TT)):
                act.wait_ge(ln_bias, n + 1)
                for t in tiles:
                    act.activation(hs[:, t, :], xs[:, t, :], ACT.Identity, scale=rs_a[:, t:t + 1],
                                   bias=nm_a[:, t:t + 1]).then_inc(hs_done, 1)

            def x_high(n, chunks=range(KC)):
                for k in chunks:
                    act.wait_ge(xt_tr, n * KC + k + 1)
                    act.activation(xt_hi[:, k, :], bank[k % 2][:, :], ACT.Copy).then_inc(xt_h, 1)

            def q_high(n, m):
                act.wait_ge(q_mm, n * KC + m + 1)
                act.activation(q_hi[:, m, :], bank[2 + m % 2][:, :], ACT.Identity,
                               bias=bcol[:, 0, m:m + 1]).then_inc(q_h, 1)

            def k_high(n):
                for g in range(4):
                    r = slice(g * HD, g * HD + HD)
                    act.activation(kbd_hi[r, :, (g % 2) * T:(g % 2) * T + T], k_all[r, :, bass.ds(n * T, T)],
                                   ACT.Copy).then_inc(k_h, 1)

            def v_high(n):
                for i in range(4):
                    q, g = i // 2, i % 2
                    act.activation(vbd_hi[g * T:g * T + T, :, q, 2 * q + g, :], v_heads(n, q, g),
                                   ACT.Copy).then_inc(v_h, 1)

            def o_high(n, m):
                act.wait_ge(o_nd, n * KC + m + 1)
                act.activation(o_hi[:, m, :], o_n[:, m % 2, :], ACT.Copy).then_inc(o_h, 1)

            def h_copy(n, t, tail=False):
                act.wait_ge(h_tr, n * TT + t + 1)
                if tail and t >= 2:
                    act.wait_ge(lg_mm, n * TT + t - 1)
                act.activation(ht[:, t % 2, :, :].rearrange("p k n -> p (k n)"), h_bank(t, tail)[:, :],
                               ACT.Copy).then_inc(h_ev, 1)

            def batch(b, back, front):
                for s in range(PAIRS + 1):
                    if s == 0:
                        q_high(b, 2)
                    if s < PAIRS:
                        act.wait_ge(s_clip, b * PAIRS + s + 1)
                        if s >= 2 or back:
                            act.wait_ge(e_l, b * PAIRS + s - 1)
                        act.activation(ex[:, s % 2, :], sc[:, s % 2, :], ACT.Exp, scale=INV_SCALE).then_inc(s_exp, 1)
                        act.wait_ge(s_exp, b * PAIRS + s + 1)
                        if s >= 2 or back:
                            act.wait_ge(pair_mm, b * PAIRS + s - 1)
                        act.activation(ex_hi[:, s % 2, :], ex[:, s % 2, :], ACT.Copy).then_inc(e_h, 1)
                    if s == 0:
                        if back:
                            o_high(b - 1, 0)
                            o_high(b - 1, 1)
                        q_high(b, 3)
                        if back:
                            o_high(b - 1, 2)
                            o_high(b - 1, 3)
                    if s == 3 and front:
                        normalise_x(b + 1)
                    if s == 4 and front:
                        x_high(b + 1)
                    if s in (6, 7) and front:
                        q_high(b + 1, s - 6)
                    if s == PAIRS and front:
                        act.wait_ge(s_mm, b * PAIRS + PAIRS)
                        k_high(b + 1)
                    if s >= 5 and back:
                        h_copy(b - 1, s - 5)
                    if s >= 2 and s % 2 == 0:
                        act.wait_ge(pair_mm, b * PAIRS + s)
                        if s == PAIRS:
                            act.activation(den[:, :], bank[7][0:NH, :], ACT.Copy, scale=1.0 + 1e-8).then_inc(den_c, 1)
                        act.activation(o_un[:, s // 2 - 1, :], bank[6][:, :], ACT.Copy).then_inc(o_ev, 1)
                    if s == PAIRS and front:
                        v_high(b + 1)

            split_weight(0)
            split_weight(1)
            act.wait_ge(cload, 80)
            act.activation(tg[:, 0:2], gsc[:, 0:2], ACT.Tanh).then_inc(gates_ready, 1)
            normalise_x(0)
            x_high(0, range(0, 2))
            split_weight(2)
            x_high(0, range(2, KC))
            act.wait_ge(setup, 12)
            act.wait_ge(pad_store, 48)
            act.wait_ge(kv_sb, 5)
            k_high(0)
            v_high(0)
            q_high(0, 0)
            q_high(0, 1)
            split_weight(3)
            batch(0, False, True)
            with act.Fori(1, NB - 1) as b:
                batch(b, True, True)
            batch(NB - 1, True, False)
            for m in range(KC):
                o_high(NB - 1, m)

            def split_hi(dst, p, done):
                act.activation(dst.rearrange("p k n -> p (k n)"), raw[:, p, :], ACT.Copy).then_inc(done, 1)

            def first_gu(p):
                act.wait_ge(raw_in[p], 16)
                split_hi(g_hi[:, p, :, :], p, gu_hi)

            act.wait_ge(d_mm, NT)
            first_gu(0)
            h_copy(NB - 1, 0, tail=True)
            first_gu(1)
            h_copy(NB - 1, 1, tail=True)
            h_copy(NB - 1, 2, tail=True)
            h_copy(NB - 1, 3, tail=True)
            first_gu(2)
            act.wait_ge(rt, diff_step[0])
            act.activation(wk[:, 1, :], wk[:, 1, :], ACT.Exp).then_inc(rt_act, 1)
            first_gu(3)

            act.wait_ge(tables, 1)
            act.wait_ge(gt_tr, 1)
            act.activation(gt_hi[:, :, :].rearrange("p k n -> p (k n)"), bank[6][:, :], ACT.Copy).then_inc(gt_h, 1)
            act.activation(w_cur[:, :], xg[:, H:H + 1], ACT.Copy).then_inc(w_next, 1)
            used = act.value_load(n_tiles[0:1, 0:1], min_val=1, max_val=MAXT)
            act.preload_act_table(ACT.Silu)
            with act.Fori(0, used) as g:
                expert = tile_entry(act, g, 0, E - 1)
                last = tile_entry(act, g, 1, 1)
                first = tile_entry(act, g, 2, 1)

                def hidden_hi(p):
                    act.wait_ge(hd_tr, g * GU + p + 1)
                    act.activation(hd_hi[:, 2 * p:2 * p + 2, :].rearrange("p k n -> p (k n)"),
                                   bank[4 + p % 2][:, 0:256], ACT.Copy).then_inc(hd_h, 1)

                def next_hi(p):
                    act.wait_ge(raw_in[p], expert * 16 + 32)
                    split_hi(g_hi[:, p, :, :], p, gu_hi)

                def down_hi(p):
                    act.wait_ge(raw_in[GU + p], expert * 16 + 16)
                    split_hi(dn_hi[:, p, :, :], GU + p, dn_h)

                with act.If(first):
                    down_hi(0)
                for p in range(GU):
                    act.wait_ge(gu_mm, g * GU + p + 1)
                    act.activation(silu[:, p, :], bank[p][:, 0:256], ACT.Silu).then_inc(silu_done, 1)
                    if p >= 2:
                        hidden_hi(p - 2)
                    if p < 3:
                        with act.If(last):
                            next_hi(p)
                    if p == 0:
                        with act.If(first):
                            down_hi(1)
                hidden_hi(GU - 2)
                hidden_hi(GU - 1)
                act.wait_ge(gt_tr, g + 2)
                act.activation(gt_hi[:, :, :].rearrange("p k n -> p (k n)"), bank[6][:, :], ACT.Copy).then_inc(gt_h, 1)
                with act.If(last):
                    next_hi(3)
                act.wait_ge(y_mm, g + 1)
                act.wait_ge(y_free, g + 1)
                act.wait_ge(w_next, g + 1)
                act.activation(y_sb[:, :], bank[7][:, :], ACT.Copy, scale=w_cur[:, 0:1]).then_inc(y_ready, 1)
                act.wait_ge(y_ready, g + 2)
                act.activation(w_cur[:, :], xg[:, bass.ds(expert + last + H, 1)], ACT.Copy).then_inc(w_next, 1)

        @block.tensor
        def _(pe):
            pe.sem_inc(y_ready, 1)
            pe.wait_ge(setup, 12)

            def x_transposes(n, chunks=range(KC)):
                pe.wait_ge(hs_done, n * TT + TT)
                for k in chunks:
                    if k >= 2:
                        pe.wait_ge(xt_l, n * KC + k - 1)
                    for t in range(TT):
                        tr = pe.transpose(bank[k % 2][:, t * P:(t + 1) * P], hs[:, t, k * P:(k + 1) * P], ident[:, :])
                    tr.then_inc(xt_tr, 1)

            def q_product(n, m):
                if m == 0:
                    pe.wait_ge(xt_l, n * KC + KC)
                product3(pe, bank[2 + m % 2][:, :],
                         lambda k: w_hi[:, 0, k, m * P:(m + 1) * P], lambda k: w_lo[:, 0, k, m * P:(m + 1) * P],
                         lambda k: xt_hi[:, k, :], lambda k: xt_lo[:, k, :]).then_inc(q_mm, 1)

            def scores(b, s):
                m, r = s // 2, slice((s % 2) * 64, (s % 2) * 64 + 64)
                pe.wait_ge(q_l, b * KC + m + 1)
                if s == 0:
                    pe.wait_ge(k_l, b * 4 + 4)
                if s >= 2:
                    pe.wait_ge(s_clip, b * PAIRS + s - 1)
                product3(pe, bank[4 + s % 2][:, :], lambda k: kbd_hi[r, m, :], lambda k: kbd_lo[r, m, :],
                         lambda k: q_hi[r, m, :], lambda k: q_lo[r, m, :], n=1).then_inc(s_mm, 1)

            def pv(b, s, back):
                m, j = s // 2, s % 2
                pe.wait_ge(e_l, b * PAIRS + s + 1)
                if s == 0:
                    pe.wait_ge(v_l, b * 4 + 4)
                if j == 0 and (m >= 1 or back):
                    pe.wait_ge(o_ev, b * KC + m)
                if s == 0 and back:
                    pe.wait_ge(den_c, b)
                product3(pe, bank[6][:, :],
                         lambda k: vbd_hi[:, m, j, :, :].rearrange("p a d -> p (a d)"),
                         lambda k: vbd_lo[:, m, j, :, :].rearrange("p a d -> p (a d)"),
                         lambda k: ex_hi[:, j, :], lambda k: ex_lo[:, j, :], n=1, first=(j == 0), last=(j == 1))
                at = NH - 2 - 2 * s
                for a, e_ in enumerate((ex_hi, ex_lo)):
                    mm = pe.matmul(bank[7][:, :], hsel[:, at:at + P], e_[:, j, :],
                                   start=(s == 0 and a == 0), stop=(s == PAIRS - 1 and a == 1))
                mm.then_inc(pair_mm, 1)

            def spread(n, m):
                if m == 0:
                    pe.wait_ge(r_l, n + 1)
                    pe.wait_ge(lg_done, n * TT + TT)
                if m >= 2:
                    pe.wait_ge(o_nd, n * KC + m - 1)
                for a, r_ in enumerate((r_hi, r_lo)):
                    mm = pe.matmul(bank[m % 2][:, :], bsel[:, m, :, :].rearrange("p a d -> p (a d)"), r_[:, :],
                                   start=(a == 0), stop=(a == 1))
                mm.then_inc(r_mm, 1)

            def o_product(n, t):
                if t >= 2:
                    pe.wait_ge(d_ready, n * TT + t - 1)
                for k in range(KC):
                    if t == 0:
                        pe.wait_ge(o_l, n * KC + k + 1)
                    mm = product3(pe, bank[2 + t % 2][:, :],
                                  lambda _: o_hi[:, k, t * P:(t + 1) * P], lambda _: o_lo[:, k, t * P:(t + 1) * P],
                                  lambda _: w_hi[:, 1, k, :], lambda _: w_lo[:, 1, k, :],
                                  n=1, first=(k == 0), last=(k == KC - 1))
                mm.then_inc(d_mm, 1)

            def h_transposes(n, t, tail=False):
                pe.wait_ge(h_done, n * TT + t + 1)
                if t >= 2 and not tail:
                    pe.wait_ge(lg_done, n * TT + TT + t - 1)
                for k in range(KC):
                    tr = pe.transpose(h_bank(t, tail)[:, k * P:(k + 1) * P], dh[:, t, k * P:(k + 1) * P], ident[:, :])
                tr.then_inc(h_tr, 1)

            def logits_by_token(tiles):
                for t in tiles:
                    pe.wait_ge(lg_done, TT + t + 1)
                    tr = pe.transpose(bank[3][:, t * E:(t + 1) * E], logits_t[:, t * P:(t + 1) * P], ident[0:E, 0:E])
                return tr

            def router(n, t, tail=False):
                pe.wait_ge(h_ev, n * TT + t + 1)
                for k in range(KC):
                    mm = pe.matmul(h_bank(t, tail)[0:E, 0:P], gate_w[:, k, :], ht[:, t % 2, k, :],
                                   start=(k == 0), stop=(k == KC - 1))
                mm.then_inc(lg_mm, 1)

            def batch(b, back, front):
                for s in range(PAIRS + 1):
                    if s < PAIRS:
                        scores(b, s)
                    if s == 0:
                        pe.wait_ge(q_l, b * KC + 1)
                        q_product(b, 2)
                        if back:
                            spread(b - 1, 0)
                            spread(b - 1, 1)
                        pe.wait_ge(q_l, b * KC + 2)
                        q_product(b, 3)
                        if back:
                            spread(b - 1, 2)
                            spread(b - 1, 3)
                    if s == 4:
                        pv(b, s - 1, back)
                    if s == 4 and front:
                        x_transposes(b + 1, range(0, 2))
                    if 2 <= s < 6 and back:
                        if s == 2:
                            pe.wait_ge(q_l, b * KC + 3)
                        if s == 3:
                            pe.wait_ge(q_l, b * KC + 4)
                        o_product(b - 1, s - 2)
                    if s == 4 and front:
                        x_transposes(b + 1, range(2, KC))
                    if s in (6, 7) and front:
                        if back:
                            pe.wait_ge(d_ready, b * TT + s - 7)
                        q_product(b + 1, s - 6)
                    if s >= 6 and back:
                        router(b - 1, s - 6)
                    if s in (5, 6) and back:
                        if front:
                            pe.wait_ge(xt_l, b * KC + KC + s - 2)
                        else:
                            pe.wait_ge(lg_done, b * TT)
                    if s >= 5 and back:
                        h_transposes(b - 1, s - 5)
                    if s >= 1 and s != 4:
                        pv(b, s - 1, back)
                if back:
                    router(b - 1, 3)

            pe.wait_ge(c_l, 1)
            pe.wait_ge(w_lo_done, 1)
            for m in range(KC):
                mm = product3(pe, bank[6 + m // 2][:, (m % 2) * NB * T:(m % 2 + 1) * NB * T],
                              lambda k: wk_hi[:, k, m * P:(m + 1) * P], lambda k: wk_lo[:, k, m * P:(m + 1) * P],
                              lambda k: c_hi[:, k, 0:NB * T], lambda k: c_lo[:, k, 0:NB * T])
            mm.then_inc(kv_mm, 1)
            pe.wait_ge(w_lo_done, 2)
            for i, n in enumerate(V_ORDER):
                two = slice(n * T, n * T + 2 * T)
                product3(pe, bank[2 + n][:, :], lambda k: c_hi[:, k, two], lambda k: c_lo[:, k, two],
                         lambda k: wv_hi[:, k, :], lambda k: wv_lo[:, k, :]).then_inc(kv_mm, 1)
                if i < 2:
                    x_transposes(0, range(2 * i, 2 * i + 2))
            pe.wait_ge(w_lo_done, 3)
            pe.wait_ge(kv_sb, 5)
            q_product(0, 0)
            pe.wait_ge(kv_sb, 6)
            q_product(0, 1)
            pe.wait_ge(kv_sb, 2 + NB + 1)
            batch(0, False, True)
            with pe.Fori(1, NB - 1) as b:
                batch(b, True, True)
            batch(NB - 1, True, False)
            for m in range(KC):
                spread(NB - 1, m)
            for t in range(TT):
                o_product(NB - 1, t)
            for t in range(TT):
                h_transposes(NB - 1, t, tail=True)
                if t >= 1:
                    router(NB - 1, t - 1, tail=True)
            pe.wait_ge(d_ready, NT)
            logits_by_token(range(NT - TT))
            router(NB - 1, TT - 1, tail=True)
            logits_by_token(range(NT - TT, NT)).then_inc(rt_pe, 1)

            pe.wait_ge(rt_pool, 12)
            pe.wait_ge(rt, sel_step[0])
            selv = sel[:, :, :].rearrange("p t e -> p (t e)")
            width = (NT + 1) * E
            pe.matmul(bank[0][:, 0:width], upper[:, :], selv, start=True, stop=False, skip_group_check=True)
            for s in range(1, NT + 1):
                mm = pe.matmul(bank[0][:, s * E:width], ones[:, :], selv[:, 0:width - s * E],
                               start=False, stop=(s == NT), skip_group_check=True)
            mm.then_inc(rt_pe, 1)
            for c in range(TOPK):
                pe.wait_ge(rt_pool, 13 + c)
                pe.wait_ge(rt, place_step[c])
                for t in range(NT):
                    mm = pe.matmul(bank[2][:, 0:SLOTT], oh_place[:, c, t, :], tok_tile[:, c, t, :],
                                   start=(c == 0 and t == 0), stop=(c == TOPK - 1 and t == NT - 1))
            mm.then_inc(rt_pe, 1)

            pe.wait_ge(tables, 1)

            def slot_rows(n):
                pe.wait_ge(gath, n * 16 + 16)
                for k in range(KC):
                    tr = pe.transpose(bank[6][:, k * P:(k + 1) * P], xg[:, k * P:(k + 1) * P], ident[:, :])
                tr.then_inc(gt_tr, 1)

            slot_rows(0)
            used = pe.value_load(n_tiles[0:1, 0:1], min_val=1, max_val=MAXT)
            with pe.Fori(0, used) as g:
                expert = tile_entry(pe, g, 0, E - 1)

                def hidden_t(p):
                    pe.wait_ge(hid_done, g * GU + p + 1)
                    pe.wait_ge(hd_l, g * GU + p + 1)
                    for c in range(2):
                        tr = pe.transpose(bank[4 + p % 2][:, c * P:(c + 1) * P], hid[:, p, c * P:(c + 1) * P], ident[:, :])
                    tr.then_inc(hd_tr, 1)

                def down(c):
                    if c % 2 == 0:
                        pe.wait_ge(hd_l, g * GU + c // 2 + 3)
                    if c % 4 == 0:
                        pe.wait_ge(dn_split, expert * DH + c // 4 + 1)
                    if c == 0:
                        pe.wait_ge(y_ready, g + 1)
                    mm = product3(pe, bank[7][:, :], lambda k: hd_hi[:, c, :], lambda k: hd_lo[:, c, :],
                                  lambda k: dn_hi[:, c // 4, c % 4, :], lambda k: dn_lo[:, c // 4, c % 4, :],
                                  n=1, first=(c == 0), last=(c == IC - 1))
                    if c == IC - 1:
                        mm.then_inc(y_mm, 1)

                pe.wait_ge(gt_l, g + 1)
                for p in range(GU):
                    pe.wait_ge(gu_split, expert * GU + p + 1)
                    product3(pe, bank[p][:, :], lambda k: gt_hi[:, k, :], lambda k: gt_lo[:, k, :],
                             lambda k: g_hi[:, p, k, :], lambda k: g_lo[:, p, k, :]).then_inc(gu_mm, 1)
                    if p >= 2:
                        hidden_t(p - 2)
                hidden_t(GU - 2)
                down(0)
                down(1)
                hidden_t(GU - 1)
                down(2)
                down(3)
                slot_rows(g + 1)
                for c in range(4, IC):
                    down(c)


sel_step, diff_step, tile_step, place_step = [0], [0], [0], [0, 0]


def kernel(x, ctx_2048, mask_BxS2_ik0, g_xattn, g_ffn, L0_xattn_Wq, L0_xattn_bq, L0_xattn_Wk, L0_xattn_bk,
           L0_xattn_Wv, L0_xattn_bv, L0_xattn_Wo, L0_xattn_bo, L0_xattn_ln_gamma, L0_xattn_ln_beta,
           L0_xattn_residual_scale, L0_ffn_gate_weight, L0_ffn_gate_up_proj, L0_ffn_down_proj):
    import numpy as np
    import concourse.bacc as bacc
    from concourse.bass_utils import run_bass_kernel_spmd

    def c(a):
        return np.ascontiguousarray(np.asarray(a))

    def by_rows(w):
        return np.asarray(w).T.reshape(-1, P, w.shape[0]).transpose(1, 0, 2)

    mask = np.tile(np.asarray(mask_BxS2_ik0).T, (2, 1))
    ctx_t = np.asarray(ctx_2048)[[0, 1, 2, 3, 0]].transpose(2, 0, 1).reshape(KC, P, CT).transpose(1, 0, 2)
    w_attn = np.stack([by_rows(w).reshape(P, KC * H) for w in (L0_xattn_Wk, L0_xattn_Wv, L0_xattn_Wq, L0_xattn_Wo)])
    b_cols = np.stack([np.asarray(b).reshape(KC, P).T for b in (L0_xattn_bq, L0_xattn_bk)], axis=1)
    b_rows = np.stack([np.asarray(b) for b in (L0_xattn_bv, L0_xattn_bo, L0_xattn_ln_gamma, L0_xattn_ln_beta)])
    gates = np.concatenate([np.asarray(g).reshape(1) for g in (g_xattn, g_ffn, L0_xattn_residual_scale)])
    gate_t = by_rows(L0_ffn_gate_weight)
    gu = np.asarray(L0_ffn_gate_up_proj).reshape(E, 2, GU, 256, KC, P).transpose(0, 2, 5, 4, 1, 3)
    dn = np.asarray(L0_ffn_down_proj).reshape(E, H, DH, 4, P).transpose(0, 2, 4, 3, 1)
    w_exp = np.concatenate([gu.reshape(E, GU, P, PW), dn.reshape(E, DH, P, PW)], axis=1)

    ins = dict(x=np.asarray(x).reshape(TOK, H), ctx_t=ctx_t, mask=mask, w_attn=w_attn, b_cols=b_cols,
               b_rows=b_rows, gates=gates, gate_t=gate_t, w_exp=w_exp)
    nc = bacc.Bacc("TRN2", target_bir_lowering=False, num_devices=1)
    arrays, aps = {}, {}
    for name, a in ins.items():
        arrays[f"in_{name}"] = c(a)
        aps[name] = nc.dram_tensor(f"in_{name}", a.shape, mybir.dt.from_np(a.dtype), kind="ExternalInput").ap()
    out = nc.dram_tensor("out_rows", [TOK + P, H], F32, kind="ExternalOutput").ap()
    flamingo_gated_block(nc, out=out, **aps)
    r = run_bass_kernel_spmd(nc, [arrays], core_ids=[0])
    return r.results[0]["out_rows"][:TOK].reshape(NB, S, H)
```
